# Optimizing a Trainium2 kernel written in Bass

```python
import numpy as np
import jax
import jax.numpy as jnp

def _softmax(x, axis=-1):
    return jax.nn.softmax(x, axis=axis)

def _gelu(x):
    return jax.nn.gelu(x, approximate=True)

def _silu(x):
    return jax.nn.silu(x)

def _sigmoid(x):
    return jax.nn.sigmoid(x)

def _layernorm(x, axis=-1, eps=1e-05):
    m = jnp.mean(x, axis=axis, keepdims=True)
    v = jnp.var(x, axis=axis, keepdims=True)
    return (x - m) / jnp.sqrt(v + eps)

def _scatter_add(tgt, idx, src, axis=0):
    return tgt.at[idx].add(src)

def _segment_sum(src, seg, n):
    return jax.ops.segment_sum(src, seg, n)
kernel_name = 'mk_sandwich_d1_jaxref_r8_f81cf0'

def setup_inputs(seed: int=0):
    np.random.seed(seed)
    _w = jnp.asarray

    def _L0_attn_setup():
        import jax, jax.numpy as jnp
        import numpy as np
        D_MODEL = 256
        NHEADS = 32
        D_STATE = 64
        HEADDIM = D_MODEL // NHEADS
        D_INNER = D_MODEL
        D_CONV = 4
        CHUNK = 128
        BATCH = 2
        SEQLEN = 256
        CONV_DIM = D_INNER + 2 * NHEADS * D_STATE
        PROJ_DIM = 2 * D_INNER + 2 * NHEADS * D_STATE + NHEADS

        def _segsum(x):
            T = x.shape[-1]
            cs = jnp.cumsum(x, axis=-1)
            ss = cs[..., :, None] - cs[..., None, :]
            mask = jnp.tril(jnp.ones((T, T), dtype=bool))
            return jnp.where(mask, ss, -jnp.inf)

        def _ssd(X, A, B, C, block_len):
            b, l, h, p = X.shape
            c = l // block_len
            X = X.reshape(b, c, block_len, h, p)
            B = B.reshape(b, c, block_len, h, -1)
            C = C.reshape(b, c, block_len, h, -1)
            A = A.reshape(b, c, block_len, h).transpose(0, 3, 1, 2)
            A_cumsum = jnp.cumsum(A, axis=-1)
            L = jnp.exp(_segsum(A))
            Y_diag = jnp.einsum('bclhn,bcshn,bhcls,bcshp->bclhp', C, B, L, X)
            decay_states = jnp.exp(A_cumsum[..., -1:] - A_cumsum)
            states = jnp.einsum('bclhn,bhcl,bclhp->bchpn', B, decay_states, X)
            states = jnp.concatenate([jnp.zeros_like(states[:, :1]), states], axis=1)
            decay_chunk = jnp.exp(_segsum(jnp.pad(A_cumsum[..., -1], ((0, 0), (0, 0), (1, 0)))))
            new_states = jnp.einsum('bhzc,bchpn->bzhpn', decay_chunk, states)
            states = new_states[:, :-1]
            Y_off = jnp.einsum('bclhn,bchpn,bhcl->bclhp', C, states, jnp.exp(A_cumsum))
            return (Y_diag + Y_off).reshape(b, l, h, p)
        key = jax.random.key(seed)
        ks = jax.random.split(key, 6)
        s = 0.02
        return {'u': jax.random.normal(ks[0], (BATCH, SEQLEN, D_MODEL), jnp.float32), 'W_in': jax.random.normal(ks[1], (PROJ_DIM, D_MODEL), jnp.float32) * s, 'z_bias': jax.random.normal(ks[2], (D_INNER,), jnp.float32) * s, 'conv_w': jax.random.normal(ks[3], (CONV_DIM, D_CONV), jnp.float32) * s, 'conv_b': jax.random.normal(ks[4], (CONV_DIM,), jnp.float32) * s, 'D': jnp.ones((NHEADS,), jnp.float32), 'rms_w': jnp.ones((D_INNER,), jnp.float32), 'W_out': jax.random.normal(ks[5], (D_MODEL, D_INNER), jnp.float32) * s}
    _L0_attn_in = _L0_attn_setup()

    def _L0_ffn_setup():
        import jax, jax.numpy as jnp
        import numpy as np
        H = 256
        key = jax.random.key(seed)
        ks = jax.random.split(key, 10)
        s = 1.0 / np.sqrt(H)
        x = jax.random.normal(ks[0], (4, 256, H), dtype=jnp.float32)
        Wg = jax.random.uniform(ks[1], (2, H), jnp.float32, -s, s)
        W0a = jax.random.uniform(ks[2], (2 * H, H), jnp.float32, -s, s)
        b0a = jax.random.uniform(ks[3], (2 * H,), jnp.float32, -s, s)
        W0b = jax.random.uniform(ks[4], (H, 2 * H), jnp.float32, -s, s)
        b0b = jax.random.uniform(ks[5], (H,), jnp.float32, -s, s)
        W1a = jax.random.uniform(ks[6], (2 * H, H), jnp.float32, -s, s)
        b1a = jax.random.uniform(ks[7], (2 * H,), jnp.float32, -s, s)
        W1b = jax.random.uniform(ks[8], (H, 2 * H), jnp.float32, -s, s)
        b1b = jax.random.uniform(ks[9], (H,), jnp.float32, -s, s)
        return {'x': x, 'Wg': Wg, 'W0a': W0a, 'b0a': b0a, 'W0b': W0b, 'b0b': b0b, 'W1a': W1a, 'b1a': b1a, 'W1b': W1b, 'b1b': b1b}
    _L0_ffn_in = _L0_ffn_setup()
    _d = {'L0_attn_u': _L0_attn_in['u'], 'L0_attn_W_in': _L0_attn_in['W_in'], 'L0_attn_z_bias': _L0_attn_in['z_bias'], 'L0_attn_conv_w': _L0_attn_in['conv_w'], 'L0_attn_conv_b': _L0_attn_in['conv_b'], 'L0_attn_D': _L0_attn_in['D'], 'L0_attn_rms_w': _L0_attn_in['rms_w'], 'L0_attn_W_out': _L0_attn_in['W_out'], 'L0_ffn_Wg': _L0_ffn_in['Wg'], 'L0_ffn_W0a': _L0_ffn_in['W0a'], 'L0_ffn_b0a': _L0_ffn_in['b0a'], 'L0_ffn_W0b': _L0_ffn_in['W0b'], 'L0_ffn_b0b': _L0_ffn_in['b0b'], 'L0_ffn_W1a': _L0_ffn_in['W1a'], 'L0_ffn_b1a': _L0_ffn_in['b1a'], 'L0_ffn_W1b': _L0_ffn_in['W1b'], 'L0_ffn_b1b': _L0_ffn_in['b1b']}
    _x0 = _d['L0_attn_u']
    _d['L0_attn_u'] = jax.random.normal(jax.random.fold_in(jax.random.key(seed), 1), (16, 256, 256), dtype=_x0.dtype)
    del _x0
    return _d

def reference(L0_attn_u, L0_attn_W_in, L0_attn_z_bias, L0_attn_conv_w, L0_attn_conv_b, L0_attn_D, L0_attn_rms_w, L0_attn_W_out, L0_ffn_Wg, L0_ffn_W0a, L0_ffn_b0a, L0_ffn_W0b, L0_ffn_b0b, L0_ffn_W1a, L0_ffn_b1a, L0_ffn_W1b, L0_ffn_b1b):

    def _L0_attn_ref(u, W_in, z_bias, conv_w, conv_b, D, rms_w, W_out):
        import jax, jax.numpy as jnp
        import numpy as np
        D_MODEL = 256
        NHEADS = 32
        D_STATE = 64
        HEADDIM = D_MODEL // NHEADS
        D_INNER = D_MODEL
        D_CONV = 4
        CHUNK = 128
        BATCH = 2
        SEQLEN = 256
        CONV_DIM = D_INNER + 2 * NHEADS * D_STATE
        PROJ_DIM = 2 * D_INNER + 2 * NHEADS * D_STATE + NHEADS

        def _segsum(x):
            T = x.shape[-1]
            cs = jnp.cumsum(x, axis=-1)
            ss = cs[..., :, None] - cs[..., None, :]
            mask = jnp.tril(jnp.ones((T, T), dtype=bool))
            return jnp.where(mask, ss, -jnp.inf)

        def _ssd(X, A, B, C, block_len):
            b, l, h, p = X.shape
            c = l // block_len
            X = X.reshape(b, c, block_len, h, p)
            B = B.reshape(b, c, block_len, h, -1)
            C = C.reshape(b, c, block_len, h, -1)
            A = A.reshape(b, c, block_len, h).transpose(0, 3, 1, 2)
            A_cumsum = jnp.cumsum(A, axis=-1)
            L = jnp.exp(_segsum(A))
            Y_diag = jnp.einsum('bclhn,bcshn,bhcls,bcshp->bclhp', C, B, L, X)
            decay_states = jnp.exp(A_cumsum[..., -1:] - A_cumsum)
            states = jnp.einsum('bclhn,bhcl,bclhp->bchpn', B, decay_states, X)
            states = jnp.concatenate([jnp.zeros_like(states[:, :1]), states], axis=1)
            decay_chunk = jnp.exp(_segsum(jnp.pad(A_cumsum[..., -1], ((0, 0), (0, 0), (1, 0)))))
            new_states = jnp.einsum('bhzc,bchpn->bzhpn', decay_chunk, states)
            states = new_states[:, :-1]
            Y_off = jnp.einsum('bclhn,bchpn,bhcl->bclhp', C, states, jnp.exp(A_cumsum))
            return (Y_diag + Y_off).reshape(b, l, h, p)
        b, L, _ = u.shape
        proj = jnp.einsum('bld,ed->ble', u, W_in)
        xBC, z, A_log = jnp.split(proj, [CONV_DIM, CONV_DIM + D_INNER], axis=-1)
        z = z + z_bias
        A_log = -jax.nn.softplus(A_log)
        xp = jnp.pad(xBC, ((0, 0), (D_CONV - 1, 0), (0, 0)))
        conv = conv_b + sum((xp[:, w:w + L, :] * conv_w[:, w] for w in range(D_CONV)))
        xBC = jax.nn.silu(conv)
        x, Bm, Cm = jnp.split(xBC, [D_INNER, D_INNER + NHEADS * D_STATE], axis=-1)
        X = x.reshape(b, L, NHEADS, HEADDIM)
        Bm = Bm.reshape(b, L, NHEADS, D_STATE)
        Cm = Cm.reshape(b, L, NHEADS, D_STATE)
        Y = _ssd(X, A_log, Bm, Cm, CHUNK)
        Y = Y + D[None, None, :, None] * X
        y = Y.reshape(b, L, D_INNER)
        yg = y * jax.nn.silu(z)
        yn = yg * jax.lax.rsqrt(jnp.mean(yg * yg, axis=-1, keepdims=True) + 1e-05) * rms_w
        return jnp.einsum('ble,de->bld', yn, W_out)

    def _L0_ffn_ref(x, Wg, W0a, b0a, W0b, b0b, W1a, b1a, W1b, b1b):
        import jax, jax.numpy as jnp
        import numpy as np
        H = 256
        scores = jax.nn.softmax(jnp.einsum('bsh,eh->bse', x, Wg), axis=-1)
        top_expert = jnp.argmax(scores, axis=-1)
        h0 = jax.nn.gelu(jnp.einsum('bsh,fh->bsf', x, W0a) + b0a, approximate=False)
        out0 = jnp.einsum('bsf,hf->bsh', h0, W0b) + b0b
        h1 = jax.nn.relu(jnp.einsum('bsh,fh->bsf', x, W1a) + b1a)
        out1 = jnp.einsum('bsf,hf->bsh', h1, W1b) + b1b
        mask0 = (top_expert == 0).astype(x.dtype)[..., None]
        return out0 * mask0 + out1 * (1.0 - mask0)
    x = L0_attn_u
    x = x + _layernorm(_L0_attn_ref(_layernorm(x, axis=-1), L0_attn_W_in, L0_attn_z_bias, L0_attn_conv_w, L0_attn_conv_b, L0_attn_D, L0_attn_rms_w, L0_attn_W_out), axis=-1)
    x = x + _layernorm(_L0_ffn_ref(_layernorm(x, axis=-1), L0_ffn_Wg, L0_ffn_W0a, L0_ffn_b0a, L0_ffn_W0b, L0_ffn_b0b, L0_ffn_W1a, L0_ffn_b1a, L0_ffn_W1b, L0_ffn_b1b), axis=-1)
    return x

_drawn_inputs = setup_inputs


def setup_inputs(seed=0):
    import zlib

    import numpy as np

    out = dict(_drawn_inputs(seed))
    spreads = {'L0_attn_D': (1.0, 0.2), 'L0_attn_rms_w': (1.0, 0.2)}
    factors = {}
    for name, (base, spread) in spreads.items():
        noise = np.random.default_rng([zlib.crc32(name.encode()), seed]).standard_normal(out[name].shape)
        drawn = base * np.exp(spread * noise) if base else spread * noise
        out[name] = jnp.asarray(drawn.astype(out[name].dtype))
    for name, factor in factors.items():
        out[name] = (out[name] * factor).astype(out[name].dtype)
    return out
```

```python
from contextlib import ExitStack

import concourse.bass as bass
import numpy as np
from concourse import mybir

F32 = mybir.dt.float32
F32R = mybir.dt.float32r
BF16 = mybir.dt.bfloat16
ALU = mybir.AluOpType
ACT = mybir.ActivationFunctionType

P = 128
BATCH, SEQ, DM = 16, 256, 256
HEADS, NSTATE, HDIM, TAPS = 32, 64, 8, 4
PAIRS = BATCH // 2
TOK = 2 * SEQ
NBC = TOK // P
KT = DM // P
XT = HEADS * HDIM // P
NT = HEADS * NSTATE // P
TILES = XT + 2 * NT
QUADS, QH, QT = 4, 8, 8
SLOTS = 2 * NT
ZA = DM + HEADS
FF = 2 * DM
FT = FF // P
EPS = 1e-5
LAG = 11
STEP = 4
GUARDS = P // STEP - 1
CSL = 3 * QH
HPT = CSL + 3 + GUARDS

def shared_jobs(first):
    jobs = ["XH0", "XH1"]
    for n in range(SLOTS):
        jobs += slot_jobs(n, first)
    return jobs


def slot_jobs(n, first):
    jobs = []
    if n < NBC:
        jobs.append(f"ZA{n}")
    if n == 6:
        jobs += ["CST", "CSK"]
    if n == LAG:
        jobs += ["XT0", "XT1"]
    g = n - LAG
    prev = g < 0
    q, u = (g % SLOTS) // QH, g % QH
    tag = "-" if prev else ""
    if not (prev and first):
        if u in (0, 1):
            jobs.append(f"BT{q}{u}{tag}")
        if u == 3:
            jobs.append(f"ST{q}{tag}")
    if not first:
        if n == 15:
            jobs += ["YT0-", "YT1-"]
        if n in (16, 17):
            jobs.append(f"OP{n - 16}-")
    return jobs


JOBS = {True: shared_jobs(True), False: shared_jobs(False)}
TAIL_JOBS = ["BT30-", "BT31-", "ST3-", "YT0-", "YT1-", "OP0-", "OP1-"]
JOBS_FIRST, JOBS_EACH = len(JOBS[True]), len(JOBS[False])


def lay_out():
    nx, ns = HEADS * HDIM, HEADS * NSTATE
    rows = list(range(nx))
    for t in range(NT):
        rows += range(nx + t * P, nx + (t + 1) * P)
        rows += range(nx + ns + t * P, nx + ns + (t + 1) * P)
    return np.array(rows)


def constants():
    s = np.arange(P)
    ident = np.eye(P, dtype=np.float32)
    upto = -(s[:, None] <= s[None, :]).astype(np.float32)
    beyond = -(s[:, None] > s[None, :]).astype(np.float32)
    mats = np.stack([ident, upto, beyond], axis=1).reshape(P, 3 * P)
    pick = np.zeros((HPT, QH, NBC, P), np.float32)
    for part in range(3):
        for k in range(QH):
            pick[part * QH + k, k] = -1.0
    for r in range(GUARDS):
        pick[CSL + 3 + r, :, :, :(r + 1) * STEP] = -1e30
    marks = np.zeros((HPT - CSL, QUADS, NBC, P), np.float32)
    marks[:3] = 1.0
    for r in range(GUARDS):
        marks[3 + r, :, :, (r + 1) * STEP:(r + 2) * STEP] = 1.0
    return np.ascontiguousarray(mats), pick.reshape(HPT, QH, TOK), marks.reshape(HPT - CSL, QUADS, TOK)


def mamba_block(nc, u, w_tiles, w_za, z_bias, conv_w, conv_b, d_skip, rms_w, w_out, mats, pick, marks, cs_dram, x1_dram):
    with ExitStack() as ctx:
        def sb(name, shape, dt=F32):
            return ctx.enter_context(nc.sbuf_tensor(name, shape, dt))

        def ps(name, shape=(P, 512)):
            return ctx.enter_context(nc.psum_tensor(name, list(shape), F32))

        def sem(name):
            return ctx.enter_context(nc.semaphore(name))

        w_hi, w_lo = sb("w_hi", [P, KT, TILES * P], F32R), sb("w_lo", [P, KT, TILES * P], F32R)
        za_hi, za_lo = sb("za_hi", [P, KT, ZA], F32R), sb("za_lo", [P, KT, ZA], F32R)
        wo_hi, wo_lo = sb("wo_hi", [P, KT, DM], F32R), sb("wo_lo", [P, KT, DM], F32R)
        bc = sb("bc", [P, 2 * QT, TOK])
        xT = sb("xT", [P, XT, TOK])
        u_in = sb("u_in", [P, NBC, DM])
        u_norm = sb("u_norm", [P, NBC, DM])
        xh_hi, xh_lo = sb("xh_hi", [P, KT, TOK], F32R), sb("xh_lo", [P, KT, TOK], F32R)
        z_raw, z_silu = sb("z_raw", [P, NBC, DM]), sb("z_silu", [P, NBC, DM])
        u_res = z_raw
        x_tok = sb("x_tok", [P, NBC, DM])
        x_skip = sb("x_skip", [P, NBC, DM])
        x_dec = sb("x_dec", [P, 2, DM])
        y_sum = sb("y_sum", [P, NBC, DM])
        y_tmp = sb("y_tmp", [P, 2, QH * HDIM])
        yg = o_sb = u_norm
        yT_hi, yT_lo = sb("yT_hi", [P, KT, TOK], F32R), sb("yT_lo", [P, KT, TOK], F32R)
        NL, NM = 4, 2
        decay = sb("decay", [P, NL, TOK])
        mixed = sb("mixed", [P, NM, TOK])
        b_tok = sb("b_tok", [P, 2, TOK])
        states = sb("states", [P, 4, 2, 2 * HDIM])
        a_log, a_abs, sp = sb("a_log", [P, NBC, HEADS]), sb("a_abs", [P, NBC, HEADS]), sb("sp", [P, NBC, HEADS])
        cs_k, e_cs = sb("cs_k", [P, NBC, HEADS]), sb("e_cs", [P, NBC, HEADS])
        cs_rest = sb("cs_rest", [HEADS, TOK])
        cs_parts = sb("cs_parts", [HEADS, 3, TOK], BF16)
        d_stat = sb("d_stat", [HPT, QUADS, TOK], BF16)
        d_mov = sb("d_mov", [HPT, 2, QH, TOK], BF16)
        mats_sb = sb("mats_sb", [P, 3 * P])
        ident, upto, beyond = (mats_sb[:, k * P:(k + 1) * P] for k in range(3))
        cw, cb = sb("cw", [P, TILES, TAPS]), sb("cb", [P, TILES])
        zb = sb("zb", [P, DM])
        dsk = sb("dsk", [P, HEADS])
        rw = sb("rw", [P, KT])
        stats, mv = sb("stats", [P, NBC, 6]), sb("mv", [P, NBC, 2])
        ve, rstd = sb("ve", [P, NBC]), sb("rstd", [P, NBC])
        stats2, mv2 = sb("stats2", [P, NBC, 6]), sb("mv2", [P, NBC, 2])
        ve2, rstd2 = sb("ve2", [P, NBC]), sb("rstd2", [P, NBC])
        ss, ms, rms = sb("ss", [P, NBC]), sb("ms", [P, NBC]), sb("rms", [P, NBC])
        mhalf = sb("mhalf", [P, NBC])

        p_proj = [ps("p_proj0"), ps("p_proj1")]
        p_g = [ps("p_g0"), ps("p_g1")]
        p_d, p_y = ps("p_d"), ps("p_y")
        p_t = [ps("p_t0"), ps("p_t1")]

        s_const, s_wld, s_wo = sem("s_const"), [sem("s_wld0"), sem("s_wld1")], sem("s_wo")
        s_wsplit, s_small = sem("s_wsplit"), sem("s_small")
        s_init, s_pick = sem("s_init"), sem("s_pick")
        s_u = sem("s_u")
        s_ln, s_lnpow = sem("s_ln"), sem("s_lnpow")
        s_tfull, s_tdone = sem("s_tfull"), sem("s_tdone")
        s_tc = sem("s_tc")
        s_proj = sem("s_proj")
        s_tap3 = sem("s_tap3")
        s_tap2, s_tap1, s_tap0 = sem("s_tap2"), sem("s_tap1"), sem("s_tap0")
        s_silu = sem("s_silu")
        s_xsilu, s_zsilu = sem("s_xsilu"), sem("s_zsilu")
        s_abs, s_sp1, s_sp2, s_sp = sem("s_abs"), sem("s_sp1"), sem("s_sp2"), sem("s_sp")
        s_parts = sem("s_parts")
        s_csst, s_dstat, s_dmov = sem("s_csst"), sem("s_dstat"), [sem("s_dmov0"), sem("s_dmov1")]
        s_ecs = sem("s_ecs")
        s_d, s_exp, s_mask = sem("s_d"), sem("s_exp"), sem("s_mask")
        s_g, s_m, s_y = sem("s_g"), sem("s_m"), sem("s_y")
        s_xdec, s_xskip = sem("s_xdec"), sem("s_xskip")
        s_yoff = sem("s_yoff")
        s_yev = sem("s_yev")
        s_yg, s_sq, s_ms, s_rms, s_yn = sem("s_yg"), sem("s_sq"), sem("s_ms"), sem("s_rms"), sem("s_yn")
        s_ln2, s_ln2pow, s_x1, s_x1out, s_ures = sem("s_ln2"), sem("s_ln2pow"), sem("s_x1"), sem("s_x1out"), sem("s_ures")
        s_xn2, s_held = sem("s_xn2"), sem("s_held")

        u_p = u.rearrange("(i b) (c p) d -> i p (b c) d", b=2, p=P)
        x1_p = x1_dram.rearrange("i (k p) d -> i p k d", p=P)

        def of_pass(t, i):
            if isinstance(i, int):
                return t[i]
            return t[bass.ds(i, 1)].rearrange("o p k d -> (o p) k d")

        def job(name, i):
            if isinstance(i, int) and i == 0:
                return JOBS[True].index(name)
            if isinstance(i, int) and i == PAIRS:
                return JOBS_FIRST + JOBS_EACH * (PAIRS - 1) + TAIL_JOBS.index(name)
            return i * JOBS_EACH + (JOBS_FIRST - JOBS_EACH + JOBS[False].index(name))

        def jobs_before(i):
            return i * JOBS_EACH + (JOBS_FIRST - JOBS_EACH)

        def bank(name, i):
            if isinstance(i, int) and i == 0:
                return JOBS[True].index(name) % 2
            if isinstance(i, int) and i == PAIRS:
                return (JOBS_FIRST + JOBS_EACH * (PAIRS - 1) + TAIL_JOBS.index(name)) % 2
            return (JOBS_FIRST + JOBS[False].index(name)) % 2

        assert JOBS_EACH % 2 == 0

        def heads_at(n, i):
            g = n - LAG
            if g >= 0:
                return (i, g)
            return None if isinstance(i, int) and i == 0 else (i - 1, g + SLOTS)

        def tile_of(n):
            return n % (2 * QT)

        WQ = TILES * P // 2
        stage = bc[:, :, :].rearrange("p a b -> p (a b)")

        block = ctx.enter_context(nc.Block())

        @block.sync
        def _(sp_):
            w_src = w_tiles.rearrange("(k p) n -> p k n", p=P)
            sp_.dma_start(u_in[:], of_pass(u_p, 0)).then_inc(s_u, 16)
            sp_.dma_start(mats_sb[:], mats).then_inc(s_const, 16)
            sp_.dma_start(cw[:], conv_w).then_inc(s_const, 16)
            sp_.dma_start(cb[:], conv_b).then_inc(s_const, 16)
            sp_.dma_start(zb[:], z_bias.rearrange("(o n) -> o n", o=1).broadcast_to([P, DM])).then_inc(s_const, 16)
            sp_.dma_start(dsk[:], d_skip.rearrange("(o n) -> o n", o=1).broadcast_to([P, HEADS])).then_inc(s_const, 16)
            sp_.dma_start(rw[:], rms_w).then_inc(s_const, 16)
            sp_.dma_start(u_res[:, 0:2, :].rearrange("p a b -> p (a b)"),
                          w_out.rearrange("(k p) n -> p k n", p=P)).then_inc(s_wo, 16)
            sp_.dma_start(z_silu[:, 0:3, :].rearrange("p a b -> p (a b)")[:, 0:KT * ZA],
                          w_za.rearrange("(k p) n -> p k n", p=P)).then_inc(s_wo, 16)
            for c in range(4):
                if c >= 2:
                    sp_.wait_ge(s_wsplit, 2 * (c - 1))
                sp_.dma_start(stage[:, (c % 2) * WQ:(c % 2 + 1) * WQ],
                              w_src[:, c // 2, (c % 2) * WQ:(c % 2 + 1) * WQ]).then_inc(s_wld[c % 2], 16)

            def one_pass(i):
                first = isinstance(i, int)
                if not first:
                    sp_.wait_ge(s_ln, i * 13)
                    sp_.dma_start(u_in[:], of_pass(u_p, i)).then_inc(s_u, 16)
                sp_.wait_ge(s_parts, i * 3 + 3)
                sp_.sem_inc(s_held, 1)
                if not first:
                    sp_.wait_ge(s_dmov[0], i * 32)
                    sp_.wait_ge(s_dmov[1], i * 32)
                sp_.dma_start(cs_dram.rearrange("a h n -> h a n"), cs_parts[:]).then_inc(s_csst, 16)
                sp_.wait_ge(s_csst, i * 16 + 16)
                sp_.sem_inc(s_held, 1)
                if not first:
                    sp_.wait_ge(s_d, i * SLOTS)
                else:
                    sp_.wait_ge(s_pick, 48)
                for part in range(3):
                    sp_.dma_start(d_stat[part * QH:(part + 1) * QH],
                                  cs_dram[part].rearrange("(q k) n -> k q n", k=QH)).then_inc(s_dstat, 16)
                for q in range(QUADS):
                    if q == 2 and not first:
                        residual(i - 1, i)
                    if q >= 2 or not first:
                        sp_.wait_ge(s_d, i * SLOTS + QH * (q - 1))
                    sp_.dma_start(d_mov[CSL:CSL + 3, q % 2],
                                  cs_dram[:, q * QH:(q + 1) * QH, :]).then_inc(s_dmov[q % 2], 16)
                    if q == 2 and not first:
                        store(i - 1)

            def residual(i, body):
                sp_.wait_ge(s_zsilu, body + 1)
                sp_.dma_start(u_res[:], of_pass(u_p, i)).then_inc(s_ures, 16)

            def store(i):
                sp_.wait_ge(s_x1, i + 1)
                sp_.dma_start(of_pass(x1_p, i), o_sb[:]).then_inc(s_x1out, 16)

            sp_.sem_inc(s_x1out, 16)
            one_pass(0)
            with sp_.Fori(1, PAIRS) as i:
                one_pass(i)
            residual(PAIRS - 1, PAIRS - 1)
            store(PAIRS - 1)
            sp_.wait_ge(s_x1out, 16 * (PAIRS + 1))

        @block.tensor
        def _(pe):
            def split3(out, a, a2, b, b2, k, last, start=None):
                for m, (x, y) in enumerate(((a, b), (a, b2), (a2, b))):
                    r = nc.tensor.matmul(out, x, y, start=(k == 0 and m == 0), stop=(last and m == 2))
                return r

            def open_job(name, i):
                j = job(name, i)
                if not (isinstance(j, int) and j < 2):
                    pe.wait_ge(s_tdone, j - 1)
                return p_t[bank(name, i)]

            def norm_transposes(i):
                pe.wait_ge(s_ln, i * 13 + 13)
                for k in range(KT):
                    t = open_job(f"XH{k}", i)
                    for c in range(NBC):
                        r = nc.tensor.transpose(t[:, c * P:(c + 1) * P], u_norm[:, c, k * P:(k + 1) * P], ident)
                    r.then_inc(s_tfull, 1)

            def project(i, m):
                if not (isinstance(i, int) and i == 0 and m < 2):
                    pe.wait_ge(s_tap0, i * TILES + m - 1)
                if m == 0:
                    pe.wait_ge(s_tdone, job("XH1", i) + 1)
                for k in range(KT):
                    cols = slice(m * P, (m + 1) * P)
                    r = split3(p_proj[m % 2][:], w_hi[:, k, cols], w_lo[:, k, cols], xh_hi[:, k], xh_lo[:, k], k, k == KT - 1)
                r.then_inc(s_proj, 1)

            def project_za(i, c):
                t = open_job(f"ZA{c}", i)
                for k in range(KT):
                    cols = slice(c * P, (c + 1) * P)
                    r = split3(t[:, 0:ZA], xh_hi[:, k, cols], xh_lo[:, k, cols], za_hi[:, k], za_lo[:, k], k, k == KT - 1)
                r.then_inc(s_tfull, 1)

            def cumsums(i):
                t = open_job("CST", i)
                pe.wait_ge(s_sp, i + 1)
                for c in range(NBC):
                    r = nc.tensor.matmul(t[0:HEADS, c * P:(c + 1) * P], sp[:, c], upto, start=True, stop=True)
                r.then_inc(s_tfull, 1)
                t = open_job("CSK", i)
                for c in range(NBC):
                    r = nc.tensor.matmul(t[:, c * HEADS:(c + 1) * HEADS], upto if c % 2 else beyond, sp[:, c],
                                         start=True, stop=True)
                r.then_inc(s_tfull, 1)

            def x_transposes(i):
                pe.wait_ge(s_xsilu, i + 1)
                for x in range(XT):
                    t = open_job(f"XT{x}", i)
                    for c in range(NBC):
                        r = nc.tensor.transpose(t[:, c * P:(c + 1) * P], xT[:, x, c * P:(c + 1) * P], ident)
                    r.then_inc(s_tfull, 1)

            def decay_exponents(i, g):
                q, k = g // QH, g % QH
                if not (isinstance(i, int) and i == 0 and g == 0):
                    pe.wait_ge(s_exp, i * SLOTS + g)
                if k == 0:
                    pe.wait_ge(s_dmov[q % 2], i * 32 + 16 * (q // 2 + 1))
                    if q == 0:
                        pe.wait_ge(s_dstat, i * 48 + 48)
                for c in range(NBC):
                    r = nc.tensor.matmul(p_d[:, c * P:(c + 1) * P], d_stat[:, q, c * P:(c + 1) * P],
                                         d_mov[:, q % 2, k, c * P:(c + 1) * P], start=True, stop=True)
                r.then_inc(s_d, 1)

            def scores(i, g):
                q, k = g // QH, g % QH
                if k == 0:
                    pe.wait_ge(s_silu, i * QUADS + q + 1)
                if not (isinstance(i, int) and i == 0 and g < 2):
                    pe.wait_ge(s_m, i * SLOTS + g - 1)
                rows = slice((g % 2) * NSTATE, (g % 2 + 1) * NSTATE)
                tb = tile_of(q * QT + 2 * (k // 2))
                for c in range(NBC):
                    r = nc.tensor.matmul(p_g[g % 2][:, c * P:(c + 1) * P], bc[rows, tb, c * P:(c + 1) * P],
                                         bc[rows, tb + 1, c * P:(c + 1) * P], start=True, stop=True)
                r.then_inc(s_g, 1)

            def mix_x(i, g):
                q, k = g // QH, g % QH
                pe.wait_ge(s_m, i * SLOTS + g + 1)
                if k == 0 and not (isinstance(i, int) and i == 0 and q == 0):
                    pe.wait_ge(s_yev, i * 12 + 3 * q)
                if g == 0:
                    pe.wait_ge(s_tdone, job("XT1", i) + 1)
                for c in range(NBC):
                    r = nc.tensor.matmul(p_y[:, c * 64 + k * HDIM:c * 64 + (k + 1) * HDIM],
                                         mixed[:, g % NM, c * P:(c + 1) * P],
                                         x_tok[:, c, g * HDIM:(g + 1) * HDIM], start=True, stop=True)
                r.then_inc(s_y, 1)

            def b_transposes(i, q, h, body, tag):
                t = open_job(f"BT{q}{h}{tag}", body)
                for j in range(2):
                    for b in range(2):
                        tb = tile_of(q * QT + 2 * (2 * h + j))
                        r = nc.tensor.transpose(t[:, (2 * j + b) * P:(2 * j + b + 1) * P],
                                                bc[:, tb, 2 * b * P:(2 * b + 1) * P], ident)
                r.then_inc(s_tfull, 1)

            def chunk_states(i, q, body, tag):
                t = open_job(f"ST{q}{tag}", body)
                pe.wait_ge(s_tdone, job(f"BT{q}1{tag}", body) + 1)
                pe.wait_ge(s_xdec, i + 1)
                for j in range(4):
                    for b in range(2):
                        a = (j % 2) * 2 + b
                        at = (2 * j + b) * 2 * HDIM
                        r = nc.tensor.matmul(t[:, at:at + 2 * HDIM], b_tok[:, j // 2, a * P:(a + 1) * P],
                                             x_dec[:, b, (q * QH + 2 * j) * HDIM:(q * QH + 2 * j + 2) * HDIM],
                                             start=True, stop=True)
                r.then_inc(s_tfull, 1)

            def y_from_state(i, q, body, tag):
                pe.wait_ge(s_tdone, job(f"ST{q}{tag}", body) + 1)
                for j in range(4):
                    for b in range(2):
                        tc_ = tile_of(q * QT + 2 * j + 1)
                        at = 256 + b * 64 + 2 * j * HDIM
                        r = nc.tensor.matmul(p_y[:, at:at + 2 * HDIM], bc[:, tc_, (2 * b + 1) * P:(2 * b + 2) * P],
                                             states[:, j, b, :], start=True, stop=True)
                r.then_inc(s_yoff, 1)

            def y_transposes(i, body):
                pe.wait_ge(s_yn, i * 4 + 4)
                for k in range(KT):
                    t = open_job(f"YT{k}-", body)
                    for c in range(NBC):
                        r = nc.tensor.transpose(t[:, c * P:(c + 1) * P], yg[:, c, k * P:(k + 1) * P], ident)
                    r.then_inc(s_tfull, 1)

            def project_out(i, h, body):
                t = open_job(f"OP{h}-", body)
                pe.wait_ge(s_tdone, job("YT1-", body) + 1)
                for j in range(2):
                    for k in range(KT):
                        cols = slice((2 * h + j) * P, (2 * h + j + 1) * P)
                        r = split3(t[:, j * DM:(j + 1) * DM], yT_hi[:, k, cols], yT_lo[:, k, cols],
                                   wo_hi[:, k], wo_lo[:, k], k, k == KT - 1)
                r.then_inc(s_tfull, 1)

            def attend(n, i, tail=False):
                at = (lambda m: (i - 1, m - LAG + SLOTS) if m - LAG < 0 else None) if tail else (lambda m: heads_at(m, i))
                ahead = at(n + 1) if n + 1 < SLOTS else (i, n + 1 - LAG)
                if ahead:
                    decay_exponents(*ahead)
                now = at(n)
                if now:
                    ii, g = now
                    q, u = g // QH, g % QH
                    tag = "-" if n - LAG < 0 else ""
                    scores(ii, g)
                behind = heads_at(n - 1, i) if n >= 1 else (None if isinstance(i, int) and i == 0 else (i - 1, SLOTS - 1 - LAG))
                if behind:
                    mix_x(*behind)
                if n == LAG and not tail:
                    x_transposes(i)
                if now:
                    if u in (0, 1):
                        b_transposes(ii, q, u, i, tag)
                    if u == 3:
                        chunk_states(ii, q, i, tag)
                    if u == 4:
                        y_from_state(ii, q, i, tag)

            def one_pass(i):
                first = isinstance(i, int)
                norm_transposes(i)
                project(i, 0)
                project(i, 1)
                for n in range(SLOTS):
                    project(i, XT + n)
                    if n < NBC:
                        project_za(i, n)
                    if n == 6:
                        cumsums(i)
                    attend(n, i)
                    if not first:
                        if n == 15:
                            y_transposes(i - 1, i)
                        if n in (16, 17):
                            project_out(i - 1, n - 16, i)

            pe.wait_ge(s_const, 16 * 6)
            pe.wait_ge(s_wsplit, 8)
            pe.wait_ge(s_small, 2)
            one_pass(0)
            with pe.Fori(1, PAIRS) as i:
                one_pass(i)
            for n in range(LAG + 1):
                attend(n, PAIRS, tail=True)
            y_transposes(PAIRS - 1, PAIRS)
            project_out(PAIRS - 1, 0, PAIRS)
            project_out(PAIRS - 1, 1, PAIRS)

        @block.scalar
        def _(act):
            def newest_tap(i, m):
                if m >= XT:
                    n = m - XT
                    q, j = n // QT, (n % QT) // 2
                    if q >= 2:
                        act.wait_ge(s_g, i * SLOTS + (q - 2) * QH + 2 * j + 2)
                        act.wait_ge(s_yoff, i * QUADS + q - 1)
                    elif not isinstance(i, int):
                        act.wait_ge(s_g, i * SLOTS + (q - 2) * QH + 2 * j + 2)
                        act.wait_ge(s_yoff, i * QUADS + q - 1)
                    elif m == XT:
                        act.wait_ge(s_wsplit, 8)
                    dst = bc[:, tile_of(n)]
                else:
                    if m == 0:
                        if isinstance(i, int):
                            act.wait_ge(s_const, 16 * 6)
                        else:
                            act.wait_ge(s_tfull, jobs_before(i))
                    dst = xT[:, m]
                act.wait_ge(s_proj, i * TILES + m + 1)
                nc.scalar.activation(dst, p_proj[m % 2][:], ACT.Identity, bias=cb[:, m:m + 1],
                                     scale=cw[:, m, TAPS - 1:TAPS]).then_inc(s_tap3, 1)

            def silu_group(i, q):
                act.wait_ge(s_tap0, i * TILES + XT + (q + 1) * QT)
                t0 = tile_of(q * QT)
                v = bc[:, t0:t0 + QT].rearrange("p a b -> p (a b)")
                nc.scalar.activation(v, v, ACT.Silu).then_inc(s_silu, 1)

            def silu_x(i):
                v = xT[:].rearrange("p a b -> p (a b)")
                act.wait_ge(s_tap0, i * TILES + XT)
                nc.scalar.activation(v, v, ACT.Silu).then_inc(s_xsilu, 1)

            def silu_z(i):
                act.wait_ge(s_tdone, job("ZA3", i) + 1)
                if isinstance(i, int):
                    act.wait_ge(s_small, 2)
                else:
                    act.wait_ge(s_yg, i)
                nc.scalar.activation(z_silu[:].rearrange("p a b -> p (a b)"), z_raw[:].rearrange("p a b -> p (a b)"),
                                     ACT.Silu).then_inc(s_zsilu, 1)

            def softplus(i):
                act.wait_ge(s_abs, i + 1)
                nc.scalar.activation(a_abs[:].rearrange("p a b -> p (a b)"), a_abs[:].rearrange("p a b -> p (a b)"),
                                     ACT.Exp, scale=-1.0).then_inc(s_sp1, 1)
                act.wait_ge(s_sp1, i + 1)
                nc.scalar.activation(a_abs[:].rearrange("p a b -> p (a b)"), a_abs[:].rearrange("p a b -> p (a b)"),
                                     ACT.Ln, bias=1.0).then_inc(s_sp2, 1)

            def exp_cs(i):
                act.wait_ge(s_tdone, job("CSK", i) + 1)
                if not isinstance(i, int):
                    act.wait_ge(s_yev, i * 12)
                    act.wait_ge(s_xdec, i)
                nc.scalar.activation(e_cs[:].rearrange("p a b -> p (a b)"), cs_k[:].rearrange("p a b -> p (a b)"),
                                     ACT.Exp).then_inc(s_ecs, 1)

            def decays(i, g):
                act.wait_ge(s_d, i * SLOTS + g + 1)
                if not (isinstance(i, int) and i == 0 and g < NL):
                    act.wait_ge(s_m, i * SLOTS + g - NL + 1)
                nc.scalar.activation(decay[:, g % NL], p_d[:], ACT.Exp).then_inc(s_exp, 1)

            def squares(i):
                act.wait_ge(s_yg, i + 1)
                if not (isinstance(i, int) and i == 0):
                    act.wait_ge(s_ms, i)
                for c in range(NBC):
                    if not (isinstance(i, int) and i == 0 and c == 0):
                        act.wait_ge(s_sq, i * NBC + c)
                    nc.scalar.activation(y_sum[:, c], yg[:, c], ACT.Square, accum_out=ss[:, c:c + 1]).then_inc(s_sq, 1)

            def one_pass(i):
                first = isinstance(i, int)
                newest_tap(i, 0)
                newest_tap(i, 1)
                for n in range(SLOTS):
                    ahead = heads_at(n + 1, i) if n + 1 < SLOTS else (i, n + 1 - LAG)
                    if ahead:
                        decays(*ahead)
                    newest_tap(i, XT + n)
                    if n == 5:
                        softplus(i)
                    if n % QT == 1:
                        q = (n // QT - 1) % QUADS
                        if n > QT or not first:
                            silu_group(i if n > QT else i - 1, q)
                        if n == QT + 1:
                            silu_x(i)
                        if n == 2 * QT + 1:
                            silu_z(i)
                    if n == 12:
                        exp_cs(i)
                    if n == 13 and not first:
                        squares(i - 1)

            one_pass(0)
            with act.Fori(1, PAIRS) as i:
                one_pass(i)
            for n in range(LAG - 1):
                decays(PAIRS - 1, n + 1 - LAG + SLOTS)
                if n == 1:
                    silu_group(PAIRS - 1, QUADS - 1)
            squares(PAIRS - 1)

        @block.gpsimd
        def _(pool):
            pool.memset(mhalf[:], -0.5).then_inc(s_init, 1)
            pool.memset(states[:].rearrange("p a b c -> p (a b c)"), 0.0).then_inc(s_init, 1)
            pool.dma_start(d_stat[CSL:HPT], marks).then_inc(s_pick, 16)
            for half in range(2):
                pool.dma_start(d_mov[:, half], pick).then_inc(s_pick, 16)
            pool.wait_ge(s_init, 2)

            def causal(i, g):
                pool.wait_ge(s_exp, i * SLOTS + g + 1)
                pool.sem_inc(s_held, 1)
                v = decay[:, g % NL].rearrange("p (c l) -> p c l", c=NBC)
                pool.affine_select(out=v, in_=v, compare_op=ALU.is_ge, fill=0.0, base=0,
                                   pattern=[[0, NBC], [1, P]], channel_multiplier=-1).then_inc(s_mask, 1)

            def pow_of(out, src, done, ready, value, i):
                pool.wait_ge(ready, value)
                pool.tensor_tensor(out, src, mhalf[:], ALU.pow).then_inc(done, 1)

            def x_scaled(i):
                pool.wait_ge(s_tdone, job("XT1", i) + 1)
                if not isinstance(i, int):
                    pool.wait_ge(s_yev, i * 12)
                for b in range(2):
                    if b == 0:
                        pool.wait_ge(s_ecs, i + 1)
                    pool.tensor_tensor(x_dec[:, b].rearrange("p (h d) -> p h d", d=HDIM),
                                       x_tok[:, 2 * b].rearrange("p (h d) -> p h d", d=HDIM),
                                       e_cs[:, 2 * b].unsqueeze(2).broadcast_to([P, HEADS, HDIM]), ALU.mult)\
                        .then_inc(s_xdec if b else s_xskip, 1)
                for c in range(NBC):
                    pool.tensor_tensor(x_skip[:, c].rearrange("p (h d) -> p h d", d=HDIM),
                                       x_tok[:, c].rearrange("p (h d) -> p h d", d=HDIM),
                                       dsk[:].unsqueeze(2).broadcast_to([P, HEADS, HDIM]), ALU.mult)\
                        .then_inc(s_xskip, 1)

            def one_pass(i):
                first = isinstance(i, int)
                pow_of(rstd[:], ve[:], s_lnpow, s_ln, i * 13 + 9, i)
                for n in range(SLOTS):
                    ahead = heads_at(n + 1, i) if n + 1 < SLOTS else (i, n + 1 - LAG)
                    if ahead:
                        causal(*ahead)
                    if n == 12:
                        x_scaled(i)
                    if not first:
                        if n == 14:
                            pow_of(rms[:], ms[:], s_rms, s_ms, i, i)
                        if n == 18:
                            pow_of(rstd2[:], ve2[:], s_ln2pow, s_ln2, i * 9, i)

            one_pass(0)
            with pool.Fori(1, PAIRS) as i:
                one_pass(i)
            for n in range(LAG - 1):
                causal(PAIRS - 1, n + 1 - LAG + SLOTS)
            pow_of(rms[:], ms[:], s_rms, s_ms, PAIRS, PAIRS)
            pow_of(rstd2[:], ve2[:], s_ln2pow, s_ln2, PAIRS * 9, PAIRS)

        @block.vector
        def _(dve):
            def split_weights(c):
                dve.wait_ge(s_wld[c % 2], 16 * (c // 2 + 1))
                cols = slice((c % 2) * WQ, (c % 2 + 1) * WQ)
                raw = stage[:, cols]
                nc.vector.tensor_copy(w_hi[:, c // 2, cols], raw).then_inc(s_wsplit, 1)
                dve.wait_ge(s_wsplit, 2 * c + 1)
                nc.vector.tensor_tensor(w_lo[:, c // 2, cols], raw, w_hi[:, c // 2, cols].bitcast(F32),
                                        ALU.subtract).then_inc(s_wsplit, 1)

            def split_small():
                dve.wait_ge(s_const, 16 * 6)
                dve.wait_ge(s_wo, 32)
                wo = u_res[:, 0:2, :]
                for k in range(KT):
                    nc.vector.tensor_scalar(o_sb[:, k], wo[:, k], rw[:, k:k + 1], None, ALU.mult).then_inc(s_tc, 1)
                dve.wait_ge(s_tc, 2)
                nc.vector.tensor_copy(wo_hi[:].rearrange("p a b -> p (a b)"), o_sb[:, 0:2].rearrange("p a b -> p (a b)")).then_inc(s_tc, 1)
                za = z_silu[:, 0:3, :].rearrange("p a b -> p (a b)")[:, 0:KT * ZA]
                nc.vector.tensor_copy(za_hi[:].rearrange("p a b -> p (a b)"), za).then_inc(s_tc, 1)
                dve.wait_ge(s_tc, 4)
                nc.vector.tensor_tensor(wo_lo[:].rearrange("p a b -> p (a b)"), o_sb[:, 0:2].rearrange("p a b -> p (a b)"),
                                        wo_hi[:].rearrange("p a b -> p (a b)").bitcast(F32), ALU.subtract).then_inc(s_small, 1)
                nc.vector.tensor_tensor(za_lo[:].rearrange("p a b -> p (a b)"), za,
                                        za_hi[:].rearrange("p a b -> p (a b)").bitcast(F32), ALU.subtract).then_inc(s_small, 1)

            TC0 = 4

            def layernorm_in(i):
                dve.wait_ge(s_u, i * 16 + 16)
                if not isinstance(i, int):
                    dve.wait_ge(s_x1out, i * 16)
                    dve.wait_ge(s_tfull, jobs_before(i))
                for c in range(NBC):
                    nc.vector.bn_stats(stats[:, c], u_in[:, c]).then_inc(s_ln, 1)
                for c in range(NBC):
                    dve.wait_ge(s_ln, i * 13 + c + 1)
                    dve.sem_inc(s_held, 1)
                    nc.vector.bn_aggr(mv[:, c], stats[:, c]).then_inc(s_ln, 1)
                dve.wait_ge(s_ln, i * 13 + 8)
                nc.vector.tensor_scalar(ve[:], mv[:, :, 1], EPS, None, ALU.add).then_inc(s_ln, 1)
                dve.wait_ge(s_lnpow, i + 1)
                for c in range(NBC):
                    nc.vector.tensor_scalar(u_norm[:, c], u_in[:, c], mv[:, c, 0:1], rstd[:, c:c + 1],
                                            ALU.subtract, ALU.mult).then_inc(s_ln, 1)

            def take(name, i):
                dve.wait_ge(s_tfull, job(name, i) + 1)
                return p_t[bank(name, i)]

            def split_job(name, i, hi, lo, count):
                t = take(name, i)
                nc.vector.tensor_copy(hi, t[:]).then_inc(s_tc, 1)
                dve.wait_ge(s_tc, count)
                nc.vector.tensor_tensor(lo, t[:], hi.bitcast(F32), ALU.subtract).then_inc(s_tdone, 1)

            def take_norm(i):
                if not isinstance(i, int):
                    dve.wait_ge(s_proj, i * TILES)
                for k in range(KT):
                    base = i * 4 + (TC0 + k + 1 - 2) if not isinstance(i, int) else TC0 + k + 1
                    split_job(f"XH{k}", i, xh_hi[:, k], xh_lo[:, k], base)

            def take_za(i, c):
                t = take(f"ZA{c}", i)
                if not isinstance(i, int) and c == 0:
                    dve.wait_ge(s_zsilu, i)
                nc.vector.tensor_tensor(z_raw[:, c], t[:, 0:DM], zb[:], ALU.add)
                nc.vector.tensor_copy(a_log[:, c], t[:, DM:ZA]).then_inc(s_tdone, 1)

            def flat(t):
                return t[:].rearrange("p a b -> p (a b)")

            def abs_a(i):
                dve.wait_ge(s_tdone, job("ZA3", i) + 1)
                nc.vector.scalar_tensor_tensor(out=flat(a_abs), in0=flat(a_log), scalar=-1.0, in1=flat(a_log),
                                               op0=ALU.mult, op1=ALU.max).then_inc(s_abs, 1)

            def softplus_sum(i):
                dve.wait_ge(s_sp2, i + 1)
                if not isinstance(i, int):
                    dve.wait_ge(s_tfull, jobs_before(i))
                nc.vector.scalar_tensor_tensor(out=flat(sp), in0=flat(a_log), scalar=0.0, in1=flat(a_abs),
                                               op0=ALU.max, op1=ALU.add).then_inc(s_sp, 1)

            def take_cs(i):
                t = take("CST", i)
                if not isinstance(i, int):
                    dve.wait_ge(s_csst, i * 16)
                cs = t[0:HEADS, :]
                nc.vector.tensor_copy(cs_parts[:, 0], cs).then_inc(s_parts, 1)
                dve.wait_ge(s_parts, i * 3 + 1)
                nc.vector.tensor_tensor(cs_rest[:], cs, cs_parts[:, 0], ALU.subtract).then_inc(s_parts, 1)
                dve.wait_ge(s_parts, i * 3 + 2)
                nc.vector.tensor_copy(cs_parts[:, 1], cs_rest[:]).then_inc(s_tdone, 1)
                t = take("CSK", i)
                if not isinstance(i, int):
                    dve.wait_ge(s_ecs, i)
                nc.vector.tensor_copy(flat(cs_k), t[:, 0:NBC * HEADS]).then_inc(s_tdone, 1)
                dve.wait_ge(s_tdone, job("CST", i) + 1)
                nc.vector.tensor_tensor(cs_parts[:, 2], cs_rest[:], cs_parts[:, 1], ALU.subtract).then_inc(s_parts, 1)

            def take_x(i):
                for x in range(XT):
                    t = take(f"XT{x}", i)
                    if not isinstance(i, int) and x == 0:
                        dve.wait_ge(s_y, i * SLOTS)
                        dve.wait_ge(s_xskip, i * 5)
                    nc.vector.tensor_copy(x_tok[:, :, x * P:(x + 1) * P],
                                          t[:].rearrange("p (c n) -> p c n", c=NBC)).then_inc(s_tdone, 1)

            def take_b(i, q, h, body, tag):
                t = take(f"BT{q}{h}{tag}", body)
                nc.vector.tensor_copy(b_tok[:, h], t[:]).then_inc(s_tdone, 1)

            def take_states(i, q, body, tag):
                t = take(f"ST{q}{tag}", body)
                if not (isinstance(i, int) and i == 0 and q == 0):
                    dve.wait_ge(s_yoff, i * QUADS + q)
                for e in range(2):
                    rows = slice(e * NSTATE, (e + 1) * NSTATE)
                    cols = slice(e * HDIM, (e + 1) * HDIM)
                    r = nc.vector.tensor_copy(states[rows, :, :, cols].rearrange("p a b c -> p (a b) c"),
                                              t[rows, 0:16 * HDIM].rearrange("p (a c) -> p a c", c=2 * HDIM)[:, :, cols])
                r.then_inc(s_tdone, 1)

            def taps(i, m, w):
                shift = TAPS - 1 - w
                dst = xT[:, m] if m < XT else bc[:, tile_of(m - XT)]
                d3 = dst.rearrange("p (b t) -> p b t", b=2)
                src = p_proj[m % 2][:].rearrange("p (b t) -> p b t", b=2)
                before, done = {2: (s_tap3, s_tap2), 1: (s_tap2, s_tap1), 0: (s_tap1, s_tap0)}[w]
                dve.wait_ge(before, i * TILES + m + 1)
                nc.vector.scalar_tensor_tensor(out=d3[:, :, shift:], in0=src[:, :, :SEQ - shift], scalar=cw[:, m, w:w + 1],
                                               in1=d3[:, :, shift:], op0=ALU.mult, op1=ALU.add).then_inc(done, 1)

            def mix(i, g):
                dve.wait_ge(s_mask, i * SLOTS + g + 1)
                dve.wait_ge(s_g, i * SLOTS + g + 1)
                if not (isinstance(i, int) and i == 0 and g < NM):
                    dve.wait_ge(s_y, i * SLOTS + g - NM + 1)
                nc.vector.tensor_tensor(mixed[:, g % NM], p_g[g % 2][:], decay[:, g % NL], ALU.mult).then_inc(s_m, 1)

            def take_y(i, q):
                dve.wait_ge(s_y, i * SLOTS + (q + 1) * QH)
                dve.wait_ge(s_yoff, i * QUADS + q + 1)
                dve.wait_ge(s_xskip, i * 5 + 5)
                cols = slice(q * QH * HDIM, (q + 1) * QH * HDIM)
                nc.vector.tensor_tensor(y_sum[:, :, cols], p_y[:, 0:256].rearrange("p (c n) -> p c n", c=NBC),
                                        x_skip[:, :, cols], ALU.add).then_inc(s_yev, 1)
                nc.vector.tensor_tensor(y_tmp[:].rearrange("p b (h d) -> p b h d", d=HDIM),
                                        p_y[:, 256:384].rearrange("p (b h d) -> p b h d", b=2, d=HDIM),
                                        e_cs[:, 1::2, q * QH:(q + 1) * QH].unsqueeze(3).broadcast_to([P, 2, QH, HDIM]),
                                        ALU.mult).then_inc(s_yev, 1)
                dve.wait_ge(s_yev, i * 12 + 3 * q + 2)
                nc.vector.tensor_tensor(y_sum[:, 1::2, cols], y_sum[:, 1::2, cols], y_tmp[:], ALU.add).then_inc(s_yev, 1)

            def gate(i):
                dve.wait_ge(s_yev, i * 12 + 12)
                dve.wait_ge(s_zsilu, i + 1)
                dve.wait_ge(s_x1out, i * 16 + 16)
                nc.vector.tensor_tensor(flat(yg), flat(y_sum), flat(z_silu), ALU.mult).then_inc(s_yg, 1)

            def mean_squares(i):
                dve.wait_ge(s_sq, i * 4 + 4)
                nc.vector.tensor_scalar(ms[:], ss[:], 1.0 / DM, EPS, ALU.mult, ALU.add).then_inc(s_ms, 1)

            def rms_norm(i):
                dve.wait_ge(s_rms, i + 1)
                for c in range(NBC):
                    nc.vector.tensor_scalar(yg[:, c], yg[:, c], rms[:, c:c + 1], None, ALU.mult).then_inc(s_yn, 1)

            def take_yT(i, body):
                for k in range(KT):
                    if isinstance(i, int):
                        count = TC0 + 4 * (PAIRS - 1) + 2 + k + 1
                    else:
                        count = body * 4 + (TC0 + k + 1)
                    split_job(f"YT{k}-", body, yT_hi[:, k], yT_lo[:, k], count)

            def take_out(i, h, body):
                t = take(f"OP{h}-", body)
                nc.vector.tensor_copy(o_sb[:, 2 * h:2 * h + 2].rearrange("p a b -> p (a b)"), t[:]).then_inc(s_tdone, 1)

            def layernorm_out(i, body):
                for c in range(NBC):
                    dve.wait_ge(s_tdone, job("OP1-", body) + 1)
                    nc.vector.bn_stats(stats2[:, c], o_sb[:, c]).then_inc(s_ln2, 1)
                for c in range(NBC):
                    dve.wait_ge(s_ln2, i * 9 + c + 1)
                    dve.sem_inc(s_held, 1)
                    nc.vector.bn_aggr(mv2[:, c], stats2[:, c]).then_inc(s_ln2, 1)
                dve.wait_ge(s_ln2, i * 9 + 8)
                nc.vector.tensor_scalar(ve2[:], mv2[:, :, 1], EPS, None, ALU.add).then_inc(s_ln2, 1)

            def residual_sum(i):
                dve.wait_ge(s_ln2pow, i + 1)
                for c in range(NBC):
                    nc.vector.tensor_scalar(o_sb[:, c], o_sb[:, c], mv2[:, c, 0:1], rstd2[:, c:c + 1],
                                            ALU.subtract, ALU.mult).then_inc(s_xn2, 1)
                dve.wait_ge(s_xn2, i * 4 + 4)
                dve.wait_ge(s_ures, i * 16 + 16)
                nc.vector.tensor_tensor(flat(o_sb), flat(o_sb), flat(u_res), ALU.add).then_inc(s_x1, 1)

            def slot_attention(n, i, tail=False):
                now = ((i - 1, n - LAG + SLOTS) if n < LAG else None) if tail else heads_at(n, i)
                if now:
                    ii, g = now
                    q, h = g // QH, g % QH
                    tag = "-" if n < LAG else ""
                    mix(ii, g)
                    if h in (0, 1):
                        take_b(ii, q, h, i, tag)
                    if h == 3:
                        take_states(ii, q, i, tag)
                behind = heads_at(n - 1, i) if n >= 1 else (None if isinstance(i, int) and i == 0 else (i - 1, SLOTS - 1 - LAG))
                if behind and behind[1] % QH == QH - 1:
                    take_y(behind[0], behind[1] // QH)

            def one_pass(i):
                first = isinstance(i, int)
                layernorm_in(i)
                take_norm(i)
                for w in (2, 1, 0):
                    taps(i, 0, w)
                    taps(i, 1, w)
                for n in range(SLOTS):
                    taps(i, XT + n, 2)
                    if n:
                        taps(i, XT + n - 1, 0)
                    taps(i, XT + n, 1)
                    if n < NBC:
                        take_za(i, n)
                    if n == NBC:
                        abs_a(i)
                    if n == 5:
                        softplus_sum(i)
                    if n == 6:
                        take_cs(i)
                    if n == LAG:
                        take_x(i)
                    slot_attention(n, i)
                    if not first:
                        if n == 12:
                            gate(i - 1)
                        if n == 13:
                            mean_squares(i - 1)
                        if n == 14:
                            rms_norm(i - 1)
                        if n == 15:
                            take_yT(i - 1, i)
                        if n in (16, 17):
                            take_out(i - 1, n - 16, i)
                        if n == 17:
                            layernorm_out(i - 1, i)
                        if n == 19:
                            residual_sum(i - 1)
                taps(i, TILES - 1, 0)

            split_small()
            for c in range(4):
                split_weights(c)
            one_pass(0)
            with dve.Fori(1, PAIRS) as i:
                one_pass(i)
            for n in range(LAG + 1):
                slot_attention(n, PAIRS, tail=True)
            gate(PAIRS - 1)
            mean_squares(PAIRS - 1)
            rms_norm(PAIRS - 1)
            take_yT(PAIRS - 1, PAIRS)
            take_out(PAIRS - 1, 0, PAIRS)
            take_out(PAIRS - 1, 1, PAIRS)
            layernorm_out(PAIRS - 1, PAIRS)
            residual_sum(PAIRS - 1)


def expert_block(nc, x1_dram, w_up, b_up, w_down, b_down, w_gate, mats, out):
    with ExitStack() as ctx:
        def sb(name, shape, dt=F32):
            return ctx.enter_context(nc.sbuf_tensor(name, shape, dt))

        def ps(name):
            return ctx.enter_context(nc.psum_tensor(name, [P, 512], F32))

        def sem(name):
            return ctx.enter_context(nc.semaphore(name))

        E = 2
        up_hi, up_lo = sb("up_hi", [P, E * KT, FF], F32R), sb("up_lo", [P, E * KT, FF], F32R)
        dn_hi, dn_lo = sb("dn_hi", [P, E * FT, DM], F32R), sb("dn_lo", [P, E * FT, DM], F32R)
        gt_hi, gt_lo = sb("gt_hi", [P, KT * E], F32R), sb("gt_lo", [P, KT * E], F32R)
        raw_up, raw_dn, raw_gt = sb("raw_up", [P, E * KT, FF]), sb("raw_dn", [P, E * FT, DM]), sb("raw_gt", [P, KT * E])
        ident = sb("f_ident", [P, P])
        bu = sb("bu", [P, E * FT])
        bd = sb("bd", [P, E, DM])
        x_in, x_norm, x_res = sb("x_in", [P, NBC, DM]), sb("x_norm", [P, NBC, DM]), sb("x_res", [P, NBC, DM])
        xh_hi, xh_lo = sb("f_xh_hi", [P, KT, TOK], F32R), sb("f_xh_lo", [P, KT, TOK], F32R)
        hid = sb("hid", [P, 2, TOK])
        h_hi, h_lo = sb("h_hi", [P, E * FT, TOK], F32R), sb("h_lo", [P, E * FT, TOK], F32R)
        y0, y1 = sb("y0", [P, NBC, DM]), sb("y1", [P, NBC, DM])
        first_wins, second_wins = sb("first_wins", [P, NBC]), sb("second_wins", [P, NBC])
        logits = sb("logits", [P, NBC, E])
        stats, mv = sb("f_stats", [P, NBC, 6]), sb("f_mv", [P, NBC, 2])
        ve, rstd = sb("f_ve", [P, NBC]), sb("f_rstd", [P, NBC])
        stats2, mv2 = sb("f_stats2", [P, NBC, 6]), sb("f_mv2", [P, NBC, 2])
        ve2, rstd2 = sb("f_ve2", [P, NBC]), sb("f_rstd2", [P, NBC])
        mhalf = sb("f_mhalf", [P, NBC])

        p_up = [ps("p_up0"), ps("p_up1")]
        p_dn = [[ps(f"p_dn{h}{e}") for e in range(E)] for h in range(2)]
        p_x, p_gt = ps("p_x"), ps("p_gt")

        f_wld, f_wsplit, f_x, f_ln, f_pow, f_init = (sem(n) for n in ("f_wld", "f_wsplit", "f_x", "f_ln", "f_pow", "f_init"))
        f_tr, f_xh, f_gl, f_gate = (sem(n) for n in ("f_tr", "f_xh", "f_gl", "f_gate"))
        f_up, f_act, f_h, f_hhi, f_dn, f_y = (sem(n) for n in ("f_up", "f_act", "f_h", "f_hhi", "f_dn", "f_y"))
        f_ln2, f_pow2, f_res, f_sum, f_out, f_comb = (sem(n) for n in ("f_ln2", "f_pow2", "f_res", "f_sum", "f_out", "f_comb"))
        f_nrm, f_held = sem("f_nrm"), sem("f_held")

        x1_p = x1_dram.rearrange("i (k p) d -> i p k d", p=P)
        out_p = out.rearrange("(i b) (c p) d -> i p (b c) d", b=2, p=P)

        def of_pass(t, i):
            if isinstance(i, int):
                return t[i]
            return t[bass.ds(i, 1)].rearrange("o p k d -> (o p) k d")

        def flat(t):
            return t[:].rearrange("p a b -> p (a b)")

        block = ctx.enter_context(nc.Block())

        def start_only(i, n=1):
            return isinstance(i, int) and i < n

        def run(eng, one_pass):
            one_pass(0)
            with eng.Fori(1, PAIRS - 1) as i:
                one_pass(i)
            one_pass(PAIRS - 1)

        def is_last(i):
            return isinstance(i, int) and i == PAIRS - 1

        @block.sync
        def _(sp_):
            sp_.dma_start(x_in[:], of_pass(x1_p, 0)).then_inc(f_x, 16)
            sp_.dma_start(raw_up[:], w_up.rearrange("e (k p) n -> p (e k) n", p=P)).then_inc(f_wld, 16)
            sp_.dma_start(raw_dn[:], w_down.rearrange("e (f p) n -> p (e f) n", p=P)).then_inc(f_wld, 16)
            sp_.dma_start(raw_gt[:], w_gate).then_inc(f_wld, 16)
            sp_.dma_start(ident[:], mats[:, 0:P]).then_inc(f_wld, 16)
            sp_.dma_start(bu[:], b_up).then_inc(f_wld, 16)
            sp_.dma_start(flat(bd), b_down.rearrange("(o n) -> o n", o=1).broadcast_to([P, E * DM])).then_inc(f_wld, 16)

            def one_pass(i):
                if not is_last(i):
                    sp_.wait_ge(f_ln, i * 13 + 13)
                    sp_.dma_start(x_in[:], of_pass(x1_p, i + 1)).then_inc(f_x, 16)
                if not start_only(i):
                    sp_.wait_ge(f_sum, i)
                sp_.dma_start(x_res[:], of_pass(x1_p, i)).then_inc(f_res, 16)
                sp_.wait_ge(f_sum, i + 1)
                sp_.dma_start(of_pass(out_p, i), y0[:]).then_inc(f_out, 16)

            run(sp_, one_pass)
            sp_.wait_ge(f_out, 16 * PAIRS)

        @block.tensor
        def _(pe):
            def split3(out_, a, a2, b, b2, first, last):
                for m, (x, y) in enumerate(((a, b), (a, b2), (a2, b))):
                    r = nc.tensor.matmul(out_, x, y, start=(first and m == 0), stop=(last and m == 2))
                return r

            def transposes(i):
                pe.wait_ge(f_ln, i * 13 + 13)
                for k in range(KT):
                    if not (start_only(i) and k == 0):
                        pe.wait_ge(f_xh, i * 4 + 2 * k)
                    for c in range(NBC):
                        r = nc.tensor.transpose(p_x[:, c * P:(c + 1) * P], x_norm[:, c, k * P:(k + 1) * P], ident[:])
                    r.then_inc(f_tr, 1)

            def gate_logits(i):
                pe.wait_ge(f_xh, i * 4 + 4)
                if not start_only(i):
                    pe.wait_ge(f_gate, i * 3)
                for c in range(NBC):
                    cols = slice(c * P, (c + 1) * P)
                    for k in range(KT):
                        r = split3(p_gt[:, c * E:(c + 1) * E], xh_hi[:, k, cols], xh_lo[:, k, cols],
                                   gt_hi[:, k * E:(k + 1) * E], gt_lo[:, k * E:(k + 1) * E], k == 0, k == KT - 1)
                r.then_inc(f_gl, 1)

            def up(i):
                for m in range(E * FT):
                    e, f = m // FT, m % FT
                    if not (start_only(i) and m < 2):
                        pe.wait_ge(f_act, i * (E * FT) + m - 1)
                    cols = slice(f * P, (f + 1) * P)
                    for k in range(KT):
                        r = split3(p_up[m % 2][:], up_hi[:, e * KT + k, cols], up_lo[:, e * KT + k, cols],
                                   xh_hi[:, k], xh_lo[:, k], k == 0, k == KT - 1)
                    r.then_inc(f_up, 1)

            def down(i):
                for e in range(E):
                    pe.wait_ge(f_h, i * (E * FT) + (e + 1) * FT)
                    for h in range(2):
                        if not start_only(i):
                            pe.wait_ge(f_y, (i - 1) * 4 + 2 * h + e + 1)
                        for c in range(2):
                            cols = slice((2 * h + c) * P, (2 * h + c + 1) * P)
                            for f in range(FT):
                                r = split3(p_dn[h][e][:, c * DM:(c + 1) * DM], h_hi[:, e * FT + f, cols],
                                           h_lo[:, e * FT + f, cols], dn_hi[:, e * FT + f], dn_lo[:, e * FT + f],
                                           f == 0, f == FT - 1)
                        r.then_inc(f_dn, 1)

            def one_pass(i):
                gate_logits(i)
                up(i)
                if not is_last(i):
                    transposes(i + 1)
                down(i)

            pe.wait_ge(f_wld, 16 * 6)
            transposes(0)
            pe.wait_ge(f_wsplit, 6)
            run(pe, one_pass)

        @block.scalar
        def _(act):
            def one_pass(i):
                for m in range(E * FT):
                    act.wait_ge(f_up, i * (E * FT) + m + 1)
                    if not (start_only(i) and m < 2):
                        act.wait_ge(f_h, i * (E * FT) + m - 1)
                    nc.scalar.activation(hid[:, m % 2], p_up[m % 2][:], ACT.Gelu if m < FT else ACT.Relu,
                                         bias=bu[:, m:m + 1]).then_inc(f_act, 1)

            act.wait_ge(f_wld, 16 * 6)
            run(act, one_pass)

        @block.gpsimd
        def _(pool):
            def norm_pow(i):
                pool.wait_ge(f_ln, i * 13 + 9)
                pool.tensor_tensor(rstd[:], ve[:], mhalf[:], ALU.pow).then_inc(f_pow, 1)

            def one_pass(i):
                if not is_last(i):
                    norm_pow(i + 1)
                pool.wait_ge(f_ln2, i * 9 + 9)
                pool.tensor_tensor(rstd2[:], ve2[:], mhalf[:], ALU.pow).then_inc(f_pow2, 1)

            pool.memset(mhalf[:], -0.5).then_inc(f_init, 1)
            pool.wait_ge(f_init, 1)
            norm_pow(0)
            run(pool, one_pass)

        @block.vector
        def _(dve):
            def split(hi, lo, raw, n):
                nc.vector.tensor_copy(flat(hi) if len(hi.shape) == 3 else hi[:], raw).then_inc(f_wsplit, 1)
                dve.wait_ge(f_wsplit, n + 1)
                nc.vector.tensor_tensor(flat(lo) if len(lo.shape) == 3 else lo[:], raw,
                                        (flat(hi) if len(hi.shape) == 3 else hi[:]).bitcast(F32),
                                        ALU.subtract).then_inc(f_wsplit, 1)

            def norm_stats(i):
                dve.wait_ge(f_x, i * 16 + 16)
                for c in range(NBC):
                    nc.vector.bn_stats(stats[:, c], x_in[:, c]).then_inc(f_ln, 1)
                for c in range(NBC):
                    dve.wait_ge(f_ln, i * 13 + c + 1)
                    dve.sem_inc(f_held, 1)
                    nc.vector.bn_aggr(mv[:, c], stats[:, c]).then_inc(f_ln, 1)
                dve.wait_ge(f_ln, i * 13 + 8)
                nc.vector.tensor_scalar(ve[:], mv[:, :, 1], EPS, None, ALU.add).then_inc(f_ln, 1)

            def norm_apply(i):
                dve.wait_ge(f_pow, i + 1)
                if not start_only(i):
                    dve.wait_ge(f_tr, i * KT)
                for c in range(NBC):
                    nc.vector.tensor_scalar(x_norm[:, c], x_in[:, c], mv[:, c, 0:1], rstd[:, c:c + 1],
                                            ALU.subtract, ALU.mult).then_inc(f_ln, 1)

            def split_norm(i):
                if not start_only(i):
                    dve.wait_ge(f_up, i * (E * FT))
                for k in range(KT):
                    dve.wait_ge(f_tr, i * KT + k + 1)
                    nc.vector.tensor_copy(xh_hi[:, k], p_x[:]).then_inc(f_xh, 1)
                    dve.wait_ge(f_xh, i * 4 + 2 * k + 1)
                    nc.vector.tensor_tensor(xh_lo[:, k], p_x[:], xh_hi[:, k].bitcast(F32), ALU.subtract).then_inc(f_xh, 1)

            def gate(i):
                dve.wait_ge(f_gl, i + 1)
                nc.vector.tensor_copy(flat(logits), p_gt[:, 0:NBC * E]).then_inc(f_gate, 1)
                dve.wait_ge(f_gate, i * 3 + 1)
                nc.vector.tensor_tensor(first_wins[:], logits[:, :, 0], logits[:, :, 1], ALU.is_ge).then_inc(f_gate, 1)
                dve.wait_ge(f_gate, i * 3 + 2)
                nc.vector.tensor_scalar(second_wins[:], first_wins[:], -1.0, 1.0, ALU.mult, ALU.add).then_inc(f_gate, 1)

            def split_hidden(i, m):
                dve.wait_ge(f_act, i * (E * FT) + m + 1)
                if not start_only(i) and m % FT == 0:
                    dve.wait_ge(f_dn, (i - 1) * 4 + 2 * (m // FT) + 2)
                nc.vector.tensor_copy(h_hi[:, m], hid[:, m % 2]).then_inc(f_hhi, 1)
                dve.wait_ge(f_hhi, i * (E * FT) + m + 1)
                nc.vector.tensor_tensor(h_lo[:, m], hid[:, m % 2], h_hi[:, m].bitcast(F32), ALU.subtract).then_inc(f_h, 1)

            def combine(i):
                dve.wait_ge(f_gate, i * 3 + 3)
                if not start_only(i):
                    dve.wait_ge(f_out, i * 16)
                for h in range(2):
                    for e, y in enumerate((y0, y1)):
                        dve.wait_ge(f_dn, i * 4 + 2 * e + h + 1)
                        nc.vector.tensor_tensor(y[:, 2 * h:2 * h + 2], p_dn[h][e][:].rearrange("p (c n) -> p c n", c=2),
                                                bd[:, e].unsqueeze(1).broadcast_to([P, 2, DM]), ALU.add).then_inc(f_y, 1)
                n = i * 12
                for c in range(NBC):
                    dve.wait_ge(f_y, i * 4 + 2 * (c // 2) + 2)
                    nc.vector.tensor_scalar(y1[:, c], y1[:, c], second_wins[:, c:c + 1], None, ALU.mult).then_inc(f_comb, 1)
                for c in range(NBC):
                    dve.wait_ge(f_comb, i * 8 + c + 1)
                    nc.vector.scalar_tensor_tensor(out=y0[:, c], in0=y0[:, c], scalar=first_wins[:, c:c + 1],
                                                   in1=y1[:, c], op0=ALU.mult, op1=ALU.add).then_inc(f_comb, 1)
                for c in range(NBC):
                    dve.wait_ge(f_comb, i * 8 + 4 + c + 1)
                    nc.vector.bn_stats(stats2[:, c], y0[:, c]).then_inc(f_ln2, 1)
                for c in range(NBC):
                    dve.wait_ge(f_ln2, i * 9 + c + 1)
                    dve.sem_inc(f_held, 1)
                    nc.vector.bn_aggr(mv2[:, c], stats2[:, c]).then_inc(f_ln2, 1)
                dve.wait_ge(f_ln2, i * 9 + 8)
                nc.vector.tensor_scalar(ve2[:], mv2[:, :, 1], EPS, None, ALU.add).then_inc(f_ln2, 1)
                dve.wait_ge(f_pow2, i + 1)
                dve.wait_ge(f_res, i * 16 + 16)
                for c in range(NBC):
                    nc.vector.tensor_scalar(y1[:, c], y0[:, c], mv2[:, c, 0:1], rstd2[:, c:c + 1],
                                            ALU.subtract, ALU.mult).then_inc(f_nrm, 1)
                dve.wait_ge(f_nrm, i * 4 + 4)
                nc.vector.tensor_tensor(flat(y0), flat(y1), flat(x_res), ALU.add).then_inc(f_sum, 1)

            def one_pass(i):
                gate(i)
                for m in range(E * FT):
                    split_hidden(i, m)
                    if not is_last(i):
                        if m == 2:
                            norm_stats(i + 1)
                        if m == 4:
                            norm_apply(i + 1)
                if not is_last(i):
                    split_norm(i + 1)
                combine(i)

            norm_stats(0)
            norm_apply(0)
            split_norm(0)
            dve.wait_ge(f_wld, 16 * 6)
            split(up_hi, up_lo, flat(raw_up), 0)
            split(dn_hi, dn_lo, flat(raw_dn), 2)
            split(gt_hi, gt_lo, raw_gt[:], 4)
            run(dve, one_pass)


def kernel(L0_attn_u, L0_attn_W_in, L0_attn_z_bias, L0_attn_conv_w, L0_attn_conv_b, L0_attn_D, L0_attn_rms_w,
           L0_attn_W_out, L0_ffn_Wg, L0_ffn_W0a, L0_ffn_b0a, L0_ffn_W0b, L0_ffn_b0b, L0_ffn_W1a, L0_ffn_b1a,
           L0_ffn_W1b, L0_ffn_b1b):
    import concourse.bacc as bacc
    from concourse.bass_utils import run_bass_kernel_spmd

    a = np.asarray
    rows = lay_out()
    w_in = a(L0_attn_W_in)
    conv_rows = HEADS * HDIM + 2 * HEADS * NSTATE
    mats, pick, marks = constants()
    arrays = {
        "u": a(L0_attn_u),
        "w_tiles": w_in[rows].T,
        "w_za": w_in[conv_rows:].T,
        "z_bias": a(L0_attn_z_bias),
        "conv_w": a(L0_attn_conv_w)[rows].reshape(TILES, P, TAPS).transpose(1, 0, 2),
        "conv_b": a(L0_attn_conv_b)[rows].reshape(TILES, P).T,
        "d_skip": a(L0_attn_D),
        "rms_w": a(L0_attn_rms_w).reshape(KT, P).T,
        "w_out": a(L0_attn_W_out).T,
        "mats": mats,
        "pick": pick,
        "marks": marks,
        "w_up": np.stack([a(L0_ffn_W0a).T, a(L0_ffn_W1a).T]),
        "b_up": np.concatenate([a(L0_ffn_b0a), a(L0_ffn_b1a)]).reshape(-1, P).T,
        "w_down": np.stack([a(L0_ffn_W0b).T, a(L0_ffn_W1b).T]),
        "b_down": np.concatenate([a(L0_ffn_b0b), a(L0_ffn_b1b)]),
        "w_gate": a(L0_ffn_Wg).reshape(2, KT, P).transpose(2, 1, 0).reshape(P, KT * 2),
    }
    arrays = {k: np.ascontiguousarray(v) for k, v in arrays.items()}
    nc = bacc.Bacc("TRN2", target_bir_lowering=False, num_devices=1)
    t = {k: nc.dram_tensor(k, v.shape, F32, kind="ExternalInput").ap() for k, v in arrays.items()}
    out = nc.dram_tensor("out", (BATCH, SEQ, DM), F32, kind="ExternalOutput").ap()
    cs_dram = nc.dram_tensor("cs_dram", (3, HEADS, TOK), BF16, kind="Internal").ap()
    x1_dram = nc.dram_tensor("x1_dram", (PAIRS, TOK, DM), F32, kind="Internal").ap()
    mamba_block(nc, t["u"], t["w_tiles"], t["w_za"], t["z_bias"], t["conv_w"], t["conv_b"], t["d_skip"], t["rms_w"],
                t["w_out"], t["mats"], t["pick"], t["marks"],
                cs_dram, x1_dram)
    expert_block(nc, x1_dram, t["w_up"], t["b_up"], t["w_down"], t["b_down"], t["w_gate"], t["mats"], out)
    r = run_bass_kernel_spmd(nc, [arrays], core_ids=[0])
    return r.results[0]["out"]
```

```python
from contextlib import ExitStack

import concourse.bass as bass
import numpy as np
from concourse import mybir

F32 = mybir.dt.float32
F32R = mybir.dt.float32r
BF16 = mybir.dt.bfloat16
ALU = mybir.AluOpType
ACT = mybir.ActivationFunctionType

P = 128
BATCH, SEQ, DM = 16, 256, 256
HEADS, NSTATE, HDIM, TAPS = 32, 64, 8, 4
PAIRS = BATCH // 2
TOK = 2 * SEQ
NBC = TOK // P
KT = DM // P
XT = HEADS * HDIM // P
NT = HEADS * NSTATE // P
TILES = XT + 2 * NT
QUADS, QH, QT = 4, 8, 8
SLOTS = 2 * NT
ZA = DM + HEADS
FF = 2 * DM
FT = FF // P
EPS = 1e-5
LAG = 11
STEP = 4
GUARDS = P // STEP - 1
CSL = 3 * QH
HPT = CSL + 3 + GUARDS

def slot_jobs(n, first):
    jobs = []
    g = n - LAG
    q, u = (g % SLOTS) // QH, g % QH
    tag = "-" if g < 0 else ""
    if u == 3 and (g >= 0 or not first):
        jobs.append(f"ST{q}{tag}")
    if n < NBC:
        jobs.append(f"ZA{n}")
    if n in (6, 7):
        jobs.append("CST" if n == 6 else "CSK")
    if n == LAG:
        jobs += ["XT0", "XT1"]
    if u in (0, 1) and (g >= 0 or not first):
        jobs.append(f"BT{q}{u}{tag}")
    if not first:
        if n == 15:
            jobs += ["YT0-", "YT1-"]
        if n in (16, 17):
            jobs.append(f"OP{n - 16}-")
    if n == SLOTS - 1:
        jobs += ["XH0+", "XH1+"]
    return jobs


JOBS = {first: sum((slot_jobs(n, first) for n in range(SLOTS)), []) for first in (True, False)}
TAIL_JOBS = ["BT30-", "BT31-", "ST3-", "YT0-", "YT1-", "OP0-", "OP1-"]
JOBS_AHEAD = KT
JOBS_FIRST, JOBS_EACH = len(JOBS[True]), len(JOBS[False])


def taker(name):
    return "act" if name[:2] in ("BT", "XT", "OP") else "dve"


def count_of(names, engine):
    return sum(taker(name) == engine for name in names)


assert JOBS_EACH % 2 == 0

LEAD = [3, 2, 1, 1, 1, 1, 1, 2]


def decays_of(n):
    return range(LEAD[(n - 1) % QH], LEAD[n % QH] + 1)


def seq(n):
    return (1, 3)[n] if n < 2 else n + XT


def lay_out():
    nx, ns = HEADS * HDIM, HEADS * NSTATE
    first = {0: 0, 2: P}
    for t in range(NT):
        first[seq(2 * t)] = nx + t * P
        first[seq(2 * t + 1)] = nx + ns + t * P
    return np.concatenate([np.arange(P) + first[m] for m in range(TILES)])


def constants():
    s = np.arange(P)
    ident = np.eye(P, dtype=np.float32)
    upto = -(s[:, None] <= s[None, :]).astype(np.float32)
    beyond = -(s[:, None] > s[None, :]).astype(np.float32)
    mats = np.stack([ident, upto, beyond], axis=1).reshape(P, 3 * P)
    pick = np.zeros((HPT, QH, NBC, P), np.float32)
    for part in range(3):
        for k in range(QH):
            pick[part * QH + k, k] = -1.0
    for r in range(GUARDS):
        pick[CSL + 3 + r, :, :, :(r + 1) * STEP] = -1e30
    marks = np.zeros((HPT - CSL, QUADS, NBC, P), np.float32)
    marks[:3] = 1.0
    for r in range(GUARDS):
        marks[3 + r, :, :, (r + 1) * STEP:(r + 2) * STEP] = 1.0
    return np.ascontiguousarray(mats), pick.reshape(HPT, QH, TOK), marks.reshape(HPT - CSL, QUADS, TOK)


def mamba_block(nc, u, w_tiles, w_za, z_bias, conv_w, conv_b, d_skip, rms_w, w_out, mats, pick, marks, cs_dram, x1_dram):
    with ExitStack() as ctx:
        def sb(name, shape, dt=F32):
            return ctx.enter_context(nc.sbuf_tensor(name, shape, dt))

        def ps(name, shape=(P, 512)):
            return ctx.enter_context(nc.psum_tensor(name, list(shape), F32))

        def sem(name):
            return ctx.enter_context(nc.semaphore(name))

        w_hi, w_lo = sb("w_hi", [P, KT, TILES * P], F32R), sb("w_lo", [P, KT, TILES * P], F32R)
        za_hi, za_lo = sb("za_hi", [P, KT, ZA], F32R), sb("za_lo", [P, KT, ZA], F32R)
        wo_hi, wo_lo = sb("wo_hi", [P, KT, DM], F32R), sb("wo_lo", [P, KT, DM], F32R)
        bc = sb("bc", [P, 2 * QT, TOK])
        xT = sb("xT", [P, XT, TOK])
        u_in = sb("u_in", [P, NBC, DM])
        u_norm = sb("u_norm", [P, NBC, DM])
        xh_hi, xh_lo = sb("xh_hi", [P, KT, TOK], F32R), sb("xh_lo", [P, KT, TOK], F32R)
        z_raw, z_silu = sb("z_raw", [P, NBC, DM]), sb("z_silu", [P, NBC, DM])
        u_res = z_raw
        x_tok = sb("x_tok", [P, NBC, DM])
        x_skip = sb("x_skip", [P, NBC, DM])
        x_dec = sb("x_dec", [P, 2, DM])
        y_sum = sb("y_sum", [P, NBC, DM])
        y_tmp = sb("y_tmp", [P, 2, QH * HDIM])
        yg = o_sb = u_norm
        yT_hi, yT_lo = sb("yT_hi", [P, KT, TOK], F32R), sb("yT_lo", [P, KT, TOK], F32R)
        NL, NM = 4, 2
        decay = sb("decay", [P, NL, TOK])
        mixed = sb("mixed", [P, NM, TOK])
        b_tok = sb("b_tok", [P, 2, TOK])
        states = sb("states", [P, 4, 2, 2 * HDIM])
        a_log, a_abs, sp = sb("a_log", [P, NBC, HEADS]), sb("a_abs", [P, NBC, HEADS]), sb("sp", [P, NBC, HEADS])
        cs_k, e_cs = sb("cs_k", [P, NBC, HEADS]), sb("e_cs", [P, NBC, HEADS])
        cs_rest = sb("cs_rest", [HEADS, TOK])
        cs_parts = sb("cs_parts", [HEADS, 3, TOK], BF16)
        d_stat = sb("d_stat", [HPT, QUADS, TOK], BF16)
        d_mov = sb("d_mov", [HPT, 2, QH, TOK], BF16)
        mats_sb = sb("mats_sb", [P, 3 * P])
        ident, upto, beyond = (mats_sb[:, k * P:(k + 1) * P] for k in range(3))
        cw, cb = sb("cw", [P, TILES, TAPS]), sb("cb", [P, TILES])
        zb = sb("zb", [P, DM])
        dsk = sb("dsk", [P, HEADS])
        rw = sb("rw", [P, KT])
        stats, mv = sb("stats", [P, NBC, 6]), sb("mv", [P, NBC, 2])
        ve, rstd = sb("ve", [P, NBC]), sb("rstd", [P, NBC])
        stats2, mv2 = sb("stats2", [P, NBC, 6]), sb("mv2", [P, NBC, 2])
        ve2, rstd2 = sb("ve2", [P, NBC]), sb("rstd2", [P, NBC])
        ss, ms, rms = sb("ss", [P, NBC]), sb("ms", [P, NBC]), sb("rms", [P, NBC])
        mhalf = sb("mhalf", [P, NBC])

        p_proj = [ps("p_proj0"), ps("p_proj1")]
        p_g = [ps("p_g0"), ps("p_g1")]
        p_d, p_y = ps("p_d"), ps("p_y")
        p_t = [ps("p_t0"), ps("p_t1")]

        s_const, s_wld, s_wo = sem("s_const"), [sem("s_wld0"), sem("s_wld1")], sem("s_wo")
        s_wsplit, s_small = sem("s_wsplit"), sem("s_small")
        s_init, s_pick = sem("s_init"), sem("s_pick")
        s_u = sem("s_u")
        s_ln, s_lnpow = sem("s_ln"), sem("s_lnpow")
        s_tfull = sem("s_tfull")
        s_tdone = {"dve": sem("s_tdone_dve"), "act": sem("s_tdone_act")}
        s_tc = sem("s_tc")
        s_proj = sem("s_proj")
        s_tap3 = sem("s_tap3")
        s_tap2, s_tap1, s_tap0 = sem("s_tap2"), sem("s_tap1"), sem("s_tap0")
        s_silu = sem("s_silu")
        s_xsilu, s_zsilu = sem("s_xsilu"), sem("s_zsilu")
        s_abs, s_sp1, s_sp2, s_sp = sem("s_abs"), sem("s_sp1"), sem("s_sp2"), sem("s_sp")
        s_parts = sem("s_parts")
        s_csst, s_dstat, s_dmov = sem("s_csst"), sem("s_dstat"), [sem("s_dmov0"), sem("s_dmov1")]
        s_ecs = sem("s_ecs")
        s_d, s_exp, s_mask = sem("s_d"), sem("s_exp"), sem("s_mask")
        s_g, s_m, s_y = sem("s_g"), sem("s_m"), sem("s_y")
        s_xdec, s_xskip = sem("s_xdec"), sem("s_xskip")
        s_yoff = sem("s_yoff")
        s_yev = sem("s_yev")
        s_yg, s_sq, s_ms, s_rms, s_yn = sem("s_yg"), sem("s_sq"), sem("s_ms"), sem("s_rms"), sem("s_yn")
        s_ln2, s_ln2pow, s_x1, s_x1out, s_ures = sem("s_ln2"), sem("s_ln2pow"), sem("s_x1"), sem("s_x1out"), sem("s_ures")
        s_xn2, s_held = sem("s_xn2"), sem("s_held")

        u_p = u.rearrange("(i b) (c p) d -> i p (b c) d", b=2, p=P)
        x1_p = x1_dram.rearrange("i (k p) d -> i p k d", p=P)

        def of_pass(t, i):
            if isinstance(i, int):
                return t[i]
            return t[bass.ds(i, 1)].rearrange("o p k d -> (o p) k d")

        def jobs_before(i):
            if isinstance(i, int) and i == 0:
                return JOBS_AHEAD
            return i * JOBS_EACH + (JOBS_AHEAD + JOBS_FIRST - JOBS_EACH)

        def place(name, i):
            if isinstance(i, int) and i == PAIRS:
                return TAIL_JOBS.index(name)
            return JOBS[isinstance(i, int) and i == 0].index(name)

        def job(name, i):
            return jobs_before(i) + place(name, i)

        def bank(name, i):
            ahead = jobs_before(i) if isinstance(i, int) else JOBS_AHEAD + JOBS_FIRST
            return (ahead + place(name, i)) % 2

        def jobs_of(i):
            return TAIL_JOBS if isinstance(i, int) and i == PAIRS else JOBS[isinstance(i, int) and i == 0]

        def taken_before(engine, i):
            ahead = JOBS_AHEAD if engine == "dve" else 0
            if isinstance(i, int) and i == 0:
                return ahead
            each = count_of(JOBS[False], engine)
            return i * each + (ahead + count_of(JOBS[True], engine) - each)

        def wait_taken(eng, name, i):
            upto_it = jobs_of(i)[:place(name, i) + 1]
            eng.wait_ge(s_tdone[taker(name)], taken_before(taker(name), i) + count_of(upto_it, taker(name)))

        def wait_bank(eng, name, i):
            k = place(name, i)
            if k >= 2:
                wait_taken(eng, jobs_of(i)[k - 2], i)
            else:
                eng.wait_ge(s_tdone["dve"], taken_before("dve", i) + (k - 1))

        def flat(t):
            return t[:].rearrange("p a b -> p (a b)")

        def heads_at(n, i):
            g = n - LAG
            if g >= 0:
                return (i, g)
            return None if isinstance(i, int) and i == 0 else (i - 1, g + SLOTS)

        def decay_heads(n, i):
            found = []
            for d in decays_of(n):
                g = n - LAG + d
                if g >= 0:
                    found.append((i, g))
                elif not (isinstance(i, int) and i == 0):
                    found.append((i - 1, g + SLOTS))
            return found

        def tile_of(n):
            return n % (2 * QT)

        WQ = TILES * P // 2
        stage = bc[:, :, :].rearrange("p a b -> p (a b)")

        block = ctx.enter_context(nc.Block())

        @block.sync
        def _(sp_):
            w_src = w_tiles.rearrange("(k p) n -> p k n", p=P)
            sp_.dma_start(u_in[:], of_pass(u_p, 0)).then_inc(s_u, 16)
            sp_.dma_start(mats_sb[:], mats).then_inc(s_const, 16)
            sp_.dma_start(cw[:], conv_w).then_inc(s_const, 16)
            sp_.dma_start(cb[:], conv_b).then_inc(s_const, 16)
            sp_.dma_start(zb[:], z_bias.rearrange("(o n) -> o n", o=1).broadcast_to([P, DM])).then_inc(s_const, 16)
            sp_.dma_start(dsk[:], d_skip.rearrange("(o n) -> o n", o=1).broadcast_to([P, HEADS])).then_inc(s_const, 16)
            sp_.dma_start(rw[:], rms_w).then_inc(s_const, 16)
            sp_.dma_start(u_res[:, 0:2, :].rearrange("p a b -> p (a b)"),
                          w_out.rearrange("(k p) n -> p k n", p=P)).then_inc(s_wo, 16)
            sp_.dma_start(z_silu[:, 0:3, :].rearrange("p a b -> p (a b)")[:, 0:KT * ZA],
                          w_za.rearrange("(k p) n -> p k n", p=P)).then_inc(s_wo, 16)
            for c in range(4):
                if c >= 2:
                    sp_.wait_ge(s_wsplit, 2 * (c - 1))
                sp_.dma_start(stage[:, (c % 2) * WQ:(c % 2 + 1) * WQ],
                              w_src[:, c // 2, (c % 2) * WQ:(c % 2 + 1) * WQ]).then_inc(s_wld[c % 2], 16)

            def one_pass(i):
                first = isinstance(i, int)
                sp_.wait_ge(s_ln, i * 13 + 13)
                sp_.dma_start(u_in[:], of_pass(u_p, (i + 1) % PAIRS)).then_inc(s_u, 16)
                sp_.wait_ge(s_parts, i * 3 + 3)
                sp_.sem_inc(s_held, 1)
                if not first:
                    sp_.wait_ge(s_dmov[0], i * 32)
                    sp_.wait_ge(s_dmov[1], i * 32)
                sp_.dma_start(cs_dram.rearrange("a h n -> h a n"), cs_parts[:]).then_inc(s_csst, 16)
                sp_.wait_ge(s_csst, i * 16 + 16)
                sp_.sem_inc(s_held, 1)
                if not first:
                    sp_.wait_ge(s_d, i * SLOTS)
                else:
                    sp_.wait_ge(s_pick, 48)
                for part in range(3):
                    sp_.dma_start(d_stat[part * QH:(part + 1) * QH],
                                  cs_dram[part].rearrange("(q k) n -> k q n", k=QH)).then_inc(s_dstat, 16)
                for q in range(QUADS):
                    if q == 2 and not first:
                        residual(i - 1, i)
                    if q >= 2 or not first:
                        sp_.wait_ge(s_d, i * SLOTS + QH * (q - 1))
                    sp_.dma_start(d_mov[CSL:CSL + 3, q % 2],
                                  cs_dram[:, q * QH:(q + 1) * QH, :]).then_inc(s_dmov[q % 2], 16)
                    if q == 2 and not first:
                        store(i - 1)

            def residual(i, body):
                sp_.wait_ge(s_zsilu, body + 1)
                sp_.dma_start(u_res[:], of_pass(u_p, i)).then_inc(s_ures, 16)

            def store(i):
                sp_.wait_ge(s_x1, i + 1)
                sp_.dma_start(of_pass(x1_p, i), o_sb[:]).then_inc(s_x1out, 16)

            sp_.sem_inc(s_x1out, 16)
            one_pass(0)
            with sp_.Fori(1, PAIRS) as i:
                one_pass(i)
            residual(PAIRS - 1, PAIRS - 1)
            store(PAIRS - 1)
            sp_.wait_ge(s_x1out, 16 * (PAIRS + 1))

        @block.tensor
        def _(pe):
            def split3(out, a, a2, b, b2, k, last, start=None):
                for m, (x, y) in enumerate(((a, b), (a, b2), (a2, b))):
                    r = nc.tensor.matmul(out, x, y, start=(k == 0 and m == 0), stop=(last and m == 2))
                return r

            def open_job(name, i):
                wait_bank(pe, name, i)
                return p_t[bank(name, i)]

            def norm_transposes(i, body):
                pe.wait_ge(s_ln, i * 13 + 13)
                for k in range(KT):
                    t = p_t[k] if body is None else open_job(f"XH{k}+", body)
                    for c in range(NBC):
                        r = nc.tensor.transpose(t[:, c * P:(c + 1) * P], u_norm[:, c, k * P:(k + 1) * P], ident)
                    r.then_inc(s_tfull, 1)

            def project(i, m, between=lambda: None):
                if not (isinstance(i, int) and i == 0 and m < 2):
                    pe.wait_ge(s_tap0, i * TILES + m - 1)
                if m == 0:
                    pe.wait_ge(s_tdone["dve"], taken_before("dve", i))
                for k in range(KT):
                    if k:
                        between()
                    cols = slice(m * P, (m + 1) * P)
                    r = split3(p_proj[m % 2][:], w_hi[:, k, cols], w_lo[:, k, cols], xh_hi[:, k], xh_lo[:, k], k, k == KT - 1)
                r.then_inc(s_proj, 1)

            def project_za(i, c):
                t = open_job(f"ZA{c}", i)
                for k in range(KT):
                    cols = slice(c * P, (c + 1) * P)
                    r = split3(t[:, 0:ZA], xh_hi[:, k, cols], xh_lo[:, k, cols], za_hi[:, k], za_lo[:, k], k, k == KT - 1)
                r.then_inc(s_tfull, 1)

            def cumsums(i):
                t = open_job("CST", i)
                pe.wait_ge(s_sp, i + 1)
                for c in range(NBC):
                    r = nc.tensor.matmul(t[0:HEADS, c * P:(c + 1) * P], sp[:, c], upto, start=True, stop=True)
                r.then_inc(s_tfull, 1)

            def token_cumsums(i):
                t = open_job("CSK", i)
                for c in range(NBC):
                    r = nc.tensor.matmul(t[:, c * HEADS:(c + 1) * HEADS], upto if c % 2 else beyond, sp[:, c],
                                         start=True, stop=True)
                r.then_inc(s_tfull, 1)

            def x_transposes(i):
                pe.wait_ge(s_xsilu, i + 1)
                for x in range(XT):
                    t = open_job(f"XT{x}", i)
                    for c in range(NBC):
                        r = nc.tensor.transpose(t[:, c * P:(c + 1) * P], xT[:, x, c * P:(c + 1) * P], ident)
                    r.then_inc(s_tfull, 1)

            def decay_exponents(i, g):
                q, k = g // QH, g % QH
                if not (isinstance(i, int) and i == 0 and g == 0):
                    pe.wait_ge(s_exp, i * SLOTS + g)
                if k == 0:
                    pe.wait_ge(s_dmov[q % 2], i * 32 + 16 * (q // 2 + 1))
                    if q == 0:
                        pe.wait_ge(s_dstat, i * 48 + 48)
                for c in range(NBC):
                    r = nc.tensor.matmul(p_d[:, c * P:(c + 1) * P], d_stat[:, q, c * P:(c + 1) * P],
                                         d_mov[:, q % 2, k, c * P:(c + 1) * P], start=True, stop=True)
                r.then_inc(s_d, 1)

            def scores(i, g):
                q, k = g // QH, g % QH
                if k % 2 == 0:
                    pe.wait_ge(s_silu, i * NT + 4 * q + k // 2 + 1)
                if not (isinstance(i, int) and i == 0 and g < 2):
                    pe.wait_ge(s_m, i * SLOTS + g - 1)
                rows = slice((g % 2) * NSTATE, (g % 2 + 1) * NSTATE)
                tb = tile_of(q * QT + 2 * (k // 2))
                for c in range(NBC):
                    r = nc.tensor.matmul(p_g[g % 2][:, c * P:(c + 1) * P], bc[rows, tb, c * P:(c + 1) * P],
                                         bc[rows, tb + 1, c * P:(c + 1) * P], start=True, stop=True)
                r.then_inc(s_g, 1)

            def mix_x(i, g):
                q, k = g // QH, g % QH
                pe.wait_ge(s_m, i * SLOTS + g + 1)
                if k == 0 and not (isinstance(i, int) and i == 0 and q == 0):
                    pe.wait_ge(s_yev, i * 12 + 3 * q)
                if g == 0:
                    wait_taken(pe, "XT1", i)
                for c in range(NBC):
                    r = nc.tensor.matmul(p_y[:, c * 64 + k * HDIM:c * 64 + (k + 1) * HDIM],
                                         mixed[:, g % NM, c * P:(c + 1) * P],
                                         x_tok[:, c, g * HDIM:(g + 1) * HDIM], start=True, stop=True)
                r.then_inc(s_y, 1)

            def b_transposes(i, q, h, body, tag):
                t = open_job(f"BT{q}{h}{tag}", body)
                pe.wait_ge(s_silu, i * NT + 4 * q + 2 * h + 2)
                for j in range(2):
                    for b in range(2):
                        tb = tile_of(q * QT + 2 * (2 * h + j))
                        r = nc.tensor.transpose(t[:, (2 * j + b) * P:(2 * j + b + 1) * P],
                                                bc[:, tb, 2 * b * P:(2 * b + 1) * P], ident)
                r.then_inc(s_tfull, 1)

            def chunk_states(i, q, body, tag, pairs):
                if 0 in pairs:
                    open_job(f"ST{q}{tag}", body)
                    wait_taken(pe, f"BT{q}1{tag}", body)
                    pe.wait_ge(s_xdec, i + 1)
                t = p_t[bank(f"ST{q}{tag}", body)]
                for j in pairs:
                    for b in range(2):
                        a = (j % 2) * 2 + b
                        at = (2 * j + b) * 2 * HDIM
                        r = nc.tensor.matmul(t[:, at:at + 2 * HDIM], b_tok[:, j // 2, a * P:(a + 1) * P],
                                             x_dec[:, b, (q * QH + 2 * j) * HDIM:(q * QH + 2 * j + 2) * HDIM],
                                             start=True, stop=True)
                if 3 in pairs:
                    r.then_inc(s_tfull, 1)

            def y_from_state(i, q, body, tag, pairs):
                if 0 in pairs:
                    wait_taken(pe, f"ST{q}{tag}", body)
                for j in pairs:
                    for b in range(2):
                        tc_ = tile_of(q * QT + 2 * j + 1)
                        at = 256 + b * 64 + 2 * j * HDIM
                        r = nc.tensor.matmul(p_y[:, at:at + 2 * HDIM], bc[:, tc_, (2 * b + 1) * P:(2 * b + 2) * P],
                                             states[:, j, b, :], start=True, stop=True)
                if 3 in pairs:
                    r.then_inc(s_yoff, 1)

            def y_transposes(i, body):
                pe.wait_ge(s_yn, i * 4 + 4)
                for k in range(KT):
                    t = open_job(f"YT{k}-", body)
                    for c in range(NBC):
                        r = nc.tensor.transpose(t[:, c * P:(c + 1) * P], yg[:, c, k * P:(k + 1) * P], ident)
                    r.then_inc(s_tfull, 1)

            def project_out(i, h, body):
                t = open_job(f"OP{h}-", body)
                wait_taken(pe, "YT1-", body)
                for j in range(2):
                    for k in range(KT):
                        cols = slice((2 * h + j) * P, (2 * h + j + 1) * P)
                        r = split3(t[:, j * DM:(j + 1) * DM], yT_hi[:, k, cols], yT_lo[:, k, cols],
                                   wo_hi[:, k], wo_lo[:, k], k, k == KT - 1)
                r.then_inc(s_tfull, 1)

            def some_states(n, i, pairs, tail=False):
                now = None if tail and n >= LAG else heads_at(n, i)
                if now:
                    ii, g = now
                    q, u = g // QH, g % QH
                    tag = "-" if n - LAG < 0 else ""
                    if u == 3:
                        chunk_states(ii, q, i, tag, pairs)
                    if u == 4:
                        y_from_state(ii, q, i, tag, pairs)

            def attend(n, i, tail=False):
                ahead = [(ii, g) for ii, g in decay_heads(n, i) if not tail or ii is not i]
                for ii, g in ahead[:1]:
                    decay_exponents(ii, g)
                now = None if tail and n >= LAG else heads_at(n, i)
                if now:
                    ii, g = now
                    q, u = g // QH, g % QH
                    tag = "-" if n - LAG < 0 else ""
                    scores(ii, g)
                some_states(n, i, (2,), tail)
                for ii, g in ahead[1:]:
                    decay_exponents(ii, g)
                behind = heads_at(n - 1, i)
                if behind:
                    mix_x(*behind)
                if n == LAG and not tail:
                    x_transposes(i)
                if now:
                    if u in (0, 1):
                        b_transposes(ii, q, u, i, tag)
                some_states(n, i, (3,), tail)

            def one_pass(i):
                first = isinstance(i, int)
                for n in range(SLOTS):
                    if n == 0:
                        attend(n, i)
                    if n < XT:
                        project(i, 2 * n)
                    project(i, seq(n), lambda: some_states(n, i, (0,)))
                    some_states(n, i, (1,))
                    if n < NBC:
                        project_za(i, n)
                    if n:
                        attend(n, i)
                    if n == 6:
                        cumsums(i)
                    if n == 7:
                        token_cumsums(i)
                    if not first:
                        if n == 15:
                            y_transposes(i - 1, i)
                        if n in (16, 17):
                            project_out(i - 1, n - 16, i)
                norm_transposes(i + 1, i)

            pe.wait_ge(s_const, 16 * 6)
            norm_transposes(0, None)
            pe.wait_ge(s_wsplit, 8)
            pe.wait_ge(s_small, 2)
            one_pass(0)
            with pe.Fori(1, PAIRS) as i:
                one_pass(i)
            for n in range(LAG + 1):
                some_states(n, PAIRS, (0, 1), tail=True)
                attend(n, PAIRS, tail=True)
            y_transposes(PAIRS - 1, PAIRS)
            project_out(PAIRS - 1, 0, PAIRS)
            project_out(PAIRS - 1, 1, PAIRS)

        @block.scalar
        def _(act):
            def newest_tap(i, m, n=None):
                if n is not None:
                    q, j = n // QT, (n % QT) // 2
                    if q >= 2 or not isinstance(i, int):
                        act.wait_ge(s_g, i * SLOTS + (q - 2) * QH + 2 * j + 2)
                        act.wait_ge(s_yoff, i * QUADS + q - 1)
                    elif n == 0:
                        act.wait_ge(s_wsplit, 8)
                    dst = bc[:, tile_of(n)]
                else:
                    if m == 0 and isinstance(i, int):
                        act.wait_ge(s_const, 16 * 6)
                    elif m == 0:
                        act.wait_ge(s_tfull, jobs_before(i))
                    dst = xT[:, m // 2]
                act.wait_ge(s_proj, i * TILES + m + 1)
                nc.scalar.activation(dst, p_proj[m % 2][:], ACT.Identity, bias=cb[:, m:m + 1],
                                     scale=cw[:, m, TAPS - 1:TAPS]).then_inc(s_tap3, 1)

            def silu_pairs(i, q, h):
                act.wait_ge(s_tap0, i * TILES + XT + (q + 1) * QT)
                for j in (2 * h, 2 * h + 1):
                    t0 = tile_of(q * QT + 2 * j)
                    v = bc[:, t0:t0 + 2].rearrange("p a b -> p (a b)")
                    nc.scalar.activation(v, v, ACT.Silu).then_inc(s_silu, 1)

            def silu_x(i):
                v = xT[:].rearrange("p a b -> p (a b)")
                act.wait_ge(s_tap0, i * TILES + 3)
                nc.scalar.activation(v, v, ACT.Silu).then_inc(s_xsilu, 1)

            def silu_z(i):
                wait_taken(act, "ZA3", i)
                if isinstance(i, int):
                    act.wait_ge(s_small, 2)
                else:
                    act.wait_ge(s_yg, i)
                nc.scalar.activation(z_silu[:].rearrange("p a b -> p (a b)"), z_raw[:].rearrange("p a b -> p (a b)"),
                                     ACT.Silu).then_inc(s_zsilu, 1)

            def softplus(i):
                act.wait_ge(s_abs, i + 1)
                nc.scalar.activation(a_abs[:].rearrange("p a b -> p (a b)"), a_abs[:].rearrange("p a b -> p (a b)"),
                                     ACT.Exp, scale=-1.0).then_inc(s_sp1, 1)
                act.wait_ge(s_sp1, i + 1)
                nc.scalar.activation(a_abs[:].rearrange("p a b -> p (a b)"), a_abs[:].rearrange("p a b -> p (a b)"),
                                     ACT.Ln, bias=1.0).then_inc(s_sp2, 1)

            def exp_cs(i):
                wait_taken(act, "CSK", i)
                if not isinstance(i, int):
                    act.wait_ge(s_yev, i * 12)
                    act.wait_ge(s_xdec, i)
                nc.scalar.activation(e_cs[:].rearrange("p a b -> p (a b)"), cs_k[:].rearrange("p a b -> p (a b)"),
                                     ACT.Exp).then_inc(s_ecs, 1)

            def decays(i, g):
                act.wait_ge(s_d, i * SLOTS + g + 1)
                if not (isinstance(i, int) and i == 0 and g < NL):
                    act.wait_ge(s_m, i * SLOTS + g - NL + 1)
                nc.scalar.activation(decay[:, g % NL], p_d[:], ACT.Exp).then_inc(s_exp, 1)

            def copy_out(dst, t):
                nc.scalar.activation(dst, t, ACT.Copy).then_inc(s_tdone["act"], 1)

            def take(name, i):
                act.wait_ge(s_tfull, job(name, i) + 1)
                return p_t[bank(name, i)]

            def take_x(i):
                for x in range(XT):
                    t = take(f"XT{x}", i)
                    if not isinstance(i, int) and x == 0:
                        act.wait_ge(s_y, i * SLOTS)
                        act.wait_ge(s_xskip, i * 5)
                    copy_out(x_tok[:, :, x * P:(x + 1) * P], t[:].rearrange("p (c n) -> p c n", c=NBC))

            def take_b(n, i):
                before = heads_at(n - 1, i)
                if before and before[1] % QH in (0, 1):
                    q, h = before[1] // QH, before[1] % QH
                    copy_out(b_tok[:, h], take(f"BT{q}{h}{'-' if n - 1 < LAG else ''}", i)[:])

            def take_out(i, h, body):
                if h == 0:
                    act.wait_ge(s_tfull, job("YT1-", body) + 1)
                copy_out(o_sb[:, 2 * h:2 * h + 2].rearrange("p a b -> p (a b)"), take(f"OP{h}-", body)[:])

            def rms_norm(i):
                act.wait_ge(s_rms, i + 1)
                for c in range(NBC):
                    nc.scalar.activation(yg[:, c], yg[:, c], ACT.Copy, scale=rms[:, c:c + 1]).then_inc(s_yn, 1)

            def squares(i):
                act.wait_ge(s_yg, i + 1)
                for c in range(NBC):
                    nc.scalar.activation(y_sum[:, c], yg[:, c], ACT.Square, accum_out=ss[:, c:c + 1]).then_inc(s_sq, 1)

            def one_pass(i):
                first = isinstance(i, int)
                for n in range(SLOTS):
                    if n == 0:
                        for head in decay_heads(n, i):
                            decays(*head)
                    if n < XT:
                        newest_tap(i, 2 * n)
                    newest_tap(i, seq(n), n)
                    if n % QT in (1, 2):
                        q, h = (n // QT - 1) % QUADS, n % QT - 1
                        if n > QT or not first:
                            silu_pairs(i if n > QT else i - 1, q, h)
                        if n == QT + 1:
                            silu_x(i)
                        if n == 2 * QT + 2:
                            silu_z(i)
                    for head in decay_heads(n, i) if n else []:
                        decays(*head)
                    if n == 5:
                        softplus(i)
                    if n == 12:
                        exp_cs(i)
                    take_b(n, i)
                    if n == LAG:
                        take_x(i)
                    if not first:
                        if n == 13:
                            squares(i - 1)
                        if n == 14:
                            rms_norm(i - 1)
                        if n in (17, 18):
                            take_out(i - 1, n - 17, i)

            one_pass(0)
            with act.Fori(1, PAIRS) as i:
                one_pass(i)
            for n in range(LAG):
                if n in (1, 2):
                    silu_pairs(PAIRS - 1, QUADS - 1, n - 1)
                for ii, g in decay_heads(n, PAIRS):
                    if ii < PAIRS:
                        decays(ii, g)
                take_b(n, PAIRS)
            squares(PAIRS - 1)
            rms_norm(PAIRS - 1)
            take_out(PAIRS - 1, 0, PAIRS)
            take_out(PAIRS - 1, 1, PAIRS)

        @block.gpsimd
        def _(pool):
            pool.memset(mhalf[:], -0.5).then_inc(s_init, 1)
            pool.memset(states[:].rearrange("p a b c -> p (a b c)"), 0.0).then_inc(s_init, 1)
            pool.dma_start(d_stat[CSL:HPT], marks).then_inc(s_pick, 16)
            for half in range(2):
                pool.dma_start(d_mov[:, half], pick).then_inc(s_pick, 16)
            pool.wait_ge(s_init, 2)

            def causal(i, g):
                pool.wait_ge(s_exp, i * SLOTS + g + 1)
                pool.sem_inc(s_held, 1)
                v = decay[:, g % NL].rearrange("p (c l) -> p c l", c=NBC)
                pool.affine_select(out=v, in_=v, compare_op=ALU.is_ge, fill=0.0, base=0,
                                   pattern=[[0, NBC], [1, P]], channel_multiplier=-1).then_inc(s_mask, 1)

            def pow_of(out, src, done, ready, value, i):
                pool.wait_ge(ready, value)
                pool.tensor_tensor(out, src, mhalf[:], ALU.pow).then_inc(done, 1)

            def gate(i):
                pool.wait_ge(s_yev, i * 12 + 12)
                pool.wait_ge(s_zsilu, i + 1)
                pool.wait_ge(s_x1out, i * 16 + 16)
                pool.tensor_tensor(flat(yg), flat(y_sum), flat(z_silu), ALU.mult).then_inc(s_yg, 1)

            def add_residual(i):
                pool.wait_ge(s_xn2, i * 4 + 4)
                pool.wait_ge(s_ures, i * 16 + 16)
                pool.tensor_tensor(flat(o_sb), flat(o_sb), flat(u_res), ALU.add).then_inc(s_x1, 1)

            def x_scaled(i):
                wait_taken(pool, "XT1", i)
                if not isinstance(i, int):
                    pool.wait_ge(s_yev, i * 12)
                for b in range(2):
                    if b == 0:
                        pool.wait_ge(s_ecs, i + 1)
                    pool.tensor_tensor(x_dec[:, b].rearrange("p (h d) -> p h d", d=HDIM),
                                       x_tok[:, 2 * b].rearrange("p (h d) -> p h d", d=HDIM),
                                       e_cs[:, 2 * b].unsqueeze(2).broadcast_to([P, HEADS, HDIM]), ALU.mult)\
                        .then_inc(s_xdec if b else s_xskip, 1)
                for c in range(NBC):
                    pool.tensor_tensor(x_skip[:, c].rearrange("p (h d) -> p h d", d=HDIM),
                                       x_tok[:, c].rearrange("p (h d) -> p h d", d=HDIM),
                                       dsk[:].unsqueeze(2).broadcast_to([P, HEADS, HDIM]), ALU.mult)\
                        .then_inc(s_xskip, 1)

            def one_pass(i):
                first = isinstance(i, int)
                for n in range(SLOTS):
                    for head in decay_heads(n, i):
                        causal(*head)
                    if n == 12:
                        if not first:
                            gate(i - 1)
                        x_scaled(i)
                    if not first:
                        if n == 13:
                            pow_of(rms[:], ms[:], s_rms, s_ms, i, i)
                        if n == 20:
                            pow_of(rstd2[:], ve2[:], s_ln2pow, s_ln2, i * 9, i)
                        if n == 22:
                            add_residual(i - 1)
                    if n == 26:
                        pow_of(rstd[:], ve[:], s_lnpow, s_ln, i * 13 + 22, i)

            pow_of(rstd[:], ve[:], s_lnpow, s_ln, 9, 0)
            one_pass(0)
            with pool.Fori(1, PAIRS) as i:
                one_pass(i)
            for n in range(LAG):
                for ii, g in decay_heads(n, PAIRS):
                    if ii < PAIRS:
                        causal(ii, g)
            gate(PAIRS - 1)
            pow_of(rms[:], ms[:], s_rms, s_ms, PAIRS, PAIRS)
            pow_of(rstd2[:], ve2[:], s_ln2pow, s_ln2, PAIRS * 9, PAIRS)
            add_residual(PAIRS - 1)

        @block.vector
        def _(dve):
            def split_weights(c):
                dve.wait_ge(s_wld[c % 2], 16 * (c // 2 + 1))
                cols = slice((c % 2) * WQ, (c % 2 + 1) * WQ)
                raw = stage[:, cols]
                nc.vector.tensor_copy(w_hi[:, c // 2, cols], raw).then_inc(s_wsplit, 1)
                dve.wait_ge(s_wsplit, 2 * c + 1)
                nc.vector.tensor_tensor(w_lo[:, c // 2, cols], raw, w_hi[:, c // 2, cols].bitcast(F32),
                                        ALU.subtract).then_inc(s_wsplit, 1)

            def split_small():
                dve.wait_ge(s_const, 16 * 6)
                dve.wait_ge(s_wo, 32)
                wo = u_res[:, 0:2, :]
                for k in range(KT):
                    nc.vector.tensor_scalar(o_sb[:, k], wo[:, k], rw[:, k:k + 1], None, ALU.mult).then_inc(s_tc, 1)
                dve.wait_ge(s_tc, 2)
                nc.vector.tensor_copy(wo_hi[:].rearrange("p a b -> p (a b)"), o_sb[:, 0:2].rearrange("p a b -> p (a b)")).then_inc(s_tc, 1)
                za = z_silu[:, 0:3, :].rearrange("p a b -> p (a b)")[:, 0:KT * ZA]
                nc.vector.tensor_copy(za_hi[:].rearrange("p a b -> p (a b)"), za).then_inc(s_tc, 1)
                dve.wait_ge(s_tc, 4)
                nc.vector.tensor_tensor(wo_lo[:].rearrange("p a b -> p (a b)"), o_sb[:, 0:2].rearrange("p a b -> p (a b)"),
                                        wo_hi[:].rearrange("p a b -> p (a b)").bitcast(F32), ALU.subtract).then_inc(s_small, 1)
                nc.vector.tensor_tensor(za_lo[:].rearrange("p a b -> p (a b)"), za,
                                        za_hi[:].rearrange("p a b -> p (a b)").bitcast(F32), ALU.subtract).then_inc(s_small, 1)

            TC0 = 4

            def norm_stats(i, blocks):
                if 0 in blocks:
                    dve.wait_ge(s_u, i * 16 + 16)
                for c in blocks:
                    nc.vector.bn_stats(stats[:, c], u_in[:, c]).then_inc(s_ln, 1)

            def norm_variance(i):
                dve.wait_ge(s_ln, i * 13 + 4)
                dve.sem_inc(s_held, 1)
                for c in range(NBC):
                    nc.vector.bn_aggr(mv[:, c], stats[:, c]).then_inc(s_ln, 1)
                dve.wait_ge(s_ln, i * 13 + 8)
                nc.vector.tensor_scalar(ve[:], mv[:, :, 1], EPS, None, ALU.add).then_inc(s_ln, 1)

            def norm_apply(i, body, blocks):
                if 0 in blocks:
                    dve.wait_ge(s_lnpow, i + 1)
                    if body is not None:
                        dve.wait_ge(s_x1out, body * 16 + 16)
                for c in blocks:
                    nc.vector.tensor_scalar(u_norm[:, c], u_in[:, c], mv[:, c, 0:1], rstd[:, c:c + 1],
                                            ALU.subtract, ALU.mult).then_inc(s_ln, 1)

            def take(name, i):
                dve.wait_ge(s_tfull, job(name, i) + 1)
                return p_t[bank(name, i)]

            def split_job(t, hi, lo, count):
                nc.vector.tensor_copy(hi, t[:]).then_inc(s_tc, 1)
                dve.wait_ge(s_tc, count)
                nc.vector.tensor_tensor(lo, t[:], hi.bitcast(F32), ALU.subtract).then_inc(s_tdone["dve"], 1)

            def take_norm(body):
                if body is not None:
                    dve.wait_ge(s_proj, body * TILES + TILES)
                for k in range(KT):
                    if body is None:
                        dve.wait_ge(s_tfull, k + 1)
                        split_job(p_t[k], xh_hi[:, k], xh_lo[:, k], TC0 + k + 1)
                    else:
                        done = TC0 + 2 if isinstance(body, int) else body * 4 + (TC0 + 2)
                        split_job(take(f"XH{k}+", body), xh_hi[:, k], xh_lo[:, k], done + k + 1)

            def take_za(i, c):
                t = take(f"ZA{c}", i)
                if not isinstance(i, int) and c == 0:
                    dve.wait_ge(s_zsilu, i)
                nc.vector.tensor_tensor(z_raw[:, c], t[:, 0:DM], zb[:], ALU.add)
                nc.vector.tensor_copy(a_log[:, c], t[:, DM:ZA]).then_inc(s_tdone["dve"], 1)

            def abs_a(i):
                wait_taken(dve, "ZA3", i)
                nc.vector.scalar_tensor_tensor(out=flat(a_abs), in0=flat(a_log), scalar=-1.0, in1=flat(a_log),
                                               op0=ALU.mult, op1=ALU.max).then_inc(s_abs, 1)

            def softplus_sum(i):
                dve.wait_ge(s_sp2, i + 1)
                if not isinstance(i, int):
                    dve.wait_ge(s_tfull, jobs_before(i))
                nc.vector.scalar_tensor_tensor(out=flat(sp), in0=flat(a_log), scalar=0.0, in1=flat(a_abs),
                                               op0=ALU.max, op1=ALU.add).then_inc(s_sp, 1)

            def take_cs(i):
                t = take("CST", i)
                if not isinstance(i, int):
                    dve.wait_ge(s_csst, i * 16)
                cs = t[0:HEADS, :]
                nc.vector.tensor_copy(cs_parts[:, 0], cs).then_inc(s_parts, 1)
                dve.wait_ge(s_parts, i * 3 + 1)
                nc.vector.tensor_tensor(cs_rest[:], cs, cs_parts[:, 0], ALU.subtract).then_inc(s_tdone["dve"], 1)

            def take_token_cs(i):
                wait_taken(dve, "CST", i)
                nc.vector.tensor_copy(cs_parts[:, 1], cs_rest[:]).then_inc(s_parts, 1)
                t = take("CSK", i)
                if not isinstance(i, int):
                    dve.wait_ge(s_ecs, i)
                nc.vector.tensor_copy(flat(cs_k), t[:, 0:NBC * HEADS]).then_inc(s_tdone["dve"], 1)
                dve.wait_ge(s_parts, i * 3 + 2)
                nc.vector.tensor_tensor(cs_parts[:, 2], cs_rest[:], cs_parts[:, 1], ALU.subtract).then_inc(s_parts, 1)

            def take_states(i, q, body, tag):
                t = take(f"ST{q}{tag}", body)
                if not (isinstance(i, int) and i == 0 and q == 0):
                    dve.wait_ge(s_yoff, i * QUADS + q)
                for e in range(2):
                    rows = slice(e * NSTATE, (e + 1) * NSTATE)
                    cols = slice(e * HDIM, (e + 1) * HDIM)
                    r = nc.vector.tensor_copy(states[rows, :, :, cols].rearrange("p a b c -> p (a b) c"),
                                              t[rows, 0:16 * HDIM].rearrange("p (a c) -> p a c", c=2 * HDIM)[:, :, cols])
                r.then_inc(s_tdone["dve"], 1)

            def taps(i, m, w):
                shift = TAPS - 1 - w
                n = {1: 0, 3: 1}.get(m, m - XT)
                dst = xT[:, m // 2] if m in (0, 2) else bc[:, tile_of(n)]
                d3 = dst.rearrange("p (b t) -> p b t", b=2)
                src = p_proj[m % 2][:].rearrange("p (b t) -> p b t", b=2)
                before, done = {2: (s_tap3, s_tap2), 1: (s_tap2, s_tap1), 0: (s_tap1, s_tap0)}[w]
                dve.wait_ge(before, i * TILES + m + 1)
                nc.vector.scalar_tensor_tensor(out=d3[:, :, shift:], in0=src[:, :, :SEQ - shift], scalar=cw[:, m, w:w + 1],
                                               in1=d3[:, :, shift:], op0=ALU.mult, op1=ALU.add).then_inc(done, 1)

            def mix(i, g):
                dve.wait_ge(s_mask, i * SLOTS + g + 1)
                dve.wait_ge(s_g, i * SLOTS + g + 1)
                if not (isinstance(i, int) and i == 0 and g < NM):
                    dve.wait_ge(s_y, i * SLOTS + g - NM + 1)
                nc.vector.tensor_tensor(mixed[:, g % NM], p_g[g % 2][:], decay[:, g % NL], ALU.mult).then_inc(s_m, 1)

            def take_y(i, q):
                dve.wait_ge(s_y, i * SLOTS + (q + 1) * QH)
                dve.wait_ge(s_yoff, i * QUADS + q + 1)
                dve.wait_ge(s_xskip, i * 5 + 5)
                cols = slice(q * QH * HDIM, (q + 1) * QH * HDIM)
                nc.vector.tensor_tensor(y_sum[:, :, cols], p_y[:, 0:256].rearrange("p (c n) -> p c n", c=NBC),
                                        x_skip[:, :, cols], ALU.add).then_inc(s_yev, 1)
                nc.vector.tensor_tensor(y_tmp[:].rearrange("p b (h d) -> p b h d", d=HDIM),
                                        p_y[:, 256:384].rearrange("p (b h d) -> p b h d", b=2, d=HDIM),
                                        e_cs[:, 1::2, q * QH:(q + 1) * QH].unsqueeze(3).broadcast_to([P, 2, QH, HDIM]),
                                        ALU.mult).then_inc(s_yev, 1)
                dve.wait_ge(s_yev, i * 12 + 3 * q + 2)
                nc.vector.tensor_tensor(y_sum[:, 1::2, cols], y_sum[:, 1::2, cols], y_tmp[:], ALU.add).then_inc(s_yev, 1)

            def mean_squares(i):
                dve.wait_ge(s_sq, i * 4 + 4)
                nc.vector.tensor_scalar(ms[:], ss[:], 1.0 / DM, EPS, ALU.mult, ALU.add).then_inc(s_ms, 1)

            def take_yT(i, body):
                for k in range(KT):
                    split_job(take(f"YT{k}-", body), yT_hi[:, k], yT_lo[:, k], body * 4 + (TC0 + k + 1))

            def out_stats(i, body, h):
                wait_taken(dve, f"OP{h}-", body)
                for c in (2 * h, 2 * h + 1):
                    nc.vector.bn_stats(stats2[:, c], o_sb[:, c]).then_inc(s_ln2, 1)

            def out_variance(i):
                for c in range(NBC):
                    dve.wait_ge(s_ln2, i * 9 + c + 1)
                    dve.sem_inc(s_held, 1)
                    nc.vector.bn_aggr(mv2[:, c], stats2[:, c]).then_inc(s_ln2, 1)
                dve.wait_ge(s_ln2, i * 9 + 8)
                nc.vector.tensor_scalar(ve2[:], mv2[:, :, 1], EPS, None, ALU.add).then_inc(s_ln2, 1)

            def norm_out(i, h):
                dve.wait_ge(s_ln2pow, i + 1)
                for c in (2 * h, 2 * h + 1):
                    nc.vector.tensor_scalar(o_sb[:, c], o_sb[:, c], mv2[:, c, 0:1], rstd2[:, c:c + 1],
                                            ALU.subtract, ALU.mult).then_inc(s_xn2, 1)

            def slot_jobs_done(n, i, tail=False):
                now = None if tail and n >= LAG else heads_at(n, i)
                if now:
                    ii, g = now
                    q, h = g // QH, g % QH
                    tag = "-" if n < LAG else ""
                    if h == 3:
                        take_states(ii, q, i, tag)
                behind = heads_at(n - 1, i)
                if behind and behind[1] % QH == QH - 1:
                    take_y(behind[0], behind[1] // QH)

            def one_pass(i):
                first = isinstance(i, int)
                for n in range(SLOTS):
                    now = heads_at(n, i)
                    if n == 0 and now:
                        mix(*now)
                    if n < XT:
                        if n:
                            taps(i, 2 * n - 1, 0)
                        taps(i, 2 * n, 2)
                        taps(i, 2 * n, 1)
                    m = seq(n)
                    taps(i, m - 1, 0)
                    taps(i, m, 2)
                    if n and now:
                        mix(*now)
                    taps(i, m, 1)
                    if n < NBC:
                        take_za(i, n)
                    if n == NBC:
                        abs_a(i)
                    if n == 5:
                        softplus_sum(i)
                    slot_jobs_done(n, i)
                    if n == 6:
                        take_cs(i)
                    if n == 7:
                        take_token_cs(i)
                    if not first:
                        if n == 13:
                            mean_squares(i - 1)
                        if n == 15:
                            take_yT(i - 1, i)
                        if n in (18, 19):
                            out_stats(i - 1, i, n - 18)
                        if n == 19:
                            out_variance(i - 1)
                        if n in (20, 21):
                            norm_out(i - 1, n - 20)
                    if n in (24, 25):
                        norm_stats(i + 1, (0, 1) if n == 24 else (2, 3))
                    if n == 26:
                        norm_variance(i + 1)
                    if n in (27, 28):
                        norm_apply(i + 1, i, (0, 1) if n == 27 else (2, 3))
                taps(i, TILES - 1, 0)
                take_norm(i)

            split_small()
            norm_stats(0, range(NBC))
            norm_variance(0)
            norm_apply(0, None, range(NBC))
            take_norm(None)
            for c in range(4):
                split_weights(c)
            one_pass(0)
            with dve.Fori(1, PAIRS) as i:
                one_pass(i)
            for n in range(LAG + 1):
                if n < LAG:
                    mix(*heads_at(n, PAIRS))
                slot_jobs_done(n, PAIRS, tail=True)
            mean_squares(PAIRS - 1)
            take_yT(PAIRS - 1, PAIRS)
            for h in range(2):
                out_stats(PAIRS - 1, PAIRS, h)
            out_variance(PAIRS - 1)
            for h in range(2):
                norm_out(PAIRS - 1, h)


def expert_block(nc, x1_dram, w_up, b_up, w_down, b_down, w_gate, mats, out):
    with ExitStack() as ctx:
        def sb(name, shape, dt=F32):
            return ctx.enter_context(nc.sbuf_tensor(name, shape, dt))

        def ps(name):
            return ctx.enter_context(nc.psum_tensor(name, [P, 512], F32))

        def sem(name):
            return ctx.enter_context(nc.semaphore(name))

        E = 2
        up_hi, up_lo = sb("up_hi", [P, E * KT, FF], F32R), sb("up_lo", [P, E * KT, FF], F32R)
        dn_hi, dn_lo = sb("dn_hi", [P, E * FT, DM], F32R), sb("dn_lo", [P, E * FT, DM], F32R)
        gt_hi, gt_lo = sb("gt_hi", [P, KT * E], F32R), sb("gt_lo", [P, KT * E], F32R)
        raw_up, raw_dn, raw_gt = sb("raw_up", [P, E * KT, FF]), sb("raw_dn", [P, E * FT, DM]), sb("raw_gt", [P, KT * E])
        ident = sb("f_ident", [P, P])
        bu = sb("bu", [P, E * FT])
        bd = sb("bd", [P, E, DM])
        x_in, x_norm, x_res = sb("x_in", [P, NBC, DM]), sb("x_norm", [P, NBC, DM]), sb("x_res", [P, NBC, DM])
        xh_hi, xh_lo = sb("f_xh_hi", [P, KT, TOK], F32R), sb("f_xh_lo", [P, KT, TOK], F32R)
        hid = sb("hid", [P, 2, TOK])
        h_hi, h_lo = sb("h_hi", [P, E * FT, TOK], F32R), sb("h_lo", [P, E * FT, TOK], F32R)
        y0, y1 = sb("y0", [P, NBC, DM]), sb("y1", [P, NBC, DM])
        first_wins, second_wins = sb("first_wins", [P, NBC]), sb("second_wins", [P, NBC])
        logits = sb("logits", [P, NBC, E])
        stats, mv = sb("f_stats", [P, NBC, 6]), sb("f_mv", [P, NBC, 2])
        ve, rstd = sb("f_ve", [P, NBC]), sb("f_rstd", [P, NBC])
        stats2, mv2 = sb("f_stats2", [P, NBC, 6]), sb("f_mv2", [P, NBC, 2])
        ve2, rstd2 = sb("f_ve2", [P, NBC]), sb("f_rstd2", [P, NBC])
        mhalf = sb("f_mhalf", [P, NBC])

        p_up = [ps("p_up0"), ps("p_up1")]
        p_dn = [[ps(f"p_dn{h}{e}") for e in range(E)] for h in range(2)]
        p_x, p_gt = ps("p_x"), ps("p_gt")

        f_wld, f_wsplit, f_x, f_ln, f_pow, f_init = (sem(n) for n in ("f_wld", "f_wsplit", "f_x", "f_ln", "f_pow", "f_init"))
        f_tr, f_xh, f_gl, f_gate = (sem(n) for n in ("f_tr", "f_xh", "f_gl", "f_gate"))
        f_up, f_act, f_h, f_hhi, f_dn, f_y = (sem(n) for n in ("f_up", "f_act", "f_h", "f_hhi", "f_dn", "f_y"))
        f_ln2, f_pow2, f_res, f_sum, f_out, f_comb = (sem(n) for n in ("f_ln2", "f_pow2", "f_res", "f_sum", "f_out", "f_comb"))
        f_nrm, f_held = sem("f_nrm"), sem("f_held")

        x1_p = x1_dram.rearrange("i (k p) d -> i p k d", p=P)
        out_p = out.rearrange("(i b) (c p) d -> i p (b c) d", b=2, p=P)

        def of_pass(t, i):
            if isinstance(i, int):
                return t[i]
            return t[bass.ds(i, 1)].rearrange("o p k d -> (o p) k d")

        def flat(t):
            return t[:].rearrange("p a b -> p (a b)")

        block = ctx.enter_context(nc.Block())

        def start_only(i, n=1):
            return isinstance(i, int) and i < n

        def run(eng, one_pass):
            one_pass(0)
            with eng.Fori(1, PAIRS - 1) as i:
                one_pass(i)
            one_pass(PAIRS - 1)

        def is_last(i):
            return isinstance(i, int) and i == PAIRS - 1

        @block.sync
        def _(sp_):
            sp_.dma_start(x_in[:], of_pass(x1_p, 0)).then_inc(f_x, 16)
            sp_.dma_start(raw_up[:], w_up.rearrange("e (k p) n -> p (e k) n", p=P)).then_inc(f_wld, 16)
            sp_.dma_start(raw_dn[:], w_down.rearrange("e (f p) n -> p (e f) n", p=P)).then_inc(f_wld, 16)
            sp_.dma_start(raw_gt[:], w_gate).then_inc(f_wld, 16)
            sp_.dma_start(ident[:], mats[:, 0:P]).then_inc(f_wld, 16)
            sp_.dma_start(bu[:], b_up).then_inc(f_wld, 16)
            sp_.dma_start(flat(bd), b_down.rearrange("(o n) -> o n", o=1).broadcast_to([P, E * DM])).then_inc(f_wld, 16)

            def one_pass(i):
                if not is_last(i):
                    sp_.wait_ge(f_ln, i * 13 + 13)
                    sp_.dma_start(x_in[:], of_pass(x1_p, i + 1)).then_inc(f_x, 16)
                if not start_only(i):
                    sp_.wait_ge(f_sum, i)
                sp_.dma_start(x_res[:], of_pass(x1_p, i)).then_inc(f_res, 16)
                sp_.wait_ge(f_sum, i + 1)
                sp_.dma_start(of_pass(out_p, i), y0[:]).then_inc(f_out, 16)

            run(sp_, one_pass)
            sp_.wait_ge(f_out, 16 * PAIRS)

        @block.tensor
        def _(pe):
            def split3(out_, a, a2, b, b2, first, last):
                for m, (x, y) in enumerate(((a, b), (a, b2), (a2, b))):
                    r = nc.tensor.matmul(out_, x, y, start=(first and m == 0), stop=(last and m == 2))
                return r

            def transposes(i):
                pe.wait_ge(f_ln, i * 13 + 13)
                for k in range(KT):
                    if not (start_only(i) and k == 0):
                        pe.wait_ge(f_xh, i * 4 + 2 * k)
                    for c in range(NBC):
                        r = nc.tensor.transpose(p_x[:, c * P:(c + 1) * P], x_norm[:, c, k * P:(k + 1) * P], ident[:])
                    r.then_inc(f_tr, 1)

            def gate_logits(i):
                pe.wait_ge(f_xh, i * 4 + 4)
                if not start_only(i):
                    pe.wait_ge(f_gate, i * 3)
                for c in range(NBC):
                    cols = slice(c * P, (c + 1) * P)
                    for k in range(KT):
                        r = split3(p_gt[:, c * E:(c + 1) * E], xh_hi[:, k, cols], xh_lo[:, k, cols],
                                   gt_hi[:, k * E:(k + 1) * E], gt_lo[:, k * E:(k + 1) * E], k == 0, k == KT - 1)
                r.then_inc(f_gl, 1)

            def up(i):
                for m in range(E * FT):
                    e, f = m // FT, m % FT
                    if not (start_only(i) and m < 2):
                        pe.wait_ge(f_act, i * (E * FT) + m - 1)
                    cols = slice(f * P, (f + 1) * P)
                    for k in range(KT):
                        r = split3(p_up[m % 2][:], up_hi[:, e * KT + k, cols], up_lo[:, e * KT + k, cols],
                                   xh_hi[:, k], xh_lo[:, k], k == 0, k == KT - 1)
                    r.then_inc(f_up, 1)

            def down(i):
                for e in range(E):
                    pe.wait_ge(f_h, i * (E * FT) + (e + 1) * FT)
                    for h in range(2):
                        if not start_only(i):
                            pe.wait_ge(f_y, (i - 1) * 4 + 2 * h + e + 1)
                        for c in range(2):
                            cols = slice((2 * h + c) * P, (2 * h + c + 1) * P)
                            for f in range(FT):
                                r = split3(p_dn[h][e][:, c * DM:(c + 1) * DM], h_hi[:, e * FT + f, cols],
                                           h_lo[:, e * FT + f, cols], dn_hi[:, e * FT + f], dn_lo[:, e * FT + f],
                                           f == 0, f == FT - 1)
                        r.then_inc(f_dn, 1)

            def one_pass(i):
                gate_logits(i)
                up(i)
                if not is_last(i):
                    transposes(i + 1)
                down(i)

            pe.wait_ge(f_wld, 16 * 6)
            transposes(0)
            pe.wait_ge(f_wsplit, 6)
            run(pe, one_pass)

        @block.scalar
        def _(act):
            def one_pass(i):
                for m in range(E * FT):
                    act.wait_ge(f_up, i * (E * FT) + m + 1)
                    if not (start_only(i) and m < 2):
                        act.wait_ge(f_h, i * (E * FT) + m - 1)
                    nc.scalar.activation(hid[:, m % 2], p_up[m % 2][:], ACT.Gelu if m < FT else ACT.Relu,
                                         bias=bu[:, m:m + 1]).then_inc(f_act, 1)

            act.wait_ge(f_wld, 16 * 6)
            run(act, one_pass)

        @block.gpsimd
        def _(pool):
            def norm_pow(i):
                pool.wait_ge(f_ln, i * 13 + 9)
                pool.tensor_tensor(rstd[:], ve[:], mhalf[:], ALU.pow).then_inc(f_pow, 1)

            def one_pass(i):
                if not is_last(i):
                    norm_pow(i + 1)
                pool.wait_ge(f_ln2, i * 9 + 9)
                pool.tensor_tensor(rstd2[:], ve2[:], mhalf[:], ALU.pow).then_inc(f_pow2, 1)

            pool.memset(mhalf[:], -0.5).then_inc(f_init, 1)
            pool.wait_ge(f_init, 1)
            norm_pow(0)
            run(pool, one_pass)

        @block.vector
        def _(dve):
            def split(hi, lo, raw, n):
                nc.vector.tensor_copy(flat(hi) if len(hi.shape) == 3 else hi[:], raw).then_inc(f_wsplit, 1)
                dve.wait_ge(f_wsplit, n + 1)
                nc.vector.tensor_tensor(flat(lo) if len(lo.shape) == 3 else lo[:], raw,
                                        (flat(hi) if len(hi.shape) == 3 else hi[:]).bitcast(F32),
                                        ALU.subtract).then_inc(f_wsplit, 1)

            def norm_stats(i):
                dve.wait_ge(f_x, i * 16 + 16)
                for c in range(NBC):
                    nc.vector.bn_stats(stats[:, c], x_in[:, c]).then_inc(f_ln, 1)
                for c in range(NBC):
                    dve.wait_ge(f_ln, i * 13 + c + 1)
                    dve.sem_inc(f_held, 1)
                    nc.vector.bn_aggr(mv[:, c], stats[:, c]).then_inc(f_ln, 1)
                dve.wait_ge(f_ln, i * 13 + 8)
                nc.vector.tensor_scalar(ve[:], mv[:, :, 1], EPS, None, ALU.add).then_inc(f_ln, 1)

            def norm_apply(i):
                dve.wait_ge(f_pow, i + 1)
                if not start_only(i):
                    dve.wait_ge(f_tr, i * KT)
                for c in range(NBC):
                    nc.vector.tensor_scalar(x_norm[:, c], x_in[:, c], mv[:, c, 0:1], rstd[:, c:c + 1],
                                            ALU.subtract, ALU.mult).then_inc(f_ln, 1)

            def split_norm(i):
                if not start_only(i):
                    dve.wait_ge(f_up, i * (E * FT))
                for k in range(KT):
                    dve.wait_ge(f_tr, i * KT + k + 1)
                    nc.vector.tensor_copy(xh_hi[:, k], p_x[:]).then_inc(f_xh, 1)
                    dve.wait_ge(f_xh, i * 4 + 2 * k + 1)
                    nc.vector.tensor_tensor(xh_lo[:, k], p_x[:], xh_hi[:, k].bitcast(F32), ALU.subtract).then_inc(f_xh, 1)

            def gate(i):
                dve.wait_ge(f_gl, i + 1)
                nc.vector.tensor_copy(flat(logits), p_gt[:, 0:NBC * E]).then_inc(f_gate, 1)
                dve.wait_ge(f_gate, i * 3 + 1)
                nc.vector.tensor_tensor(first_wins[:], logits[:, :, 0], logits[:, :, 1], ALU.is_ge).then_inc(f_gate, 1)
                dve.wait_ge(f_gate, i * 3 + 2)
                nc.vector.tensor_scalar(second_wins[:], first_wins[:], -1.0, 1.0, ALU.mult, ALU.add).then_inc(f_gate, 1)

            def split_hidden(i, m):
                dve.wait_ge(f_act, i * (E * FT) + m + 1)
                if not start_only(i) and m % FT == 0:
                    dve.wait_ge(f_dn, (i - 1) * 4 + 2 * (m // FT) + 2)
                nc.vector.tensor_copy(h_hi[:, m], hid[:, m % 2]).then_inc(f_hhi, 1)
                dve.wait_ge(f_hhi, i * (E * FT) + m + 1)
                nc.vector.tensor_tensor(h_lo[:, m], hid[:, m % 2], h_hi[:, m].bitcast(F32), ALU.subtract).then_inc(f_h, 1)

            def combine(i):
                dve.wait_ge(f_gate, i * 3 + 3)
                if not start_only(i):
                    dve.wait_ge(f_out, i * 16)
                for h in range(2):
                    for e, y in enumerate((y0, y1)):
                        dve.wait_ge(f_dn, i * 4 + 2 * e + h + 1)
                        nc.vector.tensor_tensor(y[:, 2 * h:2 * h + 2], p_dn[h][e][:].rearrange("p (c n) -> p c n", c=2),
                                                bd[:, e].unsqueeze(1).broadcast_to([P, 2, DM]), ALU.add).then_inc(f_y, 1)
                n = i * 12
                for c in range(NBC):
                    dve.wait_ge(f_y, i * 4 + 2 * (c // 2) + 2)
                    nc.vector.tensor_scalar(y1[:, c], y1[:, c], second_wins[:, c:c + 1], None, ALU.mult).then_inc(f_comb, 1)
                for c in range(NBC):
                    dve.wait_ge(f_comb, i * 8 + c + 1)
                    nc.vector.scalar_tensor_tensor(out=y0[:, c], in0=y0[:, c], scalar=first_wins[:, c:c + 1],
                                                   in1=y1[:, c], op0=ALU.mult, op1=ALU.add).then_inc(f_comb, 1)
                for c in range(NBC):
                    dve.wait_ge(f_comb, i * 8 + 4 + c + 1)
                    nc.vector.bn_stats(stats2[:, c], y0[:, c]).then_inc(f_ln2, 1)
                for c in range(NBC):
                    dve.wait_ge(f_ln2, i * 9 + c + 1)
                    dve.sem_inc(f_held, 1)
                    nc.vector.bn_aggr(mv2[:, c], stats2[:, c]).then_inc(f_ln2, 1)
                dve.wait_ge(f_ln2, i * 9 + 8)
                nc.vector.tensor_scalar(ve2[:], mv2[:, :, 1], EPS, None, ALU.add).then_inc(f_ln2, 1)
                dve.wait_ge(f_pow2, i + 1)
                dve.wait_ge(f_res, i * 16 + 16)
                for c in range(NBC):
                    nc.vector.tensor_scalar(y1[:, c], y0[:, c], mv2[:, c, 0:1], rstd2[:, c:c + 1],
                                            ALU.subtract, ALU.mult).then_inc(f_nrm, 1)
                dve.wait_ge(f_nrm, i * 4 + 4)
                nc.vector.tensor_tensor(flat(y0), flat(y1), flat(x_res), ALU.add).then_inc(f_sum, 1)

            def one_pass(i):
                gate(i)
                for m in range(E * FT):
                    split_hidden(i, m)
                    if not is_last(i):
                        if m == 2:
                            norm_stats(i + 1)
                        if m == 4:
                            norm_apply(i + 1)
                if not is_last(i):
                    split_norm(i + 1)
                combine(i)

            norm_stats(0)
            norm_apply(0)
            split_norm(0)
            dve.wait_ge(f_wld, 16 * 6)
            split(up_hi, up_lo, flat(raw_up), 0)
            split(dn_hi, dn_lo, flat(raw_dn), 2)
            split(gt_hi, gt_lo, raw_gt[:], 4)
            run(dve, one_pass)


def kernel(L0_attn_u, L0_attn_W_in, L0_attn_z_bias, L0_attn_conv_w, L0_attn_conv_b, L0_attn_D, L0_attn_rms_w,
           L0_attn_W_out, L0_ffn_Wg, L0_ffn_W0a, L0_ffn_b0a, L0_ffn_W0b, L0_ffn_b0b, L0_ffn_W1a, L0_ffn_b1a,
           L0_ffn_W1b, L0_ffn_b1b):
    import concourse.bacc as bacc
    from concourse.bass_utils import run_bass_kernel_spmd

    a = np.asarray
    rows = lay_out()
    w_in = a(L0_attn_W_in)
    conv_rows = HEADS * HDIM + 2 * HEADS * NSTATE
    mats, pick, marks = constants()
    arrays = {
        "u": a(L0_attn_u),
        "w_tiles": w_in[rows].T,
        "w_za": w_in[conv_rows:].T,
        "z_bias": a(L0_attn_z_bias),
        "conv_w": a(L0_attn_conv_w)[rows].reshape(TILES, P, TAPS).transpose(1, 0, 2),
        "conv_b": a(L0_attn_conv_b)[rows].reshape(TILES, P).T,
        "d_skip": a(L0_attn_D),
        "rms_w": a(L0_attn_rms_w).reshape(KT, P).T,
        "w_out": a(L0_attn_W_out).T,
        "mats": mats,
        "pick": pick,
        "marks": marks,
        "w_up": np.stack([a(L0_ffn_W0a).T, a(L0_ffn_W1a).T]),
        "b_up": np.concatenate([a(L0_ffn_b0a), a(L0_ffn_b1a)]).reshape(-1, P).T,
        "w_down": np.stack([a(L0_ffn_W0b).T, a(L0_ffn_W1b).T]),
        "b_down": np.concatenate([a(L0_ffn_b0b), a(L0_ffn_b1b)]),
        "w_gate": a(L0_ffn_Wg).reshape(2, KT, P).transpose(2, 1, 0).reshape(P, KT * 2),
    }
    arrays = {k: np.ascontiguousarray(v) for k, v in arrays.items()}
    nc = bacc.Bacc("TRN2", target_bir_lowering=False, num_devices=1)
    t = {k: nc.dram_tensor(k, v.shape, F32, kind="ExternalInput").ap() for k, v in arrays.items()}
    out = nc.dram_tensor("out", (BATCH, SEQ, DM), F32, kind="ExternalOutput").ap()
    cs_dram = nc.dram_tensor("cs_dram", (3, HEADS, TOK), BF16, kind="Internal").ap()
    x1_dram = nc.dram_tensor("x1_dram", (PAIRS, TOK, DM), F32, kind="Internal").ap()
    mamba_block(nc, t["u"], t["w_tiles"], t["w_za"], t["z_bias"], t["conv_w"], t["conv_b"], t["d_skip"], t["rms_w"],
                t["w_out"], t["mats"], t["pick"], t["marks"],
                cs_dram, x1_dram)
    expert_block(nc, x1_dram, t["w_up"], t["b_up"], t["w_down"], t["b_down"], t["w_gate"], t["mats"], out)
    r = run_bass_kernel_spmd(nc, [arrays], core_ids=[0])
    return r.results[0]["out"]
```

```python
from contextlib import ExitStack

import concourse.bass as bass
import numpy as np
from concourse import mybir

F32 = mybir.dt.float32
F32R = mybir.dt.float32r
BF16 = mybir.dt.bfloat16
ALU = mybir.AluOpType
ACT = mybir.ActivationFunctionType

P = 128
BATCH, SEQ, DM = 16, 256, 256
HEADS, NSTATE, HDIM, TAPS = 32, 64, 8, 4
PAIRS = BATCH // 2
TOK = 2 * SEQ
NBC = TOK // P
KT = DM // P
XT = HEADS * HDIM // P
NT = HEADS * NSTATE // P
TILES = XT + 2 * NT
QUADS, QH, QT = 4, 8, 8
SLOTS = 2 * NT
ZA = DM + HEADS
EXPERTS = 2
FF = 2 * DM
FT = FF // P
EPS = 1e-5
LAG = 11
STEP = 4
GUARDS = P // STEP - 1
CSL = 3 * QH
HPT = CSL + 3 + GUARDS

def za_blocks(n):
    return {0: (0, 1), 1: (2,), 2: (3,)}.get(n, ())


def slot_jobs(n, first):
    jobs = []
    g = n - LAG
    q, u = (g % SLOTS) // QH, g % QH
    tag = "-" if g < 0 else ""
    if u == 3 and (g >= 0 or not first):
        jobs.append(f"ST{q}{tag}")
    jobs += [f"ZA{c}" for c in za_blocks(n)]
    if n == LAG:
        jobs.append("XT0")
    if u in (0, 1) and (g >= 0 or not first):
        jobs.append(f"BT{q}{u}{tag}")
    if n == LAG:
        jobs.append("XT1")
    if n in (4, 5):
        jobs.append("CST" if n == 4 else "CSK")
    if not first:
        if n == 15:
            jobs += ["YT0-", "YT1-"]
        if n in (16, 17):
            jobs.append(f"OP{n - 16}-")
    if n == SLOTS - 1:
        jobs += ["XH0+", "XH1+"]
    return jobs


JOBS = {first: sum((slot_jobs(n, first) for n in range(SLOTS)), []) for first in (True, False)}
TAIL_JOBS = ["BT30-", "BT31-", "ST3-", "YT0-", "YT1-", "OP0-", "OP1-", "XE0", "XE1"]
JOBS_AHEAD = KT
JOBS_FIRST, JOBS_EACH = len(JOBS[True]), len(JOBS[False])


def taker(name):
    return "act" if name[:2] in ("BT", "XT") else "dve"


def count_of(names, engine):
    return sum(taker(name) == engine for name in names)


assert JOBS_EACH % 2 == 0

LEAD = [3, 2, 2, 2, 2, 2, 2, 2]


STATE_STEPS = [(2, "scored"), (3, "projecting"), (3, "scored"), (3, "mixed")]


def decays_of(n):
    return range(LEAD[(n - 1) % QH], LEAD[n % QH] + 1)


def seq(n):
    return (1, 3)[n] if n < 2 else n + XT


def lay_out():
    nx, ns = HEADS * HDIM, HEADS * NSTATE
    first = {0: 0, 2: P}
    for t in range(NT):
        first[seq(2 * t)] = nx + t * P
        first[seq(2 * t + 1)] = nx + ns + t * P
    return np.concatenate([np.arange(P) + first[m] for m in range(TILES)])


def constants():
    s = np.arange(P)
    ident = np.eye(P, dtype=np.float32)
    upto = -(s[:, None] <= s[None, :]).astype(np.float32)
    beyond = -(s[:, None] > s[None, :]).astype(np.float32)
    mats = np.stack([ident, upto, beyond], axis=1).reshape(P, 3 * P)
    pick = np.zeros((HPT, QH, NBC, P), np.float32)
    for part in range(3):
        for k in range(QH):
            pick[part * QH + k, k] = -1.0
    for r in range(GUARDS):
        pick[CSL + 3 + r, :, :, :(r + 1) * STEP] = -1e30
    marks = np.zeros((HPT - CSL, QUADS, NBC, P), np.float32)
    marks[:3] = 1.0
    for r in range(GUARDS):
        marks[3 + r, :, :, (r + 1) * STEP:(r + 2) * STEP] = 1.0
    return np.ascontiguousarray(mats), pick.reshape(HPT, QH, TOK), marks.reshape(HPT - CSL, QUADS, TOK)


def expert_weights(w_hi, w_lo):
    n = EXPERTS * KT * FF

    def view(t, k, at, a):
        return t[:, k, at:at + n].rearrange("p (a b) -> p a b", a=a)

    up, dn = EXPERTS * KT, EXPERTS * FT
    return {"up": (view(w_hi, 0, 0, up), view(w_lo, 0, 0, up)), "dn": (view(w_hi, 0, n, dn), view(w_lo, 0, n, dn))}


def mamba_block(nc, w_hi, w_lo, u_in, xh_hi, xh_lo, w_up, w_down, u, w_tiles, w_za, z_bias, conv_w, conv_b, d_skip, rms_w, w_out, mats, pick, marks, cs_dram, x1_dram):
    with ExitStack() as ctx:
        def sb(name, shape, dt=F32):
            return ctx.enter_context(nc.sbuf_tensor(name, shape, dt))

        def ps(name, shape=(P, 512)):
            return ctx.enter_context(nc.psum_tensor(name, list(shape), F32))

        def sem(name):
            return ctx.enter_context(nc.semaphore(name))

        za_hi, za_lo = sb("za_hi", [P, KT, ZA], F32R), sb("za_lo", [P, KT, ZA], F32R)
        wo_hi, wo_lo = sb("wo_hi", [P, KT, DM], F32R), sb("wo_lo", [P, KT, DM], F32R)
        bc = sb("bc", [P, 2 * QT, TOK])
        xT = sb("xT", [P, XT, TOK])
        u_norm = sb("u_norm", [P, NBC, DM])
        z_raw, z_silu = sb("z_raw", [P, NBC, DM]), sb("z_silu", [P, NBC, DM])
        u_res = z_raw
        x_tok = sb("x_tok", [P, NBC, DM])
        x_skip = sb("x_skip", [P, NBC, DM])
        x_dec = sb("x_dec", [P, 2, DM])
        y_sum = sb("y_sum", [P, NBC, DM])
        y_tmp = sb("y_tmp", [P, 2, QH * HDIM])
        yg = o_sb = u_norm
        yT_hi, yT_lo = sb("yT_hi", [P, KT, TOK], F32R), sb("yT_lo", [P, KT, TOK], F32R)
        NL, NM = 4, 2
        decay = sb("decay", [P, NL, TOK])
        mixed = sb("mixed", [P, NM, TOK])
        b_tok = sb("b_tok", [P, 2, TOK])
        states = sb("states", [P, 4, 2, 2 * HDIM])
        a_log, a_abs, sp = sb("a_log", [P, NBC, HEADS]), sb("a_abs", [P, NBC, HEADS]), sb("sp", [P, NBC, HEADS])
        cs_k, e_cs = sb("cs_k", [P, NBC, HEADS]), sb("e_cs", [P, NBC, HEADS])
        cs_rest = sb("cs_rest", [HEADS, TOK])
        cs_parts = sb("cs_parts", [HEADS, 3, TOK], BF16)
        d_stat = sb("d_stat", [HPT, QUADS, TOK], BF16)
        d_mov = sb("d_mov", [HPT, 2, QH, TOK], BF16)
        mats_sb = sb("mats_sb", [P, 3 * P])
        ident, upto, beyond = (mats_sb[:, k * P:(k + 1) * P] for k in range(3))
        cw, cb = sb("cw", [P, TILES, TAPS]), sb("cb", [P, TILES])
        zb = sb("zb", [P, DM])
        dsk = sb("dsk", [P, HEADS])
        rw = sb("rw", [P, KT])
        stats, mv = sb("stats", [P, NBC, 6]), sb("mv", [P, NBC, 2])
        ve, rstd = sb("ve", [P, NBC]), sb("rstd", [P, NBC])
        stats2, mv2 = sb("stats2", [P, NBC, 6]), sb("mv2", [P, NBC, 2])
        ve2, rstd2 = sb("ve2", [P, NBC]), sb("rstd2", [P, NBC])
        ss, ms, rms = sb("ss", [P, NBC]), sb("ms", [P, NBC]), sb("rms", [P, NBC])
        mhalf = sb("mhalf", [P, NBC])

        p_proj = [ps("p_proj0"), ps("p_proj1")]
        p_g = [ps("p_g0"), ps("p_g1")]
        p_d, p_y = ps("p_d"), ps("p_y")
        p_t = [ps("p_t0"), ps("p_t1")]

        s_mats, s_const, s_wo = sem("s_mats"), sem("s_const"), sem("s_wo")
        s_wld = [sem(f"s_wld{c}") for c in range(4)]
        s_whi, s_scaled = sem("s_whi"), sem("s_scaled")
        s_wsplit, s_small = sem("s_wsplit"), sem("s_small")
        s_init, s_pick = sem("s_init"), sem("s_pick")
        s_u = sem("s_u")
        s_ln, s_lnpow = sem("s_ln"), sem("s_lnpow")
        s_tfull = sem("s_tfull")
        s_tdone = {"dve": sem("s_tdone_dve"), "act": sem("s_tdone_act")}
        s_tc = sem("s_tc")
        s_proj = sem("s_proj")
        s_tap3 = sem("s_tap3")
        s_tap2, s_tap1, s_tap0 = sem("s_tap2"), sem("s_tap1"), sem("s_tap0")
        s_silu = sem("s_silu")
        s_xsilu, s_zsilu = sem("s_xsilu"), sem("s_zsilu")
        s_abs, s_sp1, s_sp2, s_sp = sem("s_abs"), sem("s_sp1"), sem("s_sp2"), sem("s_sp")
        s_parts = sem("s_parts")
        s_csst, s_dstat, s_dstat3, s_dmov = sem("s_csst"), sem("s_dstat"), sem("s_dstat3"), [sem("s_dmov0"), sem("s_dmov1")]
        s_ecs = sem("s_ecs")
        s_d, s_exp, s_mask = sem("s_d"), sem("s_exp"), sem("s_mask")
        s_g, s_m, s_y = sem("s_g"), sem("s_m"), sem("s_y")
        s_xdec, s_xskip = sem("s_xdec"), sem("s_xskip")
        s_yoff = sem("s_yoff")
        s_yev = sem("s_yev")
        s_yg, s_sq, s_ms, s_rms, s_yn = sem("s_yg"), sem("s_sq"), sem("s_ms"), sem("s_rms"), sem("s_yn")
        s_ln2, s_ln2pow, s_x1, s_x1out, s_ures = sem("s_ln2"), sem("s_ln2pow"), sem("s_x1"), sem("s_x1out"), sem("s_ures")
        s_xn2, s_held = sem("s_xn2"), sem("s_held")
        s_experts, s_ehi = [sem("s_experts_up"), sem("s_experts_dn")], sem("s_ehi")
        s_first = sem("s_first")
        s_eln, s_epow = sem("s_eln"), sem("s_epow")

        u_p = u.rearrange("(i b) (c p) d -> i p (b c) d", b=2, p=P)
        x1_p = x1_dram.rearrange("i (k p) d -> i p k d", p=P)

        def of_pass(t, i):
            if isinstance(i, int):
                return t[i]
            return t[bass.ds(i, 1)].rearrange("o p k d -> (o p) k d")

        def jobs_before(i):
            if isinstance(i, int) and i == 0:
                return JOBS_AHEAD
            return i * JOBS_EACH + (JOBS_AHEAD + JOBS_FIRST - JOBS_EACH)

        def place(name, i):
            if isinstance(i, int) and i == PAIRS:
                return TAIL_JOBS.index(name)
            return JOBS[isinstance(i, int) and i == 0].index(name)

        def job(name, i):
            return jobs_before(i) + place(name, i)

        def bank(name, i):
            ahead = jobs_before(i) if isinstance(i, int) else JOBS_AHEAD + JOBS_FIRST
            return (ahead + place(name, i)) % 2

        def jobs_of(i):
            return TAIL_JOBS if isinstance(i, int) and i == PAIRS else JOBS[isinstance(i, int) and i == 0]

        def taken_before(engine, i):
            ahead = JOBS_AHEAD if engine == "dve" else 0
            if isinstance(i, int) and i == 0:
                return ahead
            each = count_of(JOBS[False], engine)
            return i * each + (ahead + count_of(JOBS[True], engine) - each)

        def wait_taken(eng, name, i):
            upto_it = jobs_of(i)[:place(name, i) + 1]
            eng.wait_ge(s_tdone[taker(name)], taken_before(taker(name), i) + count_of(upto_it, taker(name)))

        def wait_bank(eng, name, i):
            k = place(name, i)
            if k >= 2:
                wait_taken(eng, jobs_of(i)[k - 2], i)
            else:
                eng.wait_ge(s_tdone["dve"], taken_before("dve", i) + (k - 1))

        def flat(t):
            return t[:].rearrange("p a b -> p (a b)")

        def heads_at(n, i):
            g = n - LAG
            if g >= 0:
                return (i, g)
            return None if isinstance(i, int) and i == 0 else (i - 1, g + SLOTS)

        def decay_heads(n, i):
            found = []
            for d in decays_of(n):
                g = n - LAG + d
                if g >= 0:
                    found.append((i, g))
                elif not (isinstance(i, int) and i == 0):
                    found.append((i - 1, g + SLOTS))
            return found

        def tile_of(n):
            return n % (2 * QT)

        WQ, STAGES = TILES * P // 2, 3
        free_tiles = (2 * QT * TOK - STAGES * WQ) // TOK
        bc_flat = bc[:, :, :].rearrange("p a b -> p (a b)")

        def stage(c):
            at = 2 * QT * TOK - (STAGES - c % STAGES) * WQ
            return bc_flat[:, at:at + WQ]

        def quarter(c):
            return c % KT, slice((c // KT) * WQ, (c // KT + 1) * WQ)

        def expert_stage(name):
            half = EXPERTS * KT * FF
            at = 0 if name == "up" else half
            return bc_flat[:, at:at + half].rearrange("p (a b) -> p a b", a=EXPERTS * (KT if name == "up" else FT))

        block = ctx.enter_context(nc.Block())

        @block.sync
        def _(sp_):
            w_src = w_tiles.rearrange("(k p) n -> p k n", p=P)
            def load_quarter(c):
                k, cols = quarter(c)
                sp_.dma_start(stage(c), w_src[:, k, cols]).then_inc(s_wld[c], 16)

            sp_.dma_start(u_in[:], of_pass(u_p, 0)).then_inc(s_u, 16)
            sp_.dma_start(mats_sb[:], mats).then_inc(s_mats, 16)
            load_quarter(0)
            load_quarter(1)
            sp_.dma_start(cw[:], conv_w).then_inc(s_const, 16)
            sp_.dma_start(cb[:], conv_b).then_inc(s_const, 16)
            sp_.dma_start(z_silu[:, 0:3, :].rearrange("p a b -> p (a b)")[:, 0:KT * ZA],
                          w_za.rearrange("(k p) n -> p k n", p=P)).then_inc(s_wo, 16)
            sp_.dma_start(zb[:], z_bias.rearrange("(o n) -> o n", o=1).broadcast_to([P, DM])).then_inc(s_const, 16)
            sp_.dma_start(dsk[:], d_skip.rearrange("(o n) -> o n", o=1).broadcast_to([P, HEADS])).then_inc(s_const, 16)
            sp_.dma_start(rw[:], rms_w).then_inc(s_const, 16)
            sp_.dma_start(y_sum[:, 2:4, :].rearrange("p a b -> p (a b)"),
                          w_out.rearrange("(k p) n -> p k n", p=P)).then_inc(s_wo, 16)
            load_quarter(2)
            sp_.wait_ge(s_wsplit, 1)
            load_quarter(3)

            def one_pass(i):
                first = isinstance(i, int)
                sp_.wait_ge(s_ln, i * 13 + 13)
                sp_.dma_start(u_in[:], of_pass(u_p, (i + 1) % PAIRS)).then_inc(s_u, 16)
                sp_.wait_ge(s_parts, i * 3 + 3)
                sp_.sem_inc(s_held, 1)
                if not first:
                    sp_.wait_ge(s_dstat3, i * 48)
                    sp_.sem_inc(s_held, 1)
                    sp_.wait_ge(s_dmov[0], i * 32)
                    sp_.wait_ge(s_dmov[1], i * 32)
                sp_.dma_start(cs_dram.rearrange("a h n -> h a n"), cs_parts[:]).then_inc(s_csst, 16)
                sp_.wait_ge(s_csst, i * 16 + 16)
                sp_.sem_inc(s_held, 1)
                if not first:
                    sp_.wait_ge(s_d, i * SLOTS - QH)
                else:
                    sp_.wait_ge(s_pick, 48)
                early = QUADS - 1
                for part in range(3):
                    sp_.dma_start(d_stat[part * QH:(part + 1) * QH, 0:early],
                                  cs_dram[part, 0:early * QH].rearrange("(q k) n -> k q n", k=QH)).then_inc(s_dstat, 16)
                for q in range(QUADS):
                    if q == 1:
                        if not first:
                            sp_.wait_ge(s_d, i * SLOTS)
                        for part in range(3):
                            sp_.dma_start(d_stat[part * QH:(part + 1) * QH, early],
                                          cs_dram[part, early * QH:]).then_inc(s_dstat3, 16)
                    if q == 2 and not first:
                        residual(i - 1, i)
                    if q >= 2 or not first:
                        sp_.wait_ge(s_d, i * SLOTS + QH * (q - 1))
                    sp_.dma_start(d_mov[CSL:CSL + 3, q % 2],
                                  cs_dram[:, q * QH:(q + 1) * QH, :]).then_inc(s_dmov[q % 2], 16)
                    if q == 2 and not first:
                        store(i - 1)

            def residual(i, body):
                sp_.wait_ge(s_zsilu, body + 1)
                sp_.dma_start(u_res[:], of_pass(u_p, i)).then_inc(s_ures, 16)

            def store(i):
                sp_.wait_ge(s_x1, i + 1)
                sp_.dma_start(of_pass(x1_p, i), o_sb[:]).then_inc(s_x1out, 16)

            sp_.sem_inc(s_x1out, 16)
            one_pass(0)
            with sp_.Fori(1, PAIRS) as i:
                one_pass(i)
            sp_.wait_ge(s_g, (PAIRS * QUADS - 1) * QH)
            sp_.wait_ge(s_yoff, (PAIRS * QUADS - 1) * (QH // 2))
            sp_.dma_start(expert_stage("up"), w_up.rearrange("e (k p) n -> p (e k) n", p=P)).then_inc(s_experts[0], 16)
            sp_.dma_start(expert_stage("dn"), w_down.rearrange("e (f p) n -> p (e f) n", p=P)).then_inc(s_experts[1], 16)
            sp_.wait_ge(s_ln, PAIRS * 13 + 13)
            sp_.dma_start(u_in[:], of_pass(x1_p, 0)).then_inc(s_first, 16)
            residual(PAIRS - 1, PAIRS - 1)
            store(PAIRS - 1)
            sp_.wait_ge(s_first, 16)
            sp_.wait_ge(s_x1out, 16 * (PAIRS + 1))

        @block.tensor
        def _(pe):
            def split3(out, a, a2, b, b2, k, last, start=None):
                for m, (x, y) in enumerate(((a, b), (a, b2), (a2, b))):
                    r = nc.tensor.matmul(out, x, y, start=(k == 0 and m == 0), stop=(last and m == 2))
                return r

            def open_job(name, i):
                wait_bank(pe, name, i)
                return p_t[bank(name, i)]

            def norm_transposes(i, body):
                pe.wait_ge(s_ln, i * 13 + 13)
                for k in range(KT):
                    t = p_t[k] if body is None else open_job(f"XH{k}+", body)
                    for c in range(NBC):
                        r = nc.tensor.transpose(t[:, c * P:(c + 1) * P], u_norm[:, c, k * P:(k + 1) * P], ident)
                    r.then_inc(s_tfull, 1)

            def project(i, m, between=lambda: None):
                if not (isinstance(i, int) and i == 0 and m < 2):
                    pe.wait_ge(s_tap0, i * TILES + m - 1)
                if isinstance(i, int) and m in (0, TILES // 2):
                    pe.wait_ge(s_wsplit, 4 if m else 2)
                if m == 0:
                    pe.wait_ge(s_tdone["dve"], taken_before("dve", i))
                for k in range(KT):
                    if k:
                        between()
                    cols = slice(m * P, (m + 1) * P)
                    r = split3(p_proj[m % 2][:], w_hi[:, k, cols], w_lo[:, k, cols], xh_hi[:, k], xh_lo[:, k], k, k == KT - 1)
                r.then_inc(s_proj, 1)

            def project_za(i, c):
                t = open_job(f"ZA{c}", i)
                if isinstance(i, int) and c == 0:
                    pe.wait_ge(s_small, 1)
                for k in range(KT):
                    cols = slice(c * P, (c + 1) * P)
                    r = split3(t[:, 0:ZA], xh_hi[:, k, cols], xh_lo[:, k, cols], za_hi[:, k], za_lo[:, k], k, k == KT - 1)
                r.then_inc(s_tfull, 1)

            def cumsums(i):
                t = open_job("CST", i)
                pe.wait_ge(s_sp, i + 1)
                for c in range(NBC):
                    r = nc.tensor.matmul(t[0:HEADS, c * P:(c + 1) * P], sp[:, c], upto, start=True, stop=True)
                r.then_inc(s_tfull, 1)

            def token_cumsums(i):
                t = open_job("CSK", i)
                for c in range(NBC):
                    r = nc.tensor.matmul(t[:, c * HEADS:(c + 1) * HEADS], upto if c % 2 else beyond, sp[:, c],
                                         start=True, stop=True)
                r.then_inc(s_tfull, 1)

            def x_transposes(i, x):
                if x == 0:
                    pe.wait_ge(s_xsilu, i + 1)
                t = open_job(f"XT{x}", i)
                for c in range(NBC):
                    r = nc.tensor.transpose(t[:, c * P:(c + 1) * P], xT[:, x, c * P:(c + 1) * P], ident)
                r.then_inc(s_tfull, 1)

            def decay_exponents(i, g):
                q, k = g // QH, g % QH
                if not (isinstance(i, int) and i == 0 and g == 0):
                    pe.wait_ge(s_exp, i * SLOTS + g)
                if k == 0:
                    pe.wait_ge(s_dmov[q % 2], i * 32 + 16 * (q // 2 + 1))
                    if q == 0:
                        pe.wait_ge(s_dstat, i * 48 + 48)
                    if q == QUADS - 1:
                        pe.wait_ge(s_dstat3, i * 48 + 48)
                for c in range(NBC):
                    r = nc.tensor.matmul(p_d[:, c * P:(c + 1) * P], d_stat[:, q, c * P:(c + 1) * P],
                                         d_mov[:, q % 2, k, c * P:(c + 1) * P], start=True, stop=True)
                r.then_inc(s_d, 1)

            def scores(i, g):
                q, k = g // QH, g % QH
                if k % 2 == 0:
                    pe.wait_ge(s_silu, i * NT + 4 * q + k // 2 + 1)
                if not (isinstance(i, int) and i == 0 and g < 2):
                    pe.wait_ge(s_m, i * SLOTS + g - 1)
                rows = slice((g % 2) * NSTATE, (g % 2 + 1) * NSTATE)
                tb = tile_of(q * QT + 2 * (k // 2))
                for c in range(NBC):
                    r = nc.tensor.matmul(p_g[g % 2][:, c * P:(c + 1) * P], bc[rows, tb, c * P:(c + 1) * P],
                                         bc[rows, tb + 1, c * P:(c + 1) * P], start=True, stop=True)
                r.then_inc(s_g, 1)

            def mix_x(i, g):
                q, k = g // QH, g % QH
                pe.wait_ge(s_m, i * SLOTS + g + 1)
                if k == 0 and not (isinstance(i, int) and i == 0 and q == 0):
                    pe.wait_ge(s_yev, i * 12 + 3 * q)
                if g == 0:
                    wait_taken(pe, "XT1", i)
                for c in range(NBC):
                    r = nc.tensor.matmul(p_y[:, c * 64 + k * HDIM:c * 64 + (k + 1) * HDIM],
                                         mixed[:, g % NM, c * P:(c + 1) * P],
                                         x_tok[:, c, g * HDIM:(g + 1) * HDIM], start=True, stop=True)
                r.then_inc(s_y, 1)

            def b_transposes(i, q, h, body, tag):
                t = open_job(f"BT{q}{h}{tag}", body)
                pe.wait_ge(s_silu, i * NT + 4 * q + 2 * h + 2)
                for j in range(2):
                    for b in range(2):
                        tb = tile_of(q * QT + 2 * (2 * h + j))
                        r = nc.tensor.transpose(t[:, (2 * j + b) * P:(2 * j + b + 1) * P],
                                                bc[:, tb, 2 * b * P:(2 * b + 1) * P], ident)
                r.then_inc(s_tfull, 1)

            def chunk_states(i, q, body, tag, pairs):
                if 0 in pairs:
                    open_job(f"ST{q}{tag}", body)
                    wait_taken(pe, f"BT{q}0{tag}", body)
                    pe.wait_ge(s_xdec, i + 1)
                if 2 in pairs:
                    wait_taken(pe, f"BT{q}1{tag}", body)
                t = p_t[bank(f"ST{q}{tag}", body)]
                for j in pairs:
                    for b in range(2):
                        a = (j % 2) * 2 + b
                        at = (2 * j + b) * 2 * HDIM
                        r = nc.tensor.matmul(t[:, at:at + 2 * HDIM], b_tok[:, j // 2, a * P:(a + 1) * P],
                                             x_dec[:, b, (q * QH + 2 * j) * HDIM:(q * QH + 2 * j + 2) * HDIM],
                                             start=True, stop=True)
                if 3 in pairs:
                    r.then_inc(s_tfull, 1)

            def y_from_state(i, q, body, tag, pairs):
                if 0 in pairs:
                    wait_taken(pe, f"ST{q}{tag}", body)
                for j in pairs:
                    for b in range(2):
                        tc_ = tile_of(q * QT + 2 * j + 1)
                        at = 256 + b * 64 + 2 * j * HDIM
                        r = nc.tensor.matmul(p_y[:, at:at + 2 * HDIM], bc[:, tc_, (2 * b + 1) * P:(2 * b + 2) * P],
                                             states[:, j, b, :], start=True, stop=True)
                r.then_inc(s_yoff, 1)

            def y_transposes(i, body):
                pe.wait_ge(s_yn, i * 4 + 4)
                for k in range(KT):
                    t = open_job(f"YT{k}-", body)
                    for c in range(NBC):
                        r = nc.tensor.transpose(t[:, c * P:(c + 1) * P], yg[:, c, k * P:(k + 1) * P], ident)
                    r.then_inc(s_tfull, 1)

            def project_out(i, h, body):
                t = open_job(f"OP{h}-", body)
                wait_taken(pe, "YT1-", body)
                pe.wait_ge(s_small, 2)
                for j in range(2):
                    for k in range(KT):
                        cols = slice((2 * h + j) * P, (2 * h + j + 1) * P)
                        r = split3(t[:, j * DM:(j + 1) * DM], yT_hi[:, k, cols], yT_lo[:, k, cols],
                                   wo_hi[:, k], wo_lo[:, k], k, k == KT - 1)
                r.then_inc(s_tfull, 1)

            def some_states(n, i, when, tail=False):
                now = None if tail and n >= LAG else heads_at(n, i)
                if now:
                    ii, g = now
                    q, u = g // QH, g % QH
                    tag = "-" if n - LAG < 0 else ""
                    if (u, when) in STATE_STEPS:
                        chunk_states(ii, q, i, tag, (STATE_STEPS.index((u, when)),))
                    if u >= 4 and when == "scored":
                        y_from_state(ii, q, i, tag, (u - 4,))

            def attend(n, i, tail=False):
                ahead = [(ii, g) for ii, g in decay_heads(n, i) if not tail or ii is not i]
                for ii, g in ahead[:-1]:
                    decay_exponents(ii, g)
                now = None if tail and n >= LAG else heads_at(n, i)
                if now:
                    ii, g = now
                    q, u = g // QH, g % QH
                    tag = "-" if n - LAG < 0 else ""
                    scores(ii, g)
                some_states(n, i, "scored", tail)
                for ii, g in ahead[-1:]:
                    decay_exponents(ii, g)
                if n == LAG and not tail:
                    x_transposes(i, 0)
                behind = heads_at(n - 1, i)
                if behind:
                    mix_x(*behind)
                if now:
                    if u in (0, 1):
                        b_transposes(ii, q, u, i, tag)
                if n == LAG and not tail:
                    x_transposes(i, 1)
                some_states(n, i, "mixed", tail)

            def one_pass(i):
                first = isinstance(i, int)
                for n in range(SLOTS):
                    if n == 0:
                        attend(n, i)
                    if n < XT:
                        project(i, 2 * n)
                    project(i, seq(n), lambda: some_states(n, i, "projecting"))
                    for c in za_blocks(n):
                        project_za(i, c)
                    if n:
                        attend(n, i)
                    if n == 4:
                        cumsums(i)
                    if n == 5:
                        token_cumsums(i)
                    if not first:
                        if n == 15:
                            y_transposes(i - 1, i)
                        if n in (16, 17):
                            project_out(i - 1, n - 16, i)
                norm_transposes(i + 1, i)

            pe.wait_ge(s_mats, 16)
            norm_transposes(0, None)
            one_pass(0)
            with pe.Fori(1, PAIRS) as i:
                one_pass(i)
            for n in range(LAG + 1):
                some_states(n, PAIRS, "projecting", tail=True)
                attend(n, PAIRS, tail=True)
            y_transposes(PAIRS - 1, PAIRS)
            project_out(PAIRS - 1, 0, PAIRS)
            project_out(PAIRS - 1, 1, PAIRS)
            pe.wait_ge(s_eln, 13)
            for k in range(KT):
                t = open_job(f"XE{k}", PAIRS)
                for c in range(NBC):
                    r = nc.tensor.transpose(t[:, c * P:(c + 1) * P], u_in[:, c, k * P:(k + 1) * P], ident)
                r.then_inc(s_tfull, 1)

        @block.scalar
        def _(act):
            def newest_tap(i, m, n=None):
                if n is not None:
                    q, j = n // QT, (n % QT) // 2
                    if q >= 2 or not isinstance(i, int):
                        act.wait_ge(s_g, i * SLOTS + (q - 2) * QH + 2 * j + 2)
                        if n % 2:
                            act.wait_ge(s_yoff, i * 16 + 4 * (q - 2) + j + 1)
                    elif n == free_tiles:
                        act.wait_ge(s_wsplit, 4)
                    dst = bc[:, tile_of(n)]
                else:
                    if m == 0 and isinstance(i, int):
                        act.wait_ge(s_const, 16 * 5)
                    elif m == 0:
                        act.wait_ge(s_tfull, jobs_before(i))
                    dst = xT[:, m // 2]
                act.wait_ge(s_proj, i * TILES + m + 1)
                nc.scalar.activation(dst, p_proj[m % 2][:], ACT.Identity, bias=cb[:, m:m + 1],
                                     scale=cw[:, m, TAPS - 1:TAPS]).then_inc(s_tap3, 1)

            def silu_pairs(i, q, h):
                act.wait_ge(s_tap0, i * TILES + XT + (q + 1) * QT)
                for j in (2 * h, 2 * h + 1):
                    t0 = tile_of(q * QT + 2 * j)
                    v = bc[:, t0:t0 + 2].rearrange("p a b -> p (a b)")
                    nc.scalar.activation(v, v, ACT.Silu).then_inc(s_silu, 1)

            def silu_x(i):
                v = xT[:].rearrange("p a b -> p (a b)")
                act.wait_ge(s_tap0, i * TILES + 3)
                nc.scalar.activation(v, v, ACT.Silu).then_inc(s_xsilu, 1)

            def silu_z(i):
                wait_taken(act, "ZA3", i)
                if isinstance(i, int):
                    act.wait_ge(s_small, 1)
                else:
                    act.wait_ge(s_yg, i)
                nc.scalar.activation(z_silu[:].rearrange("p a b -> p (a b)"), z_raw[:].rearrange("p a b -> p (a b)"),
                                     ACT.Silu).then_inc(s_zsilu, 1)

            def softplus(i):
                act.wait_ge(s_abs, i + 1)
                nc.scalar.activation(a_abs[:].rearrange("p a b -> p (a b)"), a_abs[:].rearrange("p a b -> p (a b)"),
                                     ACT.Exp, scale=-1.0).then_inc(s_sp1, 1)
                act.wait_ge(s_sp1, i + 1)
                nc.scalar.activation(a_abs[:].rearrange("p a b -> p (a b)"), a_abs[:].rearrange("p a b -> p (a b)"),
                                     ACT.Ln, bias=1.0).then_inc(s_sp2, 1)

            def exp_cs(i):
                wait_taken(act, "CSK", i)
                if not isinstance(i, int):
                    act.wait_ge(s_yev, i * 12)
                    act.wait_ge(s_xdec, i)
                nc.scalar.activation(e_cs[:].rearrange("p a b -> p (a b)"), cs_k[:].rearrange("p a b -> p (a b)"),
                                     ACT.Exp).then_inc(s_ecs, 1)

            def decays(i, g):
                act.wait_ge(s_d, i * SLOTS + g + 1)
                if not (isinstance(i, int) and i == 0 and g < NL):
                    act.wait_ge(s_m, i * SLOTS + g - NL + 1)
                nc.scalar.activation(decay[:, g % NL], p_d[:], ACT.Exp).then_inc(s_exp, 1)

            def copy_out(dst, t):
                nc.scalar.activation(dst, t, ACT.Copy).then_inc(s_tdone["act"], 1)

            def take(name, i):
                act.wait_ge(s_tfull, job(name, i) + 1)
                return p_t[bank(name, i)]

            def take_x(i, x):
                t = take(f"XT{x}", i)
                if not isinstance(i, int) and x == 0:
                    act.wait_ge(s_y, i * SLOTS)
                    act.wait_ge(s_xskip, i * 5)
                copy_out(x_tok[:, :, x * P:(x + 1) * P], t[:].rearrange("p (c n) -> p c n", c=NBC))

            def take_b(n, i):
                before = heads_at(n - 1, i)
                if before and before[1] % QH in (0, 1):
                    q, h = before[1] // QH, before[1] % QH
                    copy_out(b_tok[:, h], take(f"BT{q}{h}{'-' if n - 1 < LAG else ''}", i)[:])

            def rms_norm(i):
                act.wait_ge(s_rms, i + 1)
                for c in range(NBC):
                    nc.scalar.activation(yg[:, c], yg[:, c], ACT.Copy, scale=rms[:, c:c + 1]).then_inc(s_yn, 1)

            def squares(i):
                act.wait_ge(s_yg, i + 1)
                for c in range(NBC):
                    nc.scalar.activation(y_sum[:, c], yg[:, c], ACT.Square, accum_out=ss[:, c:c + 1]).then_inc(s_sq, 1)

            def one_pass(i):
                first = isinstance(i, int)
                for n in range(SLOTS):
                    if n == 0:
                        for head in decay_heads(n, i):
                            decays(*head)
                    if n < XT:
                        newest_tap(i, 2 * n)
                    newest_tap(i, seq(n), n)
                    if n % QT in (1, 2):
                        q, h = (n // QT - 1) % QUADS, n % QT - 1
                        if n > QT or not first:
                            silu_pairs(i if n > QT else i - 1, q, h)
                        if n == QT + 1:
                            silu_x(i)
                        if n == 2 * QT + 1:
                            silu_z(i)
                    if n == 3:
                        softplus(i)
                    for head in decay_heads(n, i) if n else []:
                        decays(*head)
                    if n == 12:
                        exp_cs(i)
                    if n != LAG + 1:
                        take_b(n, i)
                    if n == LAG:
                        take_x(i, 0)
                        take_b(n + 1, i)
                        take_x(i, 1)
                    if not first:
                        if n == 13:
                            squares(i - 1)
                        if n == 14:
                            rms_norm(i - 1)

            for c in range(4):
                k, cols = quarter(c)
                act.wait_ge(s_wld[c], 16)
                nc.scalar.activation(w_hi[:, k, cols], stage(c), ACT.Copy).then_inc(s_whi, 1)
            one_pass(0)
            with act.Fori(1, PAIRS) as i:
                one_pass(i)
            for n in range(LAG):
                if n in (1, 2):
                    silu_pairs(PAIRS - 1, QUADS - 1, n - 1)
                for ii, g in decay_heads(n, PAIRS):
                    if ii < PAIRS:
                        decays(ii, g)
                take_b(n, PAIRS)
                if n in (6, 8):
                    which = (n - 6) // 2
                    name = ("up", "dn")[which]
                    act.wait_ge(s_experts[which], 16)
                    act.wait_ge(s_proj, PAIRS * TILES)
                    nc.scalar.activation(expert_weights(w_hi, w_lo)[name][0], expert_stage(name), ACT.Copy).then_inc(s_ehi, 1)
            squares(PAIRS - 1)
            rms_norm(PAIRS - 1)

        @block.gpsimd
        def _(pool):
            pool.memset(mhalf[:], -0.5).then_inc(s_init, 1)
            pool.memset(states[:].rearrange("p a b c -> p (a b c)"), 0.0).then_inc(s_init, 1)
            pool.dma_start(d_stat[CSL:HPT], marks).then_inc(s_pick, 16)
            for half in range(2):
                pool.dma_start(d_mov[:, half], pick).then_inc(s_pick, 16)
            pool.wait_ge(s_init, 2)

            def causal(i, g):
                pool.wait_ge(s_exp, i * SLOTS + g + 1)
                pool.sem_inc(s_held, 1)
                v = decay[:, g % NL].rearrange("p (c l) -> p c l", c=NBC)
                pool.affine_select(out=v, in_=v, compare_op=ALU.is_ge, fill=0.0, base=0,
                                   pattern=[[0, NBC], [1, P]], channel_multiplier=-1).then_inc(s_mask, 1)

            def pow_of(out, src, done, ready, value, i):
                pool.wait_ge(ready, value)
                pool.tensor_tensor(out, src, mhalf[:], ALU.pow).then_inc(done, 1)

            def gate(i):
                pool.wait_ge(s_yev, i * 12 + 12)
                pool.wait_ge(s_zsilu, i + 1)
                pool.wait_ge(s_x1out, i * 16 + 16)
                pool.tensor_tensor(flat(yg), flat(y_sum), flat(z_silu), ALU.mult).then_inc(s_yg, 1)

            def add_residual(i):
                pool.wait_ge(s_xn2, i * 4 + 4)
                pool.wait_ge(s_ures, i * 16 + 16)
                pool.tensor_tensor(flat(o_sb), flat(o_sb), flat(u_res), ALU.add).then_inc(s_x1, 1)

            def x_decayed(i):
                wait_taken(pool, "XT1", i)
                if not isinstance(i, int):
                    pool.wait_ge(s_yoff, i * 16)
                pool.wait_ge(s_ecs, i + 1)
                for b in range(2):
                    pool.tensor_tensor(x_dec[:, b].rearrange("p (h d) -> p h d", d=HDIM),
                                       x_tok[:, 2 * b].rearrange("p (h d) -> p h d", d=HDIM),
                                       e_cs[:, 2 * b].unsqueeze(2).broadcast_to([P, HEADS, HDIM]), ALU.mult)\
                        .then_inc(s_xdec if b else s_xskip, 1)

            def x_skipped(i):
                if not isinstance(i, int):
                    pool.wait_ge(s_yev, i * 12)
                for c in range(NBC):
                    pool.tensor_tensor(x_skip[:, c].rearrange("p (h d) -> p h d", d=HDIM),
                                       x_tok[:, c].rearrange("p (h d) -> p h d", d=HDIM),
                                       dsk[:].unsqueeze(2).broadcast_to([P, HEADS, HDIM]), ALU.mult)\
                        .then_inc(s_xskip, 1)

            def one_pass(i):
                first = isinstance(i, int)
                for n in range(SLOTS):
                    for head in decay_heads(n, i):
                        causal(*head)
                    if n == 12:
                        x_decayed(i)
                        if not first:
                            gate(i - 1)
                    if n == 14:
                        x_skipped(i)
                    if not first:
                        if n == 13:
                            pow_of(rms[:], ms[:], s_rms, s_ms, i, i)
                        if n == 20:
                            pow_of(rstd2[:], ve2[:], s_ln2pow, s_ln2, i * 9, i)
                        if n == 22:
                            add_residual(i - 1)
                    if n == 26:
                        pow_of(rstd[:], ve[:], s_lnpow, s_ln, i * 13 + 22, i)

            pow_of(rstd[:], ve[:], s_lnpow, s_ln, 9, 0)
            one_pass(0)
            with pool.Fori(1, PAIRS) as i:
                one_pass(i)
            for n in range(LAG):
                for ii, g in decay_heads(n, PAIRS):
                    if ii < PAIRS:
                        causal(ii, g)
                if n == 8:
                    pow_of(rstd[:], ve[:], s_epow, s_eln, 9, PAIRS)
            gate(PAIRS - 1)
            pow_of(rms[:], ms[:], s_rms, s_ms, PAIRS, PAIRS)
            pow_of(rstd2[:], ve2[:], s_ln2pow, s_ln2, PAIRS * 9, PAIRS)
            add_residual(PAIRS - 1)

        @block.vector
        def _(dve):
            def weights_lo(c):
                k, cols = quarter(c)
                dve.wait_ge(s_whi, c + 1)
                nc.vector.tensor_tensor(w_lo[:, k, cols], stage(c), w_hi[:, k, cols].bitcast(F32),
                                        ALU.subtract).then_inc(s_wsplit, 1)

            def split_small():
                dve.wait_ge(s_const, 16 * 5)
                dve.wait_ge(s_wo, 32)
                za = z_silu[:, 0:3, :].rearrange("p a b -> p (a b)")[:, 0:KT * ZA]
                nc.vector.tensor_copy(flat(za_hi), za).then_inc(s_scaled, 1)
                dve.wait_ge(s_scaled, 1)
                nc.vector.tensor_tensor(flat(za_lo), za, flat(za_hi).bitcast(F32), ALU.subtract).then_inc(s_small, 1)
                wo, scaled = y_sum[:, 2:4, :], y_sum[:, 0:2, :].rearrange("p a b -> p (a b)")
                for k in range(KT):
                    nc.vector.tensor_scalar(y_sum[:, k], wo[:, k], rw[:, k:k + 1], None, ALU.mult).then_inc(s_scaled, 1)
                dve.wait_ge(s_scaled, 3)
                nc.vector.tensor_copy(flat(wo_hi), scaled).then_inc(s_scaled, 1)
                dve.wait_ge(s_scaled, 4)
                nc.vector.tensor_tensor(flat(wo_lo), scaled, flat(wo_hi).bitcast(F32), ALU.subtract).then_inc(s_small, 1)


            def norm_stats(i, blocks):
                if 0 in blocks:
                    dve.wait_ge(s_u, i * 16 + 16)
                for c in blocks:
                    nc.vector.bn_stats(stats[:, c], u_in[:, c]).then_inc(s_ln, 1)

            def norm_variance(i):
                dve.wait_ge(s_ln, i * 13 + 4)
                dve.sem_inc(s_held, 1)
                for c in range(NBC):
                    nc.vector.bn_aggr(mv[:, c], stats[:, c]).then_inc(s_ln, 1)
                dve.wait_ge(s_ln, i * 13 + 8)
                nc.vector.tensor_scalar(ve[:], mv[:, :, 1], EPS, None, ALU.add).then_inc(s_ln, 1)

            def norm_apply(i, body, blocks):
                if 0 in blocks:
                    dve.wait_ge(s_lnpow, i + 1)
                    if body is not None:
                        dve.wait_ge(s_x1out, body * 16 + 16)
                for c in blocks:
                    nc.vector.tensor_scalar(u_norm[:, c], u_in[:, c], mv[:, c, 0:1], rstd[:, c:c + 1],
                                            ALU.subtract, ALU.mult).then_inc(s_ln, 1)

            def take(name, i):
                dve.wait_ge(s_tfull, job(name, i) + 1)
                return p_t[bank(name, i)]

            def split_job(t, hi, lo, count):
                nc.vector.tensor_copy(hi, t[:]).then_inc(s_tc, 1)
                dve.wait_ge(s_tc, count)
                nc.vector.tensor_tensor(lo, t[:], hi.bitcast(F32), ALU.subtract).then_inc(s_tdone["dve"], 1)

            def take_norm(body):
                if body is not None:
                    dve.wait_ge(s_proj, body * TILES + TILES)
                for k in range(KT):
                    if body is None:
                        dve.wait_ge(s_tfull, k + 1)
                        split_job(p_t[k], xh_hi[:, k], xh_lo[:, k], k + 1)
                    else:
                        done = 2 if isinstance(body, int) else body * 4 + 2
                        split_job(take(f"XH{k}+", body), xh_hi[:, k], xh_lo[:, k], done + k + 1)

            def take_za(i, c):
                t = take(f"ZA{c}", i)
                if not isinstance(i, int) and c == 0:
                    dve.wait_ge(s_zsilu, i)
                nc.vector.tensor_tensor(z_raw[:, c], t[:, 0:DM], zb[:], ALU.add)
                nc.vector.tensor_copy(a_log[:, c], t[:, DM:ZA]).then_inc(s_tdone["dve"], 1)

            def abs_a(i):
                wait_taken(dve, "ZA3", i)
                nc.vector.scalar_tensor_tensor(out=flat(a_abs), in0=flat(a_log), scalar=-1.0, in1=flat(a_log),
                                               op0=ALU.mult, op1=ALU.max).then_inc(s_abs, 1)

            def softplus_sum(i):
                dve.wait_ge(s_sp2, i + 1)
                if not isinstance(i, int):
                    dve.wait_ge(s_tfull, jobs_before(i))
                nc.vector.scalar_tensor_tensor(out=flat(sp), in0=flat(a_log), scalar=0.0, in1=flat(a_abs),
                                               op0=ALU.max, op1=ALU.add).then_inc(s_sp, 1)

            def take_cs(i):
                t = take("CST", i)
                if not isinstance(i, int):
                    dve.wait_ge(s_csst, i * 16)
                cs = t[0:HEADS, :]
                nc.vector.tensor_copy(cs_parts[:, 0], cs).then_inc(s_parts, 1)
                dve.wait_ge(s_parts, i * 3 + 1)
                nc.vector.tensor_tensor(cs_rest[:], cs, cs_parts[:, 0], ALU.subtract).then_inc(s_tdone["dve"], 1)

            def take_token_cs(i):
                wait_taken(dve, "CST", i)
                nc.vector.tensor_copy(cs_parts[:, 1], cs_rest[:]).then_inc(s_parts, 1)
                t = take("CSK", i)
                if not isinstance(i, int):
                    dve.wait_ge(s_ecs, i)
                nc.vector.tensor_copy(flat(cs_k), t[:, 0:NBC * HEADS]).then_inc(s_tdone["dve"], 1)
                dve.wait_ge(s_parts, i * 3 + 2)
                nc.vector.tensor_tensor(cs_parts[:, 2], cs_rest[:], cs_parts[:, 1], ALU.subtract).then_inc(s_parts, 1)

            def take_states(i, q, body, tag):
                t = take(f"ST{q}{tag}", body)
                if not (isinstance(i, int) and i == 0 and q == 0):
                    dve.wait_ge(s_yoff, i * 16 + 4 * q)
                for e in range(2):
                    rows = slice(e * NSTATE, (e + 1) * NSTATE)
                    cols = slice(e * HDIM, (e + 1) * HDIM)
                    r = nc.vector.tensor_copy(states[rows, :, :, cols].rearrange("p a b c -> p (a b) c"),
                                              t[rows, 0:16 * HDIM].rearrange("p (a c) -> p a c", c=2 * HDIM)[:, :, cols])
                r.then_inc(s_tdone["dve"], 1)

            def taps(i, m, w):
                shift = TAPS - 1 - w
                n = {1: 0, 3: 1}.get(m, m - XT)
                dst = xT[:, m // 2] if m in (0, 2) else bc[:, tile_of(n)]
                d3 = dst.rearrange("p (b t) -> p b t", b=2)
                src = p_proj[m % 2][:].rearrange("p (b t) -> p b t", b=2)
                before, done = {2: (s_tap3, s_tap2), 1: (s_tap2, s_tap1), 0: (s_tap1, s_tap0)}[w]
                dve.wait_ge(before, i * TILES + m + 1)
                nc.vector.scalar_tensor_tensor(out=d3[:, :, shift:], in0=src[:, :, :SEQ - shift], scalar=cw[:, m, w:w + 1],
                                               in1=d3[:, :, shift:], op0=ALU.mult, op1=ALU.add).then_inc(done, 1)

            def mix(i, g):
                dve.wait_ge(s_mask, i * SLOTS + g + 1)
                dve.wait_ge(s_g, i * SLOTS + g + 1)
                if not (isinstance(i, int) and i == 0 and g < NM):
                    dve.wait_ge(s_y, i * SLOTS + g - NM + 1)
                nc.vector.tensor_tensor(mixed[:, g % NM], p_g[g % 2][:], decay[:, g % NL], ALU.mult).then_inc(s_m, 1)

            def take_y(i, q):
                dve.wait_ge(s_y, i * SLOTS + (q + 1) * QH)
                dve.wait_ge(s_yoff, i * 16 + 4 * q + 4)
                dve.wait_ge(s_xskip, i * 5 + 5)
                cols = slice(q * QH * HDIM, (q + 1) * QH * HDIM)
                nc.vector.tensor_tensor(y_sum[:, :, cols], p_y[:, 0:256].rearrange("p (c n) -> p c n", c=NBC),
                                        x_skip[:, :, cols], ALU.add).then_inc(s_yev, 1)
                nc.vector.tensor_tensor(y_tmp[:].rearrange("p b (h d) -> p b h d", d=HDIM),
                                        p_y[:, 256:384].rearrange("p (b h d) -> p b h d", b=2, d=HDIM),
                                        e_cs[:, 1::2, q * QH:(q + 1) * QH].unsqueeze(3).broadcast_to([P, 2, QH, HDIM]),
                                        ALU.mult).then_inc(s_yev, 1)
                dve.wait_ge(s_yev, i * 12 + 3 * q + 2)
                nc.vector.tensor_tensor(y_sum[:, 1::2, cols], y_sum[:, 1::2, cols], y_tmp[:], ALU.add).then_inc(s_yev, 1)

            def mean_squares(i):
                dve.wait_ge(s_sq, i * 4 + 4)
                nc.vector.tensor_scalar(ms[:], ss[:], 1.0 / DM, EPS, ALU.mult, ALU.add).then_inc(s_ms, 1)

            def take_yT(i, body):
                for k in range(KT):
                    split_job(take(f"YT{k}-", body), yT_hi[:, k], yT_lo[:, k], body * 4 + k + 1)

            def take_out(i, h, body):
                if h == 0:
                    dve.wait_ge(s_tfull, job("YT1-", body) + 1)
                nc.vector.tensor_copy(o_sb[:, 2 * h:2 * h + 2].rearrange("p a b -> p (a b)"),
                                      take(f"OP{h}-", body)[:]).then_inc(s_tdone["dve"], 1)

            def out_stats(i, body, h):
                wait_taken(dve, f"OP{h}-", body)
                for c in (2 * h, 2 * h + 1):
                    nc.vector.bn_stats(stats2[:, c], o_sb[:, c]).then_inc(s_ln2, 1)

            def out_variance(i):
                for c in range(NBC):
                    dve.wait_ge(s_ln2, i * 9 + c + 1)
                    dve.sem_inc(s_held, 1)
                    nc.vector.bn_aggr(mv2[:, c], stats2[:, c]).then_inc(s_ln2, 1)
                dve.wait_ge(s_ln2, i * 9 + 8)
                nc.vector.tensor_scalar(ve2[:], mv2[:, :, 1], EPS, None, ALU.add).then_inc(s_ln2, 1)

            def norm_out(i, h):
                dve.wait_ge(s_ln2pow, i + 1)
                for c in (2 * h, 2 * h + 1):
                    nc.vector.tensor_scalar(o_sb[:, c], o_sb[:, c], mv2[:, c, 0:1], rstd2[:, c:c + 1],
                                            ALU.subtract, ALU.mult).then_inc(s_xn2, 1)

            def slot_jobs_done(n, i, tail=False):
                now = None if tail and n >= LAG else heads_at(n, i)
                if now:
                    ii, g = now
                    q, h = g // QH, g % QH
                    tag = "-" if n < LAG else ""
                    if h == 3:
                        take_states(ii, q, i, tag)
                behind = heads_at(n - 1, i)
                if behind and behind[1] % QH == QH - 1:
                    take_y(behind[0], behind[1] // QH)

            def one_pass(i):
                first = isinstance(i, int)
                for n in range(SLOTS):
                    now = heads_at(n, i)
                    if n == 0 and now:
                        mix(*now)
                    if n < XT:
                        if n:
                            taps(i, 2 * n - 1, 0)
                        taps(i, 2 * n, 2)
                        taps(i, 2 * n, 1)
                    m = seq(n)
                    taps(i, m - 1, 0)
                    taps(i, m, 2)
                    if n and now:
                        mix(*now)
                    if n == 4:
                        softplus_sum(i)
                    taps(i, m, 1)
                    for c in za_blocks(n):
                        take_za(i, c)
                    if n == 2:
                        abs_a(i)
                    slot_jobs_done(n, i)
                    if n == 4:
                        take_cs(i)
                    if n == 5:
                        take_token_cs(i)
                    if not first:
                        if n == 13:
                            mean_squares(i - 1)
                        if n == 15:
                            take_yT(i - 1, i)
                        if n in (17, 18):
                            take_out(i - 1, n - 17, i)
                        if n in (18, 19):
                            out_stats(i - 1, i, n - 18)
                        if n == 19:
                            out_variance(i - 1)
                        if n in (20, 21):
                            norm_out(i - 1, n - 20)
                    if n in (24, 25):
                        norm_stats(i + 1, (0, 1) if n == 24 else (2, 3))
                    if n == 26:
                        norm_variance(i + 1)
                    if n in (27, 28):
                        norm_apply(i + 1, i, (0, 1) if n == 27 else (2, 3))
                taps(i, TILES - 1, 0)
                take_norm(i)

            def experts_lo(name, count):
                hi, lo = expert_weights(w_hi, w_lo)[name]
                dve.wait_ge(s_ehi, count)
                nc.vector.tensor_tensor(lo, expert_stage(name), hi.bitcast(F32), ALU.subtract)

            def experts_stats():
                dve.wait_ge(s_first, 16)
                for c in range(NBC):
                    nc.vector.bn_stats(stats[:, c], u_in[:, c]).then_inc(s_eln, 1)

            def experts_variance():
                dve.wait_ge(s_eln, 4)
                for c in range(NBC):
                    nc.vector.bn_aggr(mv[:, c], stats[:, c]).then_inc(s_eln, 1)
                dve.wait_ge(s_eln, 8)
                nc.vector.tensor_scalar(ve[:], mv[:, :, 1], EPS, None, ALU.add).then_inc(s_eln, 1)

            def experts_norm():
                dve.wait_ge(s_epow, 1)
                for c in range(NBC):
                    nc.vector.tensor_scalar(u_in[:, c], u_in[:, c], mv[:, c, 0:1], rstd[:, c:c + 1],
                                            ALU.subtract, ALU.mult).then_inc(s_eln, 1)

            def take_experts_norm():
                for k in range(KT):
                    split_job(take(f"XE{k}", PAIRS), xh_hi[:, k], xh_lo[:, k], PAIRS * 4 + KT + k + 1)

            norm_stats(0, range(NBC))
            norm_variance(0)
            norm_apply(0, None, range(NBC))
            weights_lo(0)
            take_norm(None)
            weights_lo(1)
            split_small()
            weights_lo(2)
            weights_lo(3)
            one_pass(0)
            with dve.Fori(1, PAIRS) as i:
                one_pass(i)
            for n in range(LAG + 1):
                if n < LAG:
                    mix(*heads_at(n, PAIRS))
                slot_jobs_done(n, PAIRS, tail=True)
                if n == 6:
                    experts_stats()
                if n == 7:
                    experts_variance()
                if n == 9:
                    experts_norm()
            experts_lo("up", 1)
            mean_squares(PAIRS - 1)
            experts_lo("dn", 2)
            take_yT(PAIRS - 1, PAIRS)
            for h in range(2):
                take_out(PAIRS - 1, h, PAIRS)
            for h in range(2):
                out_stats(PAIRS - 1, PAIRS, h)
            out_variance(PAIRS - 1)
            for h in range(2):
                norm_out(PAIRS - 1, h)
            take_experts_norm()


def expert_block(nc, w_hi, w_lo, x_in, xh_hi, xh_lo, x1_dram, b_up, b_down, w_gate, mats, out):
    with ExitStack() as ctx:
        def sb(name, shape, dt=F32):
            return ctx.enter_context(nc.sbuf_tensor(name, shape, dt))

        def ps(name):
            return ctx.enter_context(nc.psum_tensor(name, [P, 512], F32))

        def sem(name):
            return ctx.enter_context(nc.semaphore(name))

        E = EXPERTS
        HT = E * FT
        weights = expert_weights(w_hi, w_lo)
        up_hi, up_lo = weights["up"]
        dn_hi, dn_lo = weights["dn"]
        gt_hi, gt_lo = sb("gt_hi", [P, KT * E], F32R), sb("gt_lo", [P, KT * E], F32R)
        raw_gt = sb("raw_gt", [P, KT * E])
        ident = sb("f_ident", [P, P])
        bu = sb("bu", [P, HT])
        bd = sb("bd", [P, E, DM])
        x_norm, x_res = sb("x_norm", [P, NBC, DM]), sb("x_res", [P, NBC, DM])
        hid = sb("hid", [P, 2, TOK])
        h_hi, h_lo = sb("h_hi", [P, HT, TOK], F32R), sb("h_lo", [P, HT, TOK], F32R)
        y0, y1 = sb("y0", [P, NBC, DM]), sb("y1", [P, NBC, DM])
        bias0, bias1 = sb("bias0", [P, NBC, DM]), sb("bias1", [P, NBC, DM])
        first_wins, second_wins = sb("first_wins", [P, NBC]), sb("second_wins", [P, NBC])
        logits = sb("logits", [P, NBC, E])
        stats, mv = sb("f_stats", [P, NBC, 6]), sb("f_mv", [P, NBC, 2])
        ve, rstd = sb("f_ve", [P, NBC]), sb("f_rstd", [P, NBC])
        stats2, mv2 = sb("f_stats2", [P, NBC, 6]), sb("f_mv2", [P, NBC, 2])
        ve2, rstd2 = sb("f_ve2", [P, NBC]), sb("f_rstd2", [P, NBC])
        mhalf = sb("f_mhalf", [P, NBC])

        p_up = [ps("p_up0"), ps("p_up1")]
        p_dn = [[ps(f"p_dn{h}{e}") for e in range(E)] for h in range(2)]
        p_x, p_gt = ps("p_x"), ps("p_gt")

        f_small, f_bu, f_wgt = sem("f_small"), sem("f_bu"), sem("f_wgt")
        f_x, f_res, f_out = sem("f_x"), sem("f_res"), sem("f_out")
        f_ln, f_pow = sem("f_ln"), sem("f_pow")
        f_tr = sem("f_tr")
        f_xhi, f_xlo = sem("f_xhi"), sem("f_xlo")
        f_gl, f_gate = sem("f_gl"), sem("f_gate")
        f_up, f_act = sem("f_up"), sem("f_act")
        f_hhi, f_hlo = sem("f_hhi"), sem("f_hlo")
        f_dn = sem("f_dn")
        f_y1, f_y1b = sem("f_y1"), sem("f_y1b")
        f_sel = sem("f_sel")
        f_comb = sem("f_comb")
        f_ln2, f_pow2, f_nrm, f_sum = sem("f_ln2"), sem("f_pow2"), sem("f_nrm"), sem("f_sum")
        f_init, f_held = sem("f_init"), sem("f_held")

        x1_p = x1_dram.rearrange("i (k p) d -> i p k d", p=P)
        out_p = out.rearrange("(i b) (c p) d -> i p (b c) d", b=2, p=P)

        def of_pass(t, i):
            if isinstance(i, int):
                return t[i]
            return t[bass.ds(i, 1)].rearrange("o p k d -> (o p) k d")

        def flat(t):
            return t[:].rearrange("p a b -> p (a b)")

        block = ctx.enter_context(nc.Block())

        def is_first(i):
            return isinstance(i, int) and i == 0

        def is_last(i):
            return isinstance(i, int) and i == PAIRS - 1

        def run(eng, one_pass):
            one_pass(0)
            with eng.Fori(1, PAIRS - 1) as i:
                one_pass(i)
            one_pass(PAIRS - 1)

        @block.sync
        def _(sp_):
            sp_.sem_inc(f_x, 16)
            sp_.dma_start(bu[:], b_up).then_inc(f_bu, 16)
            sp_.dma_start(ident[:], mats[:, 0:P]).then_inc(f_small, 16)
            sp_.dma_start(raw_gt[:], w_gate).then_inc(f_small, 16)
            sp_.dma_start(flat(bd), b_down.rearrange("(o n) -> o n", o=1).broadcast_to([P, E * DM])).then_inc(f_small, 16)
            sp_.sem_inc(f_out, 16)

            def store(i):
                sp_.wait_ge(f_sum, i + 1)
                sp_.dma_start(of_pass(out_p, i), y0[:]).then_inc(f_out, 16)

            def one_pass(i):
                if not is_last(i):
                    sp_.wait_ge(f_ln, i * 13 + 13)
                    sp_.dma_start(x_in[:], of_pass(x1_p, i + 1)).then_inc(f_x, 16)
                if not is_first(i):
                    store(i - 1)
                sp_.dma_start(x_res[:], of_pass(x1_p, i)).then_inc(f_res, 16)

            run(sp_, one_pass)
            store(PAIRS - 1)
            sp_.wait_ge(f_out, 16 * (PAIRS + 1))

        @block.tensor
        def _(pe):
            def split3(out_, a, a2, b, b2, first, last):
                for m, (x, y) in enumerate(((a, b), (a, b2), (a2, b))):
                    r = nc.tensor.matmul(out_, x, y, start=(first and m == 0), stop=(last and m == 2))
                return r

            def transposes(i, k):
                if k == 0:
                    pe.wait_ge(f_ln, i * 13 + 13)
                if not (is_first(i) and k == 0):
                    pe.wait_ge(f_xlo, i * KT + k)
                for c in range(NBC):
                    r = nc.tensor.transpose(p_x[:, c * P:(c + 1) * P], x_norm[:, c, k * P:(k + 1) * P], ident[:])
                r.then_inc(f_tr, 1)

            def gate_logits(i, c):
                if not is_first(i) and c == 0:
                    pe.wait_ge(f_gate, i * 3)
                cols = slice(c * P, (c + 1) * P)
                for k in range(KT):
                    r = split3(p_gt[:, c * E:(c + 1) * E], xh_hi[:, k, cols], xh_lo[:, k, cols],
                               gt_hi[:, k * E:(k + 1) * E], gt_lo[:, k * E:(k + 1) * E], k == 0, k == KT - 1)
                if c == NBC - 1:
                    r.then_inc(f_gl, 1)

            def up(i, m):
                e, f = m // FT, m % FT
                if not (is_first(i) and m < 2):
                    pe.wait_ge(f_act, i * HT + m - 1)
                if m == 0:
                    pe.wait_ge(f_xlo, i * KT + KT)
                cols = slice(f * P, (f + 1) * P)
                for k in range(KT):
                    r = split3(p_up[m % 2][:], up_hi[:, e * KT + k, cols], up_lo[:, e * KT + k, cols],
                               xh_hi[:, k], xh_lo[:, k], k == 0, k == KT - 1)
                r.then_inc(f_up, 1)

            def down(i, e, h):
                if h == 0:
                    pe.wait_ge(f_hlo, i * HT + (e + 1) * FT)
                if not is_first(i):
                    pe.wait_ge(f_y1 if e else f_comb, (i - 1) * NBC + 2 * h + 2)
                for c in range(2):
                    cols = slice((2 * h + c) * P, (2 * h + c + 1) * P)
                    for f in range(FT):
                        r = split3(p_dn[h][e][:, c * DM:(c + 1) * DM], h_hi[:, e * FT + f, cols],
                                   h_lo[:, e * FT + f, cols], dn_hi[:, e * FT + f], dn_lo[:, e * FT + f],
                                   f == 0, f == FT - 1)
                r.then_inc(f_dn, 1)

            def one_pass(i):
                for m in range(HT):
                    up(i, m)
                    if is_first(i) and m == 1:
                        pe.wait_ge(f_small, 16 * 3)
                        pe.wait_ge(f_wgt, 2)
                    if 1 <= m <= NBC:
                        gate_logits(i, m - 1)
                down(i, 0, 0)
                down(i, 0, 1)
                if not is_last(i):
                    transposes(i + 1, 0)
                down(i, 1, 0)
                if not is_last(i):
                    transposes(i + 1, 1)
                down(i, 1, 1)

            pe.sem_inc(f_tr, KT)
            run(pe, one_pass)

        @block.scalar
        def _(act):
            def norm_hi(i, k):
                act.wait_ge(f_tr, i * KT + k + 1)
                nc.scalar.activation(xh_hi[:, k], p_x[:], ACT.Copy).then_inc(f_xhi, 1)

            def second_expert(i):
                act.wait_ge(f_gate, i * 3 + 3)
                for c in range(NBC):
                    act.wait_ge(f_dn, i * 4 + 2 + c // 2 + 1)
                    nc.scalar.activation(y1[:, c], p_dn[c // 2][1][:, (c % 2) * DM:(c % 2 + 1) * DM], ACT.Copy,
                                         scale=second_wins[:, c:c + 1]).then_inc(f_y1, 1)

            def hidden(i, m):
                act.wait_ge(f_up, i * HT + m + 1)
                if not (is_first(i) and m < 2):
                    act.wait_ge(f_hlo, i * HT + m - 1)
                nc.scalar.activation(hid[:, m % 2], p_up[m % 2][:], ACT.Gelu if m < FT else ACT.Relu,
                                     bias=bu[:, m:m + 1]).then_inc(f_act, 1)
                act.wait_ge(f_act, i * HT + m + 1)
                if not is_first(i) and m % FT == 0:
                    act.wait_ge(f_dn, (i - 1) * 4 + 2 * (m // FT) + 2)
                nc.scalar.activation(h_hi[:, m], hid[:, m % 2], ACT.Copy).then_inc(f_hhi, 1)

            def one_pass(i):
                if not is_first(i):
                    second_expert(i - 1)
                for m in range(HT):
                    hidden(i, m)
                if not is_last(i):
                    for k in range(KT):
                        norm_hi(i + 1, k)

            act.sem_inc(f_xhi, KT)
            act.wait_ge(f_bu, 16)
            run(act, one_pass)
            second_expert(PAIRS - 1)

        @block.gpsimd
        def _(pool):
            def norm_pow(i):
                pool.wait_ge(f_ln, i * 13 + 9)
                pool.tensor_tensor(rstd[:], ve[:], mhalf[:], ALU.pow).then_inc(f_pow, 1)

            def choose_bias(i):
                pool.wait_ge(f_gate, i * 3 + 3)
                pool.sem_inc(f_held, 1)
                for c in range(NBC):
                    pool.tensor_scalar(bias0[:, c], bd[:, 0], first_wins[:, c:c + 1], None, ALU.mult).then_inc(f_sel, 1)
                    pool.tensor_scalar(bias1[:, c], bd[:, 1], second_wins[:, c:c + 1], None, ALU.mult).then_inc(f_sel, 1)
                pool.wait_ge(f_sel, i * 9 + 8)
                pool.tensor_tensor(flat(bias0), flat(bias0), flat(bias1), ALU.add).then_inc(f_sel, 1)

            def add_bias(i):
                pool.wait_ge(f_sel, i * 9 + 9)
                for h in range(2):
                    pool.wait_ge(f_y1, i * NBC + 2 * h + 2)
                    half = slice(2 * h, 2 * h + 2)
                    pool.tensor_tensor(y1[:, half].rearrange("p a b -> p (a b)"), y1[:, half].rearrange("p a b -> p (a b)"),
                                       bias0[:, half].rearrange("p a b -> p (a b)"), ALU.add).then_inc(f_y1b, 1)

            def finish(i):
                pool.wait_ge(f_ln2, i * 9 + 9)
                pool.tensor_tensor(rstd2[:], ve2[:], mhalf[:], ALU.pow).then_inc(f_pow2, 1)
                pool.wait_ge(f_nrm, i * NBC + NBC)
                pool.wait_ge(f_res, i * 16 + 16)
                pool.tensor_tensor(flat(y0), flat(y0), flat(x_res), ALU.add).then_inc(f_sum, 1)

            def one_pass(i):
                if not is_first(i):
                    add_bias(i - 1)
                    finish(i - 1)
                if not is_last(i):
                    norm_pow(i + 1)
                choose_bias(i)

            pool.memset(mhalf[:], -0.5).then_inc(f_init, 1)
            pool.wait_ge(f_init, 1)
            pool.sem_inc(f_pow, 1)
            pool.wait_ge(f_small, 16 * 3)
            run(pool, one_pass)
            add_bias(PAIRS - 1)
            finish(PAIRS - 1)

        @block.vector
        def _(dve):
            def split_gate():
                dve.wait_ge(f_small, 16 * 3)
                nc.vector.tensor_copy(gt_hi[:], raw_gt[:]).then_inc(f_wgt, 1)
                dve.wait_ge(f_wgt, 1)
                nc.vector.tensor_tensor(gt_lo[:], raw_gt[:], gt_hi[:].bitcast(F32), ALU.subtract).then_inc(f_wgt, 1)

            def norm_stats(i):
                dve.wait_ge(f_x, i * 16 + 16)
                for c in range(NBC):
                    nc.vector.bn_stats(stats[:, c], x_in[:, c]).then_inc(f_ln, 1)

            def norm_variance(i):
                dve.wait_ge(f_ln, i * 13 + 4)
                dve.sem_inc(f_held, 1)
                for c in range(NBC):
                    nc.vector.bn_aggr(mv[:, c], stats[:, c]).then_inc(f_ln, 1)
                dve.wait_ge(f_ln, i * 13 + 8)
                nc.vector.tensor_scalar(ve[:], mv[:, :, 1], EPS, None, ALU.add).then_inc(f_ln, 1)

            def norm_apply(i):
                dve.wait_ge(f_pow, i + 1)
                if not is_first(i):
                    dve.wait_ge(f_tr, i * KT)
                for c in range(NBC):
                    nc.vector.tensor_scalar(x_norm[:, c], x_in[:, c], mv[:, c, 0:1], rstd[:, c:c + 1],
                                            ALU.subtract, ALU.mult).then_inc(f_ln, 1)

            def norm_lo(i, k):
                dve.wait_ge(f_xhi, i * KT + k + 1)
                nc.vector.tensor_tensor(xh_lo[:, k], p_x[:], xh_hi[:, k].bitcast(F32), ALU.subtract).then_inc(f_xlo, 1)

            def gate(i):
                dve.wait_ge(f_gl, i + 1)
                nc.vector.tensor_copy(flat(logits), p_gt[:, 0:NBC * E]).then_inc(f_gate, 1)
                dve.wait_ge(f_gate, i * 3 + 1)
                nc.vector.tensor_tensor(first_wins[:], logits[:, :, 0], logits[:, :, 1], ALU.is_ge).then_inc(f_gate, 1)
                dve.wait_ge(f_gate, i * 3 + 2)
                nc.vector.tensor_scalar(second_wins[:], first_wins[:], -1.0, 1.0, ALU.mult, ALU.add).then_inc(f_gate, 1)

            def hidden_lo(i, m):
                dve.wait_ge(f_hhi, i * HT + m + 1)
                nc.vector.tensor_tensor(h_lo[:, m], hid[:, m % 2], h_hi[:, m].bitcast(F32), ALU.subtract).then_inc(f_hlo, 1)

            def combine(i, h):
                dve.wait_ge(f_y1b, i * 2 + h + 1)
                if h == 0:
                    dve.wait_ge(f_out, i * 16 + 16)
                for c in (2 * h, 2 * h + 1):
                    nc.vector.scalar_tensor_tensor(out=y0[:, c], in0=p_dn[h][0][:, (c % 2) * DM:(c % 2 + 1) * DM],
                                                   scalar=first_wins[:, c:c + 1], in1=y1[:, c],
                                                   op0=ALU.mult, op1=ALU.add).then_inc(f_comb, 1)

            def out_stats(i):
                dve.wait_ge(f_comb, i * NBC + NBC)
                for c in range(NBC):
                    nc.vector.bn_stats(stats2[:, c], y0[:, c]).then_inc(f_ln2, 1)

            def out_variance(i):
                dve.wait_ge(f_ln2, i * 9 + 4)
                dve.sem_inc(f_held, 1)
                for c in range(NBC):
                    nc.vector.bn_aggr(mv2[:, c], stats2[:, c]).then_inc(f_ln2, 1)
                dve.wait_ge(f_ln2, i * 9 + 8)
                nc.vector.tensor_scalar(ve2[:], mv2[:, :, 1], EPS, None, ALU.add).then_inc(f_ln2, 1)

            def norm_out(i):
                dve.wait_ge(f_pow2, i + 1)
                for c in range(NBC):
                    nc.vector.tensor_scalar(y0[:, c], y0[:, c], mv2[:, c, 0:1], rstd2[:, c:c + 1],
                                            ALU.subtract, ALU.mult).then_inc(f_nrm, 1)

            def one_pass(i):
                for m in range(HT):
                    hidden_lo(i, m)
                    if not is_first(i):
                        if m in (0, 1):
                            combine(i - 1, m)
                        if m == 2:
                            out_stats(i - 1)
                            out_variance(i - 1)
                        if m == 4:
                            norm_out(i - 1)
                    if m == 6:
                        gate(i)
                    if not is_last(i):
                        if m == 3:
                            norm_stats(i + 1)
                        if m == 5:
                            norm_variance(i + 1)
                if not is_last(i):
                    norm_apply(i + 1)
                    for k in range(KT):
                        norm_lo(i + 1, k)

            dve.sem_inc(f_ln, 13)
            dve.sem_inc(f_xlo, KT)
            split_gate()
            run(dve, one_pass)
            combine(PAIRS - 1, 0)
            combine(PAIRS - 1, 1)
            out_stats(PAIRS - 1)
            out_variance(PAIRS - 1)
            norm_out(PAIRS - 1)


def program(nc, t, cs_dram, x1_dram, out):
    with ExitStack() as ctx:
        w_hi = ctx.enter_context(nc.sbuf_tensor("w_hi", [P, KT, TILES * P], F32R))
        w_lo = ctx.enter_context(nc.sbuf_tensor("w_lo", [P, KT, TILES * P], F32R))
        x_in = ctx.enter_context(nc.sbuf_tensor("x_in", [P, NBC, DM], F32))
        xh_hi = ctx.enter_context(nc.sbuf_tensor("xh_hi", [P, KT, TOK], F32R))
        xh_lo = ctx.enter_context(nc.sbuf_tensor("xh_lo", [P, KT, TOK], F32R))
        mamba_block(nc, w_hi, w_lo, x_in, xh_hi, xh_lo, t["w_up"], t["w_down"], t["u"], t["w_tiles"], t["w_za"], t["z_bias"],
                    t["conv_w"], t["conv_b"], t["d_skip"], t["rms_w"], t["w_out"], t["mats"], t["pick"], t["marks"],
                    cs_dram, x1_dram)
        expert_block(nc, w_hi, w_lo, x_in, xh_hi, xh_lo, x1_dram, t["b_up"], t["b_down"], t["w_gate"], t["mats"], out)


def kernel(L0_attn_u, L0_attn_W_in, L0_attn_z_bias, L0_attn_conv_w, L0_attn_conv_b, L0_attn_D, L0_attn_rms_w,
           L0_attn_W_out, L0_ffn_Wg, L0_ffn_W0a, L0_ffn_b0a, L0_ffn_W0b, L0_ffn_b0b, L0_ffn_W1a, L0_ffn_b1a,
           L0_ffn_W1b, L0_ffn_b1b):
    import concourse.bacc as bacc
    from concourse.bass_utils import run_bass_kernel_spmd

    a = np.asarray
    rows = lay_out()
    w_in = a(L0_attn_W_in)
    conv_rows = HEADS * HDIM + 2 * HEADS * NSTATE
    mats, pick, marks = constants()
    arrays = {
        "u": a(L0_attn_u),
        "w_tiles": w_in[rows].T,
        "w_za": w_in[conv_rows:].T,
        "z_bias": a(L0_attn_z_bias),
        "conv_w": a(L0_attn_conv_w)[rows].reshape(TILES, P, TAPS).transpose(1, 0, 2),
        "conv_b": a(L0_attn_conv_b)[rows].reshape(TILES, P).T,
        "d_skip": a(L0_attn_D),
        "rms_w": a(L0_attn_rms_w).reshape(KT, P).T,
        "w_out": a(L0_attn_W_out).T,
        "mats": mats,
        "pick": pick,
        "marks": marks,
        "w_up": np.stack([a(L0_ffn_W0a).T, a(L0_ffn_W1a).T]),
        "b_up": np.concatenate([a(L0_ffn_b0a), a(L0_ffn_b1a)]).reshape(-1, P).T,
        "w_down": np.stack([a(L0_ffn_W0b).T, a(L0_ffn_W1b).T]),
        "b_down": np.concatenate([a(L0_ffn_b0b), a(L0_ffn_b1b)]),
        "w_gate": a(L0_ffn_Wg).reshape(2, KT, P).transpose(2, 1, 0).reshape(P, KT * 2),
    }
    arrays = {k: np.ascontiguousarray(v) for k, v in arrays.items()}
    nc = bacc.Bacc("TRN2", target_bir_lowering=False, num_devices=1)
    t = {k: nc.dram_tensor(k, v.shape, F32, kind="ExternalInput").ap() for k, v in arrays.items()}
    out = nc.dram_tensor("out", (BATCH, SEQ, DM), F32, kind="ExternalOutput").ap()
    cs_dram = nc.dram_tensor("cs_dram", (3, HEADS, TOK), BF16, kind="Internal").ap()
    x1_dram = nc.dram_tensor("x1_dram", (PAIRS, TOK, DM), F32, kind="Internal").ap()
    program(nc, t, cs_dram, x1_dram, out)
    r = run_bass_kernel_spmd(nc, [arrays], core_ids=[0])
    return r.results[0]["out"]
```
